# Optimizing a Trainium2 kernel written in Bass

```python
import numpy as np
import jax
import jax.numpy as jnp

def _softmax(x, axis=-1):
    return jax.nn.softmax(x, axis=axis)

def _gelu(x):
    return jax.nn.gelu(x, approximate=True)

def _silu(x):
    return jax.nn.silu(x)

def _sigmoid(x):
    return jax.nn.sigmoid(x)

def _layernorm(x, axis=-1, eps=1e-05):
    m = jnp.mean(x, axis=axis, keepdims=True)
    v = jnp.var(x, axis=axis, keepdims=True)
    return (x - m) / jnp.sqrt(v + eps)

def _scatter_add(tgt, idx, src, axis=0):
    return tgt.at[idx].add(src)

def _segment_sum(src, seg, n):
    return jax.ops.segment_sum(src, seg, n)
kernel_name = 'mk_recurrent_d2_jaxref_r8_d6f01c'

def setup_inputs(seed: int=0):
    np.random.seed(seed)
    _w = jnp.asarray

    def _L0_attn_setup():
        import jax, jax.numpy as jnp
        import numpy as np
        DIM = 128
        DIM_HEAD = 128
        HEADS = 8
        DIM_INNER = DIM_HEAD * HEADS
        key = jax.random.key(seed)
        k_x, k_qkv, k_out = jax.random.split(key, 3)
        x = jax.random.normal(k_x, (2, 256, DIM), dtype=jnp.float32)
        gamma = jnp.ones((DIM,), dtype=jnp.float32)
        w_qkv = jax.random.uniform(k_qkv, (DIM_INNER * 3, DIM), dtype=jnp.float32, minval=-1.0, maxval=1.0) / np.sqrt(DIM)
        w_out = jax.random.uniform(k_out, (DIM, DIM_INNER), dtype=jnp.float32, minval=-1.0, maxval=1.0) / np.sqrt(DIM_INNER)
        return {'x': x, 'gamma': gamma, 'w_qkv': w_qkv, 'w_out': w_out}
    _L0_attn_in = _L0_attn_setup()

    def _L0_ffn_setup():
        import jax, jax.numpy as jnp
        import numpy as np
        EPS = 1e-08

        def _ternary_linear(x, w):
            alpha = jnp.mean(jnp.abs(w))
            w_t = jnp.sign(w) * (jnp.abs(w) > 0.5 * alpha).astype(w.dtype)
            w_q = w + jax.lax.stop_gradient(w_t - w)
            d = x.shape[-1]
            rms = jnp.sqrt(jnp.sum(x * x, axis=-1, keepdims=True)) / jnp.sqrt(jnp.asarray(d, x.dtype))
            x_norm = x / (rms + EPS)
            return jnp.einsum('bsd,fd->bsf', x_norm, w_q)
        key = jax.random.key(seed)
        k1, k2, k3 = jax.random.split(key, 3)
        d_model, d_ff = (128, 512)
        B, S = (4, 512)
        x = jax.random.normal(k1, (B, S, d_model), dtype=jnp.float32)
        w_up = jax.random.normal(k2, (d_ff, d_model), dtype=jnp.float32) * 0.02
        w_down = jax.random.normal(k3, (d_model, d_ff), dtype=jnp.float32) * 0.02
        return {'x': x, 'w_up': w_up, 'w_down': w_down}
    _L0_ffn_in = _L0_ffn_setup()

    def _L1_attn_setup():
        import jax, jax.numpy as jnp
        import numpy as np
        H = 16
        E = 128
        D = E // H
        M = 128
        EPS = 1e-12
        key = jax.random.key(seed)
        ks = jax.random.split(key, 12)
        s = 0.02
        B, S = (8, 128)
        return {'hidden_states': jax.random.normal(ks[0], (B, S, E), jnp.float32), 'Wq': jax.random.normal(ks[1], (E, E), jnp.float32) * s, 'bq': jnp.zeros((E,), jnp.float32), 'Wk': jax.random.normal(ks[2], (E, E), jnp.float32) * s, 'bk': jnp.zeros((E,), jnp.float32), 'Wv': jax.random.normal(ks[3], (E, E), jnp.float32) * s, 'bv': jnp.zeros((E,), jnp.float32), 'dist_emb': jax.random.normal(ks[4], (2 * M - 1, D), jnp.float32) * s, 'Wo': jax.random.normal(ks[5], (E, E), jnp.float32) * s, 'bo': jnp.zeros((E,), jnp.float32), 'ln_gamma': jnp.ones((E,), jnp.float32), 'ln_beta': jnp.zeros((E,), jnp.float32)}
    _L1_attn_in = _L1_attn_setup()

    def _L1_ffn_setup():
        import jax, jax.numpy as jnp
        import numpy as np
        B, S, D = (2, 256, 128)
        E, K, F = (16, 2, 64)
        FS = 128
        key = jax.random.key(seed)
        ks = jax.random.split(key, 8)

        def w(k, shape, fan_in):
            return jax.random.normal(k, shape, jnp.float32) / np.sqrt(fan_in).astype(np.float32)
        return {'x': jax.random.normal(ks[0], (B, S, D), jnp.float32), 'Wr': w(ks[1], (D, E), D), 'Wg': w(ks[2], (E, D, F), D), 'Wu': w(ks[3], (E, D, F), D), 'Wd': w(ks[4], (E, F, D), F), 'Sg': w(ks[5], (D, FS), D), 'Su': w(ks[6], (D, FS), D), 'Sd': w(ks[7], (FS, D), FS)}
    _L1_ffn_in = _L1_ffn_setup()
    _d = {'L0_attn_x': _L0_attn_in['x'], 'L0_attn_gamma': _L0_attn_in['gamma'], 'L0_attn_w_qkv': _L0_attn_in['w_qkv'], 'L0_attn_w_out': _L0_attn_in['w_out'], 'L0_ffn_w_up': _L0_ffn_in['w_up'], 'L0_ffn_w_down': _L0_ffn_in['w_down'], 'L1_attn_Wq': _L1_attn_in['Wq'], 'L1_attn_bq': _L1_attn_in['bq'], 'L1_attn_Wk': _L1_attn_in['Wk'], 'L1_attn_bk': _L1_attn_in['bk'], 'L1_attn_Wv': _L1_attn_in['Wv'], 'L1_attn_bv': _L1_attn_in['bv'], 'L1_attn_dist_emb': _L1_attn_in['dist_emb'], 'L1_attn_Wo': _L1_attn_in['Wo'], 'L1_attn_bo': _L1_attn_in['bo'], 'L1_attn_ln_gamma': _L1_attn_in['ln_gamma'], 'L1_attn_ln_beta': _L1_attn_in['ln_beta'], 'L1_ffn_Wr': _L1_ffn_in['Wr'], 'L1_ffn_Wg': _L1_ffn_in['Wg'], 'L1_ffn_Wu': _L1_ffn_in['Wu'], 'L1_ffn_Wd': _L1_ffn_in['Wd'], 'L1_ffn_Sg': _L1_ffn_in['Sg'], 'L1_ffn_Su': _L1_ffn_in['Su'], 'L1_ffn_Sd': _L1_ffn_in['Sd']}
    _x0 = _d['L0_attn_x']
    _d['L0_attn_x'] = jax.random.normal(jax.random.fold_in(jax.random.key(seed), 1), (8, 512, 128), dtype=_x0.dtype)
    del _x0
    return _d

def reference(L0_attn_x, L0_attn_gamma, L0_attn_w_qkv, L0_attn_w_out, L0_ffn_w_up, L0_ffn_w_down, L1_attn_Wq, L1_attn_bq, L1_attn_Wk, L1_attn_bk, L1_attn_Wv, L1_attn_bv, L1_attn_dist_emb, L1_attn_Wo, L1_attn_bo, L1_attn_ln_gamma, L1_attn_ln_beta, L1_ffn_Wr, L1_ffn_Wg, L1_ffn_Wu, L1_ffn_Wd, L1_ffn_Sg, L1_ffn_Su, L1_ffn_Sd):

    def _L0_attn_ref(x, gamma, w_qkv, w_out):
        import jax, jax.numpy as jnp
        import numpy as np
        DIM = 128
        DIM_HEAD = 128
        HEADS = 8
        DIM_INNER = DIM_HEAD * HEADS
        scale_norm = DIM ** 0.5
        scale_attn = DIM_HEAD ** (-0.5)
        l2 = jnp.sqrt(jnp.sum(x * x, axis=-1, keepdims=True))
        xn = x / jnp.maximum(l2, 1e-12) * scale_norm * gamma
        qkv = jnp.einsum('bnc,fc->bnf', xn, w_qkv)
        b, n, _ = qkv.shape
        qkv = qkv.reshape(b, n, 3, HEADS, DIM_HEAD)
        q, k, v = (qkv[:, :, 0], qkv[:, :, 1], qkv[:, :, 2])
        q = q * scale_attn
        sim = jnp.einsum('bihd,bjhd->bhij', q, k)
        causal_mask = jnp.triu(jnp.ones((n, n), dtype=bool), k=1)
        neg = -jnp.finfo(sim.dtype).max
        sim = jnp.where(causal_mask, neg, sim)
        attn = jax.nn.softmax(sim, axis=-1)
        out = jnp.einsum('bhij,bjhd->bihd', attn, v)
        out = out.reshape(b, n, DIM_INNER)
        return jnp.einsum('bnf,cf->bnc', out, w_out)

    def _L0_ffn_ref(x, w_up, w_down):
        import jax, jax.numpy as jnp
        import numpy as np
        EPS = 1e-08

        def _ternary_linear(x, w):
            alpha = jnp.mean(jnp.abs(w))
            w_t = jnp.sign(w) * (jnp.abs(w) > 0.5 * alpha).astype(w.dtype)
            w_q = w + jax.lax.stop_gradient(w_t - w)
            d = x.shape[-1]
            rms = jnp.sqrt(jnp.sum(x * x, axis=-1, keepdims=True)) / jnp.sqrt(jnp.asarray(d, x.dtype))
            x_norm = x / (rms + EPS)
            return jnp.einsum('bsd,fd->bsf', x_norm, w_q)
        h = jax.nn.gelu(_ternary_linear(x, w_up), approximate=False)
        return _ternary_linear(h, w_down)

    def _L1_attn_ref(hidden_states, Wq, bq, Wk, bk, Wv, bv, dist_emb, Wo, bo, ln_gamma, ln_beta):
        import jax, jax.numpy as jnp
        import numpy as np
        H = 16
        E = 128
        D = E // H
        M = 128
        EPS = 1e-12
        B, S, _ = hidden_states.shape

        def heads(x):
            return x.reshape(B, S, H, D).transpose(0, 2, 1, 3)
        q = heads(hidden_states @ Wq + bq)
        k = heads(hidden_states @ Wk + bk)
        v = heads(hidden_states @ Wv + bv)
        scores = jnp.einsum('bhqd,bhkd->bhqk', q, k)
        pos_l = jnp.arange(S)[:, None]
        pos_r = jnp.arange(S)[None, :]
        dist_idx = pos_l - pos_r + M - 1
        pos_emb = dist_emb[dist_idx]
        rel_q = jnp.einsum('bhld,lrd->bhlr', q, pos_emb)
        rel_k = jnp.einsum('bhrd,lrd->bhlr', k, pos_emb)
        scores = (scores + rel_q + rel_k) / jnp.sqrt(jnp.asarray(D, scores.dtype))
        probs = jax.nn.softmax(scores, axis=-1)
        ctx = jnp.einsum('bhqk,bhkd->bhqd', probs, v)
        ctx = ctx.transpose(0, 2, 1, 3).reshape(B, S, E)
        h = ctx @ Wo + bo + hidden_states
        mu = jnp.mean(h, axis=-1, keepdims=True)
        var = jnp.mean(jnp.square(h - mu), axis=-1, keepdims=True)
        out = (h - mu) * jax.lax.rsqrt(var + EPS) * ln_gamma + ln_beta
        return out

    def _L1_ffn_ref(x, Wr, Wg, Wu, Wd, Sg, Su, Sd):
        import jax, jax.numpy as jnp
        import numpy as np
        B, S, D = (2, 256, 128)
        E, K, F = (16, 2, 64)
        FS = 128
        b, s, d = x.shape
        T = b * s
        xf = x.reshape(T, d)
        shared = jax.nn.silu(xf @ Sg) * (xf @ Su) @ Sd
        probs = jax.nn.softmax(xf @ Wr, axis=-1)
        topk_p, topk_i = jax.lax.top_k(probs, K)
        n_exp = Wr.shape[1]
        cw = jnp.zeros((T, n_exp), x.dtype).at[jnp.arange(T)[:, None], topk_i].add(topk_p)

        def step(acc, ew):
            wg, wu, wd, c = ew
            y = jax.nn.silu(xf @ wg) * (xf @ wu) @ wd
            return (acc + y * c[:, None], None)
        routed, _ = jax.lax.scan(step, jnp.zeros_like(xf), (Wg, Wu, Wd, cw.T))
        return (routed + shared).reshape(b, s, d)
    x = L0_attn_x
    xn = _layernorm(x, axis=-1)
    s = _L0_attn_ref(xn, L0_attn_gamma, L0_attn_w_qkv, L0_attn_w_out)
    g = _silu(_L0_ffn_ref(xn, L0_ffn_w_up, L0_ffn_w_down))
    x = x + s * g
    xn = _layernorm(x, axis=-1)
    s = _L1_attn_ref(xn, L1_attn_Wq, L1_attn_bq, L1_attn_Wk, L1_attn_bk, L1_attn_Wv, L1_attn_bv, L1_attn_dist_emb, L1_attn_Wo, L1_attn_bo, L1_attn_ln_gamma, L1_attn_ln_beta)
    g = _silu(_L1_ffn_ref(xn, L1_ffn_Wr, L1_ffn_Wg, L1_ffn_Wu, L1_ffn_Wd, L1_ffn_Sg, L1_ffn_Su, L1_ffn_Sd))
    x = x + s * g
    return x

_drawn_inputs = setup_inputs


def setup_inputs(seed=0):
    import zlib

    import numpy as np

    out = dict(_drawn_inputs(seed))
    spreads = {'L0_attn_gamma': (1.0, 0.2),
     'L1_attn_bq': (0.0, 0.8),
     'L1_attn_bk': (0.0, 0.8),
     'L1_attn_bv': (0.0, 0.8),
     'L1_attn_bo': (0.0, 0.319),
     'L1_attn_ln_gamma': (1.0, 0.2),
     'L1_attn_ln_beta': (0.0, 0.292)}
    factors = {'L1_attn_Wq': 8.0,
     'L1_attn_Wk': 8.0,
     'L1_attn_Wv': 8.0,
     'L1_attn_dist_emb': 8.0,
     'L1_attn_Wo': 8.0}
    for name, (base, spread) in spreads.items():
        noise = np.random.default_rng([zlib.crc32(name.encode()), seed]).standard_normal(out[name].shape)
        drawn = base * np.exp(spread * noise) if base else spread * noise
        out[name] = jnp.asarray(drawn.astype(out[name].dtype))
    for name, factor in factors.items():
        out[name] = (out[name] * factor).astype(out[name].dtype)
    return out
```

```python
from contextlib import ExitStack

import concourse.bass as bass
from concourse import mybir

F32 = mybir.dt.float32
F16 = mybir.dt.float16
BF16 = mybir.dt.bfloat16
ALU = mybir.AluOpType
ACT = mybir.ActivationFunctionType
AX = mybir.AxisListType

P = 128
BATCH, SEQ, DIM = 8, 512, 128
TOK = BATCH * SEQ
TILES = TOK // P
LT = SEQ // P
CH = 4
CT = TILES // CH
H0 = 8
FF = 512
FT = FF // P
H1, D1 = 16, 8
HG = 8
NHG = H1 // HG
DE = D1 + 1
M_REL = 128
NDIST = 2 * M_REL - 1
JG = 8
NG = 64 // JG
TW = 2 * SEQ - JG
TOFF = SEQ - JG
NEXP, FE, PAIRS = 16, 64, 8
QK_SCALE = 64.0
SM0 = float(P) ** -0.5
SM1 = float(D1) ** -0.5
NEG = -1.0e30


def flat(ap):
    return ap.rearrange("p a b -> p (a b)")


def bc_last(col, n):
    return col.unsqueeze(2).to_broadcast([col.shape[0], col.shape[1], n])


def bc_mid(row, a):
    return row.unsqueeze(1).to_broadcast([row.shape[0], a, row.shape[1]])


def build(nc, ins, out):
    ctx = ExitStack()
    with ctx:
        def sb(name, shape, dt=F32, stack=ctx):
            return stack.enter_context(nc.sbuf_tensor(name, shape, dt))

        def pb(name, shape, dt=F32, stack=ctx):
            return stack.enter_context(nc.psum_tensor(name, shape, dt))

        def sem(name):
            return ctx.enter_context(nc.semaphore(name))

        def scratch(name, shape, dt):
            return nc.dram_tensor(name, shape, dt, kind="Internal").ap()

        X = sb("X", [P, TILES, DIM])
        S = sb("S", [P, TILES, DIM])
        ident = sb("ident", [P, P])
        ident_bf = sb("ident_bf", [P, P], BF16)
        ones_bf = sb("ones_bf", [P, P], BF16)
        q_d = scratch("q_split", (2, H1 * D1, TOK), F16)
        k_d = scratch("k_split", (2, H1 * D1, TOK), F16)
        v_d = scratch("v_ones", (TOK, H1 * DE), F32)
        rb_d = scratch("rel_bound", (TOK, H1), F32)
        ctx_d = scratch("context", (TOK, DIM), F32)

        layer0(nc, sb, pb, sem, ins, X, S, ident, ident_bf, ones_bf)
        layer1(nc, sb, pb, sem, ins, out, X, S, ident, ident_bf, ones_bf, q_d, k_d, v_d, rb_d, ctx_d)


def norm_stats(dve, nc, step, src, dst, sq, mean, var, c):
    t = slice(c * CT, (c + 1) * CT)
    step(nc.vector.tensor_reduce(mean[:, t], src[:, t, :], AX.X, ALU.add))
    step(nc.vector.tensor_scalar(mean[:, t], mean[:, t], 1.0 / DIM, None, ALU.mult))
    step(nc.vector.tensor_tensor(dst[:, t, :], src[:, t, :], bc_last(mean[:, t], DIM), ALU.subtract))
    step(nc.vector.tensor_tensor(sq[:, :, :], dst[:, t, :], dst[:, t, :], ALU.mult))
    step(nc.vector.tensor_reduce(var[:, t], sq[:, :, :], AX.X, ALU.add))


class Chain:

    def __init__(self, eng, s):
        self.eng, self.s, self.n = eng, s, 0

    def __call__(self, ins):
        self.n += 1
        ins.then_inc(self.s, 1)
        self.eng.wait_ge(self.s, self.n)


def layer0(nc, sb, pb, sem, ins, X, S, ident, ident_bf, ones_bf):
    with ExitStack() as st:
        ZH = sb("ZH", [P, TOK], F16, st)
        ZL = sb("ZL", [P, TOK], F16, st)
        UH = sb("UH", [P, TOK], F16, st)
        UL = sb("UL", [P, TOK], F16, st)
        MH = sb("MH", [P, H0, P], F16, st)
        ML = sb("ML", [P, H0, P], F16, st)
        NH = sb("NH", [P, H0, P], F16, st)
        NL = sb("NL", [P, H0, P], F16, st)
        cmask = sb("cmask", [P, 2, P], BF16, st)
        wupT = sb("wupT", [P, FF], F32, st)
        wdnT = sb("wdnT", [P, FT, P], F32, st)
        l0_prepare(nc, sb, pb, sem, ins, X, S, ident, ident_bf, ones_bf,
                   ZH, ZL, UH, UL, MH, ML, NH, NL, cmask, wupT, wdnT)
        l0_attention(nc, sb, pb, sem, S, ident_bf, ones_bf, ZH, ZL, MH, ML, NH, NL, cmask)
        l0_ffn(nc, sb, pb, sem, X, S, UH, UL, wupT, wdnT)


def l0_prepare(nc, sb, pb, sem, ins, X, S, ident, ident_bf, ones_bf,
               ZH, ZL, UH, UL, MH, ML, NH, NL, cmask, wupT, wdnT):
    with ExitStack() as st:
        XC = sb("XC", [P, TILES, DIM], F32, st)
        Z = sb("Z", [P, 2, CT, DIM], F32, st)
        U = sb("U", [P, 2, CT, DIM], F32, st)
        sq = sb("sq0", [P, CT, DIM], F32, st)
        mean = sb("mean0", [P, TILES], F32, st)
        var = sb("var0", [P, TILES], F32, st)
        rstd = sb("rstd0", [P, TILES], F32, st)
        l2 = sb("l2", [P, TILES], F32, st)
        za = sb("za", [P, TILES], F32, st)
        ub = sb("ub", [P, TILES], F32, st)
        gamma = sb("gamma", [P, DIM], F32, st)
        wqkv = sb("wqkv", [P, 3 * H0, P], F32, st)
        woT = sb("woT", [P, H0, P], F32, st)
        cmf = sb("cmf", [P, 2, P], F32, st)
        eps = sb("eps0", [P, 1], F32, st)
        tp = [pb(f"tp{i}", [P, 512], F32, st) for i in range(4)]
        wp = [pb(f"wp{i}", [P, 512], F32, st) for i in range(2)]
        x_in = [sem(f"x_in{c}") for c in range(CH)]
        w_in, g_in, k_in = sem("w_in"), sem("g_in"), sem("k_in")
        dve_step, act_step = sem("p0_dve_step"), sem("p0_act_step")
        var_ok, rstd_ok, l2_ok, zu_ok = sem("var_ok"), sem("std_ok"), sem("l2_ok"), sem("zu_ok")
        l2_in = sem("l2_in")
        tp_ok, tp_hi, tp_lo = sem("tp_ok"), sem("tp_hi"), sem("tp_lo")
        wp_ok, wp_hi, wp_lo = sem("wp_ok"), sem("wp_hi"), sem("wp_lo")
        eps_ok, s_zero = sem("eps_ok"), sem("s_zero")
        pool_ok = sem("p0_pool")
        x_v = ins["x"].rearrange("b (t p) c -> p (b t) c", p=P)

        with nc.Block() as block:
            @block.sync
            def _(sp):
                for c in range(CH):
                    t = slice(c * CT, (c + 1) * CT)
                    sp.dma_start(X[:, t, :], x_v[:, t, :]).then_inc(x_in[c], 16)
                sp.dma_start(wqkv[:, :, :], ins["w_qkv"].rearrange("(k d) c -> d k c", d=P)).then_inc(w_in, 16)
                sp.dma_start(woT[:, :, :], ins["w_outT"].rearrange("(k d) c -> d k c", d=P)).then_inc(w_in, 16)
                sp.dma_start(wupT[:, :], ins["w_upT"]).then_inc(k_in, 16)
                sp.dma_start(wdnT[:, :, :], ins["w_downT"].rearrange("(k f) c -> f k c", f=P)).then_inc(k_in, 16)

            @block.gpsimd
            def _(pool):
                nc.gpsimd.memset(ones_bf[:, :], 1.0).then_inc(pool_ok, 1)
                nc.gpsimd.memset(S[:, :, :], 0.0).then_inc(s_zero, 1)
                pool.wait_ge(k_in, 16 * 4)
                nc.gpsimd.tensor_copy(ident_bf[:, :], ident[:, :]).then_inc(pool_ok, 1)
                nc.gpsimd.tensor_copy(cmask[:, :, :], cmf[:, :, :]).then_inc(pool_ok, 1)

            @block.vector
            def _(dve):
                step = Chain(dve, dve_step)
                nc.vector.memset(eps[:, :], 1e-5).then_inc(eps_ok, 1)
                for c in range(CH):
                    t = slice(c * CT, (c + 1) * CT)
                    dve.wait_ge(x_in[c], 16)
                    norm_stats(dve, nc, step, X, XC, sq, mean, var, c)
                    nc.vector.tensor_scalar(var[:, t], var[:, t], 1.0 / DIM, None, ALU.mult).then_inc(var_ok, 1)
                    dve.wait_ge(rstd_ok, c + 1)
                    step(nc.vector.reciprocal(rstd[:, t], rstd[:, t]))
                    step(nc.vector.tensor_tensor(XC[:, t, :], XC[:, t, :], bc_last(rstd[:, t], DIM), ALU.mult))
                    step(nc.vector.tensor_tensor(sq[:, :, :], XC[:, t, :], XC[:, t, :], ALU.mult))
                    nc.vector.tensor_reduce(l2[:, t], sq[:, :, :], AX.X, ALU.add).then_inc(l2_in, 1)
                    dve.wait_ge(l2_ok, c + 1)
                    step(nc.vector.tensor_scalar(za[:, t], l2[:, t], 1e-12, DIM ** -0.5, ALU.max, ALU.mult))
                    step(nc.vector.tensor_scalar(ub[:, t], l2[:, t], DIM ** -0.5, 1e-8, ALU.mult, ALU.add))
                    step(nc.vector.reciprocal(za[:, t], za[:, t]))
                    step(nc.vector.reciprocal(ub[:, t], ub[:, t]))
                    if c == 0:
                        dve.wait_ge(g_in, 16)
                    if c >= 2:
                        dve.wait_ge(tp_ok, 4 * (c - 1))
                    step(nc.vector.tensor_tensor(Z[:, c % 2], XC[:, t, :], bc_last(za[:, t], DIM), ALU.mult))
                    step(nc.vector.tensor_tensor(Z[:, c % 2], Z[:, c % 2], bc_mid(gamma[:, :], CT), ALU.mult))
                    nc.vector.tensor_tensor(U[:, c % 2], XC[:, t, :], bc_last(ub[:, t], DIM),
                                            ALU.mult).then_inc(zu_ok, 1)
                    dve.wait_ge(zu_ok, c + 1)
                    for i in range(4):
                        n = 4 * c + i
                        lo, hi = (ZL, ZH) if i < 2 else (UL, UH)
                        o = c * CT * P + (i % 2) * 512
                        dve.wait_ge(tp_hi, n + 1)
                        nc.vector.tensor_tensor(lo[:, o:o + 512], tp[i][:, :], hi[:, o:o + 512],
                                                ALU.subtract).then_inc(tp_lo, 1)
                for n in range(4):
                    lo, hi = (ML, MH) if n < 2 else (NL, NH)
                    h = 4 * (n % 2)
                    dve.wait_ge(wp_hi, n + 1)
                    nc.vector.scalar_tensor_tensor(out=flat(lo[:, h:h + 4, :]), in0=wp[n % 2][:, :],
                                                   scalar=QK_SCALE, in1=flat(hi[:, h:h + 4, :]),
                                                   op0=ALU.mult, op1=ALU.subtract).then_inc(wp_lo, 1)

            @block.scalar
            def _(act):
                act.dma_start(ident[:, :], ins["identity"]).then_inc(k_in, 16)
                act.dma_start(cmf[:, :, :], ins["causal"].rearrange("k p c -> p k c")).then_inc(k_in, 16)
                act.dma_start(gamma[:, :], ins["gamma"].partition_broadcast(P)).then_inc(g_in, 16)
                act.wait_ge(eps_ok, 1)
                for c in range(CH):
                    t = slice(c * CT, (c + 1) * CT)
                    act.wait_ge(var_ok, c + 1)
                    nc.scalar.activation(rstd[:, t], var[:, t], ACT.Sqrt, bias=eps[:, 0:1]).then_inc(rstd_ok, 1)
                    act.wait_ge(l2_in, c + 1)
                    nc.scalar.activation(l2[:, t], l2[:, t], ACT.Sqrt).then_inc(l2_ok, 1)
                    for i in range(4):
                        n = 4 * c + i
                        hi = ZH if i < 2 else UH
                        o = c * CT * P + (i % 2) * 512
                        act.wait_ge(tp_ok, n + 1)
                        nc.scalar.copy(hi[:, o:o + 512], tp[i][:, :]).then_inc(tp_hi, 1)
                for n in range(4):
                    hi = MH if n < 2 else NH
                    h = 4 * (n % 2)
                    act.wait_ge(wp_ok, n + 1)
                    nc.scalar.mul(flat(hi[:, h:h + 4, :]), wp[n % 2][:, :], QK_SCALE).then_inc(wp_hi, 1)

            @block.tensor
            def _(pe):
                pe.wait_ge(k_in, 64)
                for c in range(CH):
                    pe.wait_ge(zu_ok, c + 1)
                    for i in range(4):
                        if c >= 1:
                            pe.wait_ge(tp_lo, 4 * (c - 1) + i + 1)
                        src = Z if i < 2 else U
                        for k in range(4):
                            mm = nc.tensor.transpose(tp[i][:, k * P:(k + 1) * P],
                                                     src[:, c % 2, 4 * (i % 2) + k, :], ident[:, :])
                        mm.then_inc(tp_ok, 1)
                pe.wait_ge(w_in, 32)
                for n in range(4):
                    if n >= 2:
                        pe.wait_ge(wp_lo, n - 1)
                    for k in range(4):
                        h = 4 * (n % 2) + k
                        a, b = (wqkv[:, h, :], wqkv[:, H0 + h, :]) if n < 2 else (wqkv[:, 2 * H0 + h, :], woT[:, h, :])
                        mm = nc.tensor.matmul(wp[n % 2][:, k * P:(k + 1) * P], a, b, start=True, stop=True)
                    mm.then_inc(wp_ok, 1)


def l0_attention(nc, sb, pb, sem, S, ident_bf, ones_bf, ZH, ZL, MH, ML, NH, NL, cmask):
    with ExitStack() as st:
        zbH = sb("zbH", [P, SEQ], F16, st)
        zbL = sb("zbL", [P, SEQ], F16, st)
        qH = sb("qH", [P, 2, SEQ], F16, st)
        qL = sb("qL", [P, 2, SEQ], F16, st)
        V = sb("V0", [P, LT, H0, P + 1], F32, st)
        mx = sb("mx0", [P, 2, LT], F32, st)
        dmx = sb("dmx0", [P, 2, LT, P], BF16, st)
        PT = sb("PT0", [P, 2, LT, SEQ], F32, st)
        rz = sb("rz0", [P, LT], F32, st)
        Sb = sb("Sb", [P, LT, P], F32, st)
        QP = pb("QP", [P, 512], F32, st)
        AX_ = [pb(f"AXP{i}", [P, 512], F32, st) for i in range(2)]
        ST = [pb(f"STP{i}", [P, 512], F32, st) for i in range(3)]
        OPB = [pb(f"OP{i}", [P, 512], F32, st) for i in range(2)]
        OP = [o[:, 0:2 * (P + 1)].rearrange("p (t c) -> p t c", t=2) for o in OPB]
        VPS = [ST[i][:, :].rearrange("p (h c) -> p h c", h=4) for i in range(2)]
        z_ready, z_used = sem("z_ready"), sem("z_used")
        v_ready, v_even, v_odd = sem("v_ready"), sem("v_even"), sem("v_odd")
        ones_col = sem("ones_col")
        q_ready, q_hi, q_lo = sem("q_ready"), sem("q_hi"), sem("q_lo")
        aux_ready, aux_max = sem("aux_ready"), sem("aux_max")
        dmx_ready = sem("dmx_ready")
        st_ready, p_ready = sem("st_ready"), sem("p_ready")
        o_ready, o_used, rz_ready = sem("o_ready"), sem("o_used"), sem("rz_ready")
        acc_step, acc_zero, s_kept = sem("acc_step"), sem("acc_zero"), sem("s_kept")
        NV = 2 * LT

        with nc.Block() as block:
            @block.gpsimd
            def _(pool):
                nc.gpsimd.memset(V[:, :, :, P:P + 1], 1.0).then_inc(ones_col, 1)
                with pool.Fori(0, BATCH) as b:
                    pool.wait_ge(z_used, b)
                    nc.gpsimd.tensor_copy(zbH[:, :], ZH[:, bass.ds(b * SEQ, SEQ)]).then_inc(z_ready, 1)
                    nc.gpsimd.tensor_copy(zbL[:, :], ZL[:, bass.ds(b * SEQ, SEQ)]).then_inc(z_ready, 1)
                    for h in range(H0):
                        pool.wait_ge(aux_max, (b * H0 + h + 1) * LT)
                        nc.gpsimd.tensor_tensor(dmx[:, h % 2, :, :], bc_mid(ident_bf[:, :], LT),
                                                bc_last(mx[:, h % 2, :], P), ALU.mult).then_inc(dmx_ready, 1)
                    pool.wait_ge(acc_step, (b + 1) * H0 * LT)
                    nc.gpsimd.tensor_copy(S[:, bass.ds(b * LT, LT), :], Sb[:, :, :]).then_inc(s_kept, 1)

            @block.scalar
            def _(act):
                with act.Fori(0, BATCH) as b:
                    for n in range(0, NV, 2):
                        act.wait_ge(v_ready, b * NV + n + 1)
                        nc.scalar.copy(V[:, n // 2, 0:4, 0:P], VPS[n % 2]).then_inc(v_even, 1)
                    for h in range(H0 + 1):
                        if h < H0:
                            act.wait_ge(q_ready, b * H0 + h + 1)
                            nc.scalar.copy(qH[:, h % 2, :], QP[:, :]).then_inc(q_hi, 1)
                        if h >= 1:
                            g = h - 1
                            for r in range(LT):
                                act.wait_ge(st_ready, (b * H0 + g) * LT + r + 1)
                                nc.scalar.activation(PT[:, g % 2, r, r * P:SEQ], ST[(g * LT + r) % 3][:, r * P:SEQ],
                                                     ACT.Exp, scale=1.0 / QK_SCALE * SM0).then_inc(p_ready, 1)

            @block.vector
            def _(dve):
                with dve.Fori(0, BATCH) as b:
                    for n in range(1, NV, 2):
                        dve.wait_ge(v_ready, b * NV + n + 1)
                        nc.vector.tensor_copy(V[:, n // 2, 4:8, 0:P], VPS[n % 2]).then_inc(v_odd, 1)
                    for h in range(H0 + 2):
                        if h < H0:
                            dve.wait_ge(q_hi, b * H0 + h + 1)
                            nc.vector.tensor_tensor(qL[:, h % 2, :], QP[:, :], qH[:, h % 2, :],
                                                    ALU.subtract).then_inc(q_lo, 1)
                            for t in range(LT):
                                dve.wait_ge(aux_ready, (b * H0 + h) * LT + t + 1)
                                if t == 0:
                                    if h >= 2:
                                        dve.wait_ge(dmx_ready, b * H0 + h - 1)
                                    else:
                                        dve.wait_ge(dmx_ready, b * H0)
                                i = nc.vector.tensor_reduce(mx[:, h % 2, t:t + 1], AX_[t % 2][:, 0:(t + 1) * P],
                                                            AX.X, ALU.max, negate=True)
                                i.then_inc(aux_max, 1)
                        if h == 0:
                            dve.wait_ge(s_kept, b)
                            nc.vector.memset(Sb[:, :, :], 0.0).then_inc(acc_zero, 1)
                            dve.wait_ge(acc_zero, b + 1)
                        if h >= 2:
                            g = h - 2
                            for k in range(2):
                                dve.wait_ge(o_ready, (b * H0 + g) * 2 + k + 1)
                                if g >= 1:
                                    dve.wait_ge(acc_step, (b * H0 + g) * LT)
                                nc.vector.tensor_scalar(rz[:, 2 * k:2 * k + 2], OP[k][:, :, P], QK_SCALE, None,
                                                        ALU.mult).then_inc(rz_ready, 1)
                                dve.wait_ge(rz_ready, ((b * H0 + g) * 2 + k) * 2 + 1)
                                nc.vector.reciprocal(rz[:, 2 * k:2 * k + 2], rz[:, 2 * k:2 * k + 2]).then_inc(rz_ready, 1)
                                dve.wait_ge(rz_ready, ((b * H0 + g) * 2 + k) * 2 + 2)
                                for t in range(2 * k, 2 * k + 2):
                                    i = nc.vector.scalar_tensor_tensor(
                                        out=Sb[:, t, :], in0=OP[k][:, t - 2 * k, 0:P], scalar=rz[:, t:t + 1],
                                        in1=Sb[:, t, :], op0=ALU.mult, op1=ALU.add)
                                    i.then_inc(acc_step, 1)

            @block.tensor
            def _(pe):
                pe.wait_ge(ones_col, 1)
                with pe.Fori(0, BATCH) as b:
                    pe.wait_ge(z_ready, 2 * b + 2)
                    for n in range(NV):
                        if n >= 2:
                            pe.wait_ge(v_odd if n % 2 else v_even, b * LT + n // 2)
                        r, h = n // 2, 4 * (n % 2)
                        for j, (a, w) in enumerate(((zbH, NH), (zbH, NL), (zbL, NH))):
                            mm = nc.tensor.matmul(ST[n % 2][:, :], a[:, r * P:(r + 1) * P], flat(w[:, h:h + 4, :]),
                                                  start=(j == 0), stop=(j == 2))
                        mm.then_inc(v_ready, 1)

                    def query(h):
                        for j, (a, w) in enumerate(((MH, zbH), (MH, zbL), (ML, zbH))):
                            mm = nc.tensor.matmul(QP[:, :], a[:, h, :], w[:, :], start=(j == 0), stop=(j == 2))
                        mm.then_inc(q_ready, 1)

                    def aux(h):
                        pe.wait_ge(q_hi, b * H0 + h + 1)
                        for t in range(LT):
                            if t >= 2 or h >= 1:
                                pe.wait_ge(aux_max, (b * H0 + h) * LT + t - 1)
                            nc.tensor.matmul(AX_[t % 2][:, 0:(t + 1) * P], qH[:, h % 2, t * P:(t + 1) * P],
                                             zbH[:, 0:(t + 1) * P], start=True, stop=False)
                            nc.tensor.matmul(AX_[t % 2][:, t * P:(t + 1) * P], ident_bf[:, :], cmask[:, 0, :],
                                             start=False, stop=True).then_inc(aux_ready, 1)

                    def scores(h):
                        pe.wait_ge(q_lo, b * H0 + h + 1)
                        pe.wait_ge(dmx_ready, b * H0 + h + 1)
                        if h == 0:
                            pe.wait_ge(v_even, (b + 1) * LT)
                            pe.wait_ge(v_odd, (b + 1) * LT)
                        for r in range(LT):
                            o = slice(r * P, SEQ)
                            k = (h * LT + r) % 3
                            if h * LT + r >= 3:
                                pe.wait_ge(p_ready, (b * H0 + h) * LT + r - 2)
                            bank = ST[k]
                            nc.tensor.matmul(bank[:, o], zbH[:, r * P:(r + 1) * P], qH[:, h % 2, o],
                                             start=True, stop=False)
                            nc.tensor.matmul(bank[:, o], zbL[:, r * P:(r + 1) * P], qH[:, h % 2, o],
                                             start=False, stop=False)
                            nc.tensor.matmul(bank[:, o], zbH[:, r * P:(r + 1) * P], qL[:, h % 2, o],
                                             start=False, stop=False)
                            nc.tensor.matmul(bank[:, r * P:(r + 1) * P], ident_bf[:, :], cmask[:, 1, :],
                                             start=False, stop=False)
                            mm = nc.tensor.matmul(bank[:, o], ones_bf[:, :], flat(dmx[:, h % 2, r:LT, :]),
                                                  start=False, stop=True)
                            mm.then_inc(st_ready, 1)

                    def values(h):
                        pe.wait_ge(p_ready, (b * H0 + h + 1) * LT)
                        if h >= 1:
                            pe.wait_ge(acc_step, (b * H0 + h) * LT)
                        for t in range(LT):
                            for r in range(t + 1):
                                mm = nc.tensor.matmul(OP[t // 2][:, t % 2, :], PT[:, h % 2, r, t * P:(t + 1) * P],
                                                      V[:, r, h, :], start=(r == 0), stop=(r == t))
                            if t % 2:
                                mm.then_inc(o_ready, 1)

                    query(0)
                    aux(0)
                    for h in range(H0):
                        if h + 1 < H0:
                            pe.wait_ge(q_lo, b * H0 + h + 1)
                            query(h + 1)
                            aux(h + 1)
                        scores(h)
                        if h >= 1:
                            values(h - 1)
                    values(H0 - 1)
                    nc.tensor.matmul(QP[:, 0:1], ident_bf[:, :], ident_bf[:, 0:1], start=True, stop=True)\
                        .then_inc(z_used, 1)


def l0_ffn(nc, sb, pb, sem, X, S, UH, UL, wupT, wdnT):
    with ExitStack() as st:
        tu = sb("tu", [P, FF], F16, st)
        td = sb("td", [P, FT, P], F32, st)
        ta = sb("ta", [P, FF], F32, st)
        tb = sb("tb", [P, FF], F32, st)
        ones_f = sb("ones_f", [P, P], F32, st)
        rs = sb("rs", [P, 2], F32, st)
        thr = sb("thr", [P, 2], F32, st)
        nthr = sb("nthr", [P, 2], F32, st)
        Hb = sb("Hb", [P, 2, FT, 512], F32, st)
        H2 = sb("H2", [P, 2, FT, 512], F32, st)
        Y = sb("Y", [P, TILES, P], F32, st)
        ss = sb("ss", [P, TILES], F32, st)
        rr = sb("rr", [P, TILES], F32, st)
        UP = [pb(f"UP{i}", [P, 512], F32, st) for i in range(3)]
        DP = [pb(f"DP{i}", [P, 512], F32, st) for i in range(2)]
        QP = [pb(f"QQ{i}", [P, 512], F32, st) for i in range(2)]
        TP = pb("TPs", [P, 512], F32, st)
        w_step, wsum_ok, tot_ok, tern_ok = sem("w_step"), sem("wsum_ok"), sem("tot_ok"), sem("tern_ok")
        onef_ok = sem("onef_ok")
        up_ok, gelu_ok, sq_ok = sem("up_ok"), sem("gelu_ok"), sem("sq_ok")
        dn_ok, y_ok = sem("dn_ok"), sem("y_ok")
        rms_in, rms_ok, pre_ok, silu_ok, res_step = (sem(n) for n in ("rms_in", "rms_ok", "pre_ok", "silu_ok", "res_step"))
        NCK = TOK // 512

        with nc.Block() as block:
            @block.gpsimd
            def _(pool):
                nc.gpsimd.memset(ones_f[:, :], 1.0).then_inc(onef_ok, 1)

            @block.tensor
            def _(pe):
                pe.wait_ge(onef_ok, 1)
                pe.wait_ge(wsum_ok, 2)
                nc.tensor.matmul(TP[:, 0:2], ones_f[:, :], rs[:, :], start=True, stop=True).then_inc(tot_ok, 1)
                pe.wait_ge(tern_ok, 2)

                def up(c):
                    for f in range(FT):
                        n = c * FT + f
                        if n >= 3:
                            pe.wait_ge(gelu_ok, n - 2)
                        nc.tensor.matmul(UP[n % 3][:, :], tu[:, f * P:(f + 1) * P], UH[:, c * 512:(c + 1) * 512],
                                         start=True, stop=False)
                        nc.tensor.matmul(UP[n % 3][:, :], tu[:, f * P:(f + 1) * P], UL[:, c * 512:(c + 1) * 512],
                                         start=False, stop=True).then_inc(up_ok, 1)

                def down(c):
                    pe.wait_ge(sq_ok, (c + 1) * FT)
                    if c >= 2:
                        pe.wait_ge(y_ok, 2 * (c - 1))
                    for k in range(4):
                        for f in range(FT):
                            nc.tensor.matmul(DP[c % 2][:, k * P:(k + 1) * P], Hb[:, c % 2, f, k * P:(k + 1) * P],
                                             td[:, f, :], start=(f == 0), stop=(f == FT - 1))
                    for k in range(4):
                        for f in range(FT):
                            mm = nc.tensor.matmul(QP[c % 2][:, k:k + 1], H2[:, c % 2, f, k * P:(k + 1) * P],
                                                  ones_f[:, 0:1], start=(f == 0), stop=(f == FT - 1))
                    mm.then_inc(dn_ok, 1)

                for c in range(NCK + 1):
                    if c < NCK:
                        up(c)
                    if c >= 1:
                        down(c - 1)

            @block.scalar
            def _(act):
                for c in range(NCK):
                    for f in range(FT):
                        n = c * FT + f
                        act.wait_ge(up_ok, n + 1)
                        if c >= 2:
                            act.wait_ge(dn_ok, c - 1)
                        nc.scalar.activation(Hb[:, c % 2, f, :], UP[n % 3][:, :], ACT.Gelu).then_inc(gelu_ok, 1)
                act.wait_ge(rms_in, 1)
                nc.scalar.activation(rr[:, :], ss[:, :], ACT.Sqrt).then_inc(rms_ok, 1)
                for c in range(CH):
                    t = slice(c * CT, (c + 1) * CT)
                    act.wait_ge(pre_ok, c + 1)
                    nc.scalar.activation(Y[:, t, :], Y[:, t, :], ACT.Silu).then_inc(silu_ok, 1)

            @block.vector
            def _(dve):
                step = Chain(dve, w_step)
                wd = wdnT[:, :, :].rearrange("p f c -> p (f c)")
                nc.vector.tensor_reduce(rs[:, 0:1], wupT[:, :], AX.X, ALU.add, apply_absolute_value=True).then_inc(wsum_ok, 1)
                nc.vector.tensor_reduce(rs[:, 1:2], wd, AX.X, ALU.add, apply_absolute_value=True).then_inc(wsum_ok, 1)
                dve.wait_ge(tot_ok, 1)
                step(nc.vector.tensor_scalar(thr[:, :], TP[:, 0:2], 0.5 / (FF * DIM), None, ALU.mult))
                step(nc.vector.tensor_scalar(nthr[:, :], thr[:, :], -1.0, None, ALU.mult))
                for k, (w, d) in enumerate(((wupT[:, :], tu[:, :]), (wd, td[:, :, :].rearrange("p f c -> p (f c)")))):
                    step(nc.vector.tensor_scalar(ta[:, :], w, thr[:, k:k + 1], None, ALU.is_gt))
                    step(nc.vector.tensor_scalar(tb[:, :], w, nthr[:, k:k + 1], None, ALU.is_lt))
                    nc.vector.tensor_tensor(d, ta[:, :], tb[:, :], ALU.subtract).then_inc(tern_ok, 1)
                    dve.wait_ge(tern_ok, k + 1)

                def keep(c):
                    dve.wait_ge(dn_ok, c + 1)
                    nc.vector.tensor_copy(Y[:, 4 * c:4 * c + 4, :], DP[c % 2][:, :].rearrange("p (t c) -> p t c", t=4))\
                        .then_inc(y_ok, 1)
                    nc.vector.tensor_copy(ss[:, 4 * c:4 * c + 4], QP[c % 2][:, 0:4]).then_inc(y_ok, 1)

                for c in range(NCK):
                    for f in range(FT):
                        dve.wait_ge(gelu_ok, c * FT + f + 1)
                        if c >= 2:
                            dve.wait_ge(dn_ok, c - 1)
                        nc.vector.tensor_tensor(H2[:, c % 2, f, :], Hb[:, c % 2, f, :], Hb[:, c % 2, f, :],
                                                ALU.mult).then_inc(sq_ok, 1)
                    if c >= 1:
                        keep(c - 1)
                keep(NCK - 1)
                dve.wait_ge(y_ok, 2 * NCK)
                nc.vector.tensor_scalar(ss[:, :], ss[:, :], 1.0 / FF, None, ALU.mult).then_inc(rms_in, 1)
                dve.wait_ge(rms_ok, 1)
                step(nc.vector.tensor_scalar(rr[:, :], rr[:, :], 1e-8, None, ALU.add))
                step(nc.vector.reciprocal(rr[:, :], rr[:, :]))
                for c in range(CH):
                    t = slice(c * CT, (c + 1) * CT)
                    nc.vector.tensor_tensor(Y[:, t, :], Y[:, t, :], bc_last(rr[:, t], P), ALU.mult).then_inc(pre_ok, 1)
                for c in range(CH):
                    t = slice(c * CT, (c + 1) * CT)
                    dve.wait_ge(silu_ok, c + 1)
                    step(nc.vector.tensor_tensor(Y[:, t, :], Y[:, t, :], S[:, t, :], ALU.mult))
                    step(nc.vector.tensor_tensor(X[:, t, :], X[:, t, :], Y[:, t, :], ALU.add))


def layer1(nc, sb, pb, sem, ins, out, X, S, ident, ident_bf, ones_bf, q_d, k_d, v_d, rb_d, ctx_d):
    with ExitStack() as st:
        XN = sb("XN", [P, TILES, DIM], F32, st)
        XT = sb("XT", [P, TOK], F32, st)
        toep = [sb(n, [P, TW], F16, st) for n in ("fwd_hi", "fwd_lo", "bwd_hi", "bwd_lo")]
        l1_prepare(nc, sb, pb, sem, ins, X, XN, XT, toep, ident, q_d, k_d, v_d, rb_d)
        l1_attention(nc, sb, pb, sem, ins, S, toep, ident, ident_bf, ones_bf, q_d, k_d, v_d, rb_d, ctx_d)
        l1_project(nc, sb, pb, sem, ins, XN, S, ident, ctx_d)
        l1_experts(nc, sb, pb, sem, ins, out, X, XT, S, ident)


def l1_prepare(nc, sb, pb, sem, ins, X, XN, XT, toep, ident, q_d, k_d, v_d, rb_d):
    with ExitStack() as st:
        sq = sb("sq1", [P, CT, DIM], F32, st)
        mean = sb("mean1", [P, TILES], F32, st)
        var = sb("var1", [P, TILES], F32, st)
        rstd = sb("rstd1", [P, TILES], F32, st)
        eps = sb("eps1", [P, 1], F32, st)
        w3 = sb("w3", [P, 3, P], F32, st)
        bqk = sb("bqk", [P, 2], F32, st)
        bvr = sb("bvr", [P, P], F32, st)
        tf = sb("tf", [P, 2, TW], F32, st)
        dT = sb("dT", [P, NDIST], F32, st)
        dmax = sb("dmax", [P, 1], F32, st)
        headm = sb("headm", [P, H1], F32, st)
        bound = sb("bound", [P, H1], F32, st)
        qf = sb("qf", [P, 2, 512], F32, st)
        qa = sb("qa", [P, 2, 512], F32, st)
        hs = sb("hs", [P, 2, 2, 512], F16, st)
        vo = sb("vo", [P, 2, 4, H1, DE], F32, st)
        rb = sb("rb", [P, TILES, H1], F32, st)
        TPp = [pb(f"tq{i}", [P, 512], F32, st) for i in range(2)]
        PR = [pb(f"pr{i}", [P, 512], F32, st) for i in range(2)]
        VP = [pb(f"vp{i}", [P, 512], F32, st) for i in range(2)]
        RP = pb("rp", [P, 512], F32, st)
        w_in, t_in, d_in = sem("w1_in"), sem("t_in"), sem("d_in")
        step_s, var_ok, std_ok = sem("p1_step"), sem("var1_ok"), sem("std1_ok")
        eps_ok = sem("eps1_ok")
        xn_ok, tp_ok, xt_ok = sem("xn_ok"), sem("tq_ok"), sem("xt_ok")
        pr_ok, qf_ok, hi_ok, lo_ok = (sem(n) for n in ("pr_ok", "qf_ok", "hi_ok", "lo_ok"))
        qk_out = [sem("q_out"), sem("k_out")]
        abs_ok, rp_ok, rb_ok, rb_out = (sem(n) for n in ("abs_ok", "rp_ok", "rb_ok", "rb_out"))
        vp_ok, vo_ok, vones = (sem(n) for n in ("vp_ok", "vo_ok", "vones"))
        v_out = [sem("v_out0"), sem("v_out1")]
        tab_ok, bound_ok = sem("tab_ok"), sem("bound_ok")
        NCK = TOK // 512

        with nc.Block() as block:
            @block.sync
            def _(sp):
                for k, n in enumerate(("wq", "wk", "wv")):
                    sp.dma_start(w3[:, k, :], ins[n]).then_inc(w_in, 16)
                sp.dma_start(bqk[:, 0:1], ins["bq"].unsqueeze(1)).then_inc(w_in, 16)
                sp.dma_start(bqk[:, 1:2], ins["bk"].unsqueeze(1)).then_inc(w_in, 16)
                sp.dma_start(bvr[:, :], ins["bv"].partition_broadcast(P)).then_inc(w_in, 16)
                sp.dma_start(headm[:, :], ins["head"]).then_inc(w_in, 16)
                for s in range(2):
                    for k, n in enumerate(("toep_f", "toep_b")):
                        sp.dma_start(tf[64 * s:64 * s + 64, k, :], ins[n]).then_inc(t_in, 16)
                for h in range(H1):
                    sp.dma_start(dT[h * D1:(h + 1) * D1, :], ins["distT"]).then_inc(d_in, 16)
                for c in range(NCK):
                    for k, d in enumerate((q_d, k_d)):
                        n = 2 * c + k
                        sp.wait_ge(lo_ok, n + 1)
                        sp.dma_start(d[:, :, c * 512:(c + 1) * 512].rearrange("s p t -> p s t"),
                                     hs[:, n % 2, :, :]).then_inc(qk_out[k], 16)
                    sp.wait_ge(vo_ok, 4 * (c + 1))
                    sp.dma_start(v_d[c * 512:(c + 1) * 512, :].rearrange("(t p) n -> p t n", p=P),
                                 vo[:, c % 2].rearrange("p t h e -> p t (h e)")).then_inc(v_out[c % 2], 16)
                sp.wait_ge(rb_ok, NCK)
                sp.dma_start(rb_d.rearrange("(t p) h -> p t h", p=P), rb[:, :, :]).then_inc(rb_out, 16)
                for k in range(2):
                    sp.wait_ge(qk_out[k], 16 * NCK)
                    sp.wait_ge(v_out[k], 8 * NCK)
                sp.wait_ge(rb_out, 16)

            @block.gpsimd
            def _(pool):
                nc.gpsimd.memset(vo[:, :, :, :, D1:DE], 1.0).then_inc(vones, 1)

            @block.scalar
            def _(act):
                act.wait_ge(eps_ok, 1)
                for c in range(CH):
                    t = slice(c * CT, (c + 1) * CT)
                    act.wait_ge(var_ok, c + 1)
                    nc.scalar.activation(rstd[:, t], var[:, t], ACT.Sqrt, bias=eps[:, 0:1]).then_inc(std_ok, 1)
                    for i in range(2):
                        n = 2 * c + i
                        act.wait_ge(tp_ok, n + 1)
                        nc.scalar.copy(XT[:, n * 512:(n + 1) * 512], TPp[n % 2][:, :]).then_inc(xt_ok, 1)
                act.wait_ge(t_in, 64)
                for k in range(2):
                    nc.scalar.copy(toep[2 * k][:, :], tf[:, k, :]).then_inc(tab_ok, 1)
                act.wait_ge(w_in, 16 * 7)
                for n in range(2 * NCK):
                    act.wait_ge(pr_ok, n + 1)
                    if n >= 2:
                        act.wait_ge(lo_ok, n - 1)
                    if n % 2 == 0 and n >= 2:
                        act.wait_ge(abs_ok, n // 2)
                    nc.scalar.activation(qf[:, n % 2, :], PR[n % 2][:, :], ACT.Identity,
                                         bias=bqk[:, n % 2:n % 2 + 1]).then_inc(qf_ok, 1)
                    act.wait_ge(qf_ok, n + 1)
                    if n >= 2:
                        act.wait_ge(qk_out[n % 2], 16 * (n // 2))
                    nc.scalar.copy(hs[:, n % 2, 0, :], qf[:, n % 2, :]).then_inc(hi_ok, 1)
                    if n % 2 == 0:
                        if n >= 4:
                            act.wait_ge(rp_ok, n // 2 - 1)
                        nc.scalar.activation(qa[:, (n // 2) % 2, :], qf[:, 0, :], ACT.Abs).then_inc(abs_ok, 1)

            @block.vector
            def _(dve):
                step = Chain(dve, step_s)
                nc.vector.memset(eps[:, :], 1e-5).then_inc(eps_ok, 1)
                for c in range(CH):
                    t = slice(c * CT, (c + 1) * CT)
                    norm_stats(dve, nc, step, X, XN, sq, mean, var, c)
                    nc.vector.tensor_scalar(var[:, t], var[:, t], 1.0 / DIM, None, ALU.mult).then_inc(var_ok, 1)
                    dve.wait_ge(std_ok, c + 1)
                    step(nc.vector.reciprocal(rstd[:, t], rstd[:, t]))
                    nc.vector.tensor_tensor(XN[:, t, :], XN[:, t, :], bc_last(rstd[:, t], DIM), ALU.mult).then_inc(xn_ok, 1)
                dve.wait_ge(tab_ok, 2)
                for k in range(2):
                    nc.vector.tensor_tensor(toep[2 * k + 1][:, :], tf[:, k, :], toep[2 * k][:, :], ALU.subtract)
                dve.wait_ge(d_in, 16 * H1)
                step(nc.vector.tensor_reduce(dmax[:, :], dT[:, :], AX.X, ALU.max, apply_absolute_value=True))
                dve.wait_ge(w_in, 16 * 7)
                nc.vector.tensor_scalar(bound[:, :], headm[:, :], dmax[:, 0:1], None, ALU.mult).then_inc(bound_ok, 1)
                dve.wait_ge(vones, 1)
                for c in range(NCK):
                    for k in range(2):
                        n = 2 * c + k
                        dve.wait_ge(hi_ok, n + 1)
                        nc.vector.tensor_tensor(hs[:, n % 2, 1, :], qf[:, n % 2, :], hs[:, n % 2, 0, :],
                                                ALU.subtract).then_inc(lo_ok, 1)
                    if c >= 2:
                        dve.wait_ge(v_out[c % 2], 16 * (c // 2))
                    for k in range(4):
                        if k == 0:
                            dve.wait_ge(vp_ok, c + 1)
                        nc.vector.tensor_tensor(vo[:, c % 2, k, :, 0:D1],
                                                VP[c % 2][:, k * P:(k + 1) * P].rearrange("p (h e) -> p h e", h=H1),
                                                bvr[:, :].rearrange("p (h e) -> p h e", h=H1), ALU.add).then_inc(vo_ok, 1)
                    dve.wait_ge(rp_ok, c + 1)
                    nc.vector.tensor_copy(rb[:, 4 * c:4 * c + 4, :],
                                          RP[:, 0:4 * H1].rearrange("p (t h) -> p t h", t=4)).then_inc(rb_ok, 1)

            @block.tensor
            def _(pe):
                for n in range(NCK):
                    pe.wait_ge(xn_ok, n // 2 + 1)
                    if n >= 2:
                        pe.wait_ge(xt_ok, n - 1)
                    for k in range(4):
                        mm = nc.tensor.transpose(TPp[n % 2][:, k * P:(k + 1) * P], XN[:, 4 * n + k, :], ident[:, :])
                    mm.then_inc(tp_ok, 1)
                pe.wait_ge(w_in, 16 * 7)
                pe.wait_ge(xt_ok, NCK)
                for c in range(NCK):
                    for k in range(2):
                        n = 2 * c + k
                        if n >= 2:
                            pe.wait_ge(qf_ok, n - 1)
                        nc.tensor.matmul(PR[n % 2][:, :], w3[:, k, :], XT[:, c * 512:(c + 1) * 512],
                                         start=True, stop=True).then_inc(pr_ok, 1)
                    if c >= 2:
                        pe.wait_ge(vo_ok, 4 * (c - 1))
                    for k in range(4):
                        mm = nc.tensor.matmul(VP[c % 2][:, k * P:(k + 1) * P],
                                              XT[:, c * 512 + k * P:c * 512 + (k + 1) * P], w3[:, 2, :],
                                              start=True, stop=True)
                    mm.then_inc(vp_ok, 1)
                    pe.wait_ge(abs_ok, c + 1)
                    pe.wait_ge(bound_ok, 1)
                    if c >= 1:
                        pe.wait_ge(rb_ok, c)
                    for k in range(4):
                        mm = nc.tensor.matmul(RP[:, k * H1:(k + 1) * H1], qa[:, c % 2, k * P:(k + 1) * P], bound[:, :],
                                              start=True, stop=True)
                    mm.then_inc(rp_ok, 1)


def l1_attention(nc, sb, pb, sem, ins, S, toep, ident, ident_bf, ones_bf, q_d, k_d, v_d, rb_d, ctx_d):
    fwd_hi, fwd_lo, bwd_hi, bwd_lo = toep
    UPB = NHG * LT
    RC = SEQ // 64
    HALVES = 2 * LT
    with ExitStack() as st:
        kst = sb("kst", [32, NHG, HG, SEQ], F16, st)
        qst = sb("qst", [32, NHG, HG, SEQ], F16, st)
        kd = sb("kd", [P, NHG, HG, SEQ], F16, st)
        qd = sb("qd", [P, NHG, HG, SEQ], F16, st)
        spare = S[:, :, :].rearrange("p t c -> p (t c)")
        nv, ncx = NHG * LT * HG * DE, NHG * LT * HG * D1
        vb = spare[:, 0:nv].rearrange("p (g t n) -> p g t n", g=NHG, t=LT)
        cb = spare[:, nv:nv + ncx].rearrange("p (g t n) -> p g t n", g=NHG, t=LT)
        rbb = sb("rbb", [P, NHG, LT, HG], F32, st)
        gm = sb("gm", [P, JG], F16, st)
        gmf = sb("gmf", [P, JG], F32, st)
        S1 = sb("S1", [P, 2, HG, SEQ], F32, st)
        PT = sb("PT1", [P, 2, LT, HG, P], F32, st)
        dm = sb("dm", [P, 2, HG, P], BF16, st)
        mx = sb("mx1", [P, 2, HG], F32, st)
        rz = sb("rz1", [P, HG], F32, st)
        A = [pb(f"A{i}", [P, 512], F32, st) for i in range(3)]
        B = [pb(f"B{i}", [P, 512], F32, st) for i in range(3)]
        O = [pb(f"O{i}", [P, 512], F32, st) for i in range(2)]
        gm_in, gm_ok = sem("gm_in"), sem("gm_ok")
        spread_in = sem("spread_in")
        stack_in, side_in = [sem(f"stack_in{g}") for g in range(NHG)], [sem(f"side_in{g}") for g in range(NHG)]
        spread_ok = sem("spread_ok")
        a_ready, a_even, a_odd = sem("a_ready"), sem("a_even"), sem("a_odd")
        mx_step, dm_ok = sem("mx_step"), sem("dm_ok")
        b_ready, p_ready = sem("b_ready"), sem("p_ready1")
        o_ready, rz_step, c_ready, c_out = sem("o_ready1"), sem("rz_step"), sem("c_ready"), sem("c_out")
        LOADS = 12

        def v3(bank):
            return bank[:, :].rearrange("p (h c) -> p h c", h=HG)

        with nc.Block() as block:
            @block.gpsimd
            def _(pool):
                pool.dma_start(gmf[:, :], ins["group"]).then_inc(gm_in, 16)
                pool.wait_ge(gm_in, 16)
                nc.gpsimd.tensor_copy(gm[:, :], gmf[:, :]).then_inc(gm_ok, 1)
                pool.wait_ge(gm_ok, 1)

                def load(b, g):
                    hp = slice(g * HG * D1, (g + 1) * HG * D1)
                    for src, dst in ((k_d, kd), (q_d, qd)):
                        for s in range(2):
                            a = src[s, hp, :].rearrange("(h e) (b t) -> b e h t", e=D1, b=BATCH)[b]
                            for j in range(JG):
                                pool.dma_start(dst[64 * s + j:64 * s + 64:JG, g], a).then_inc(spread_in, 16)
                    for src, dst, order in ((k_d, kst, (0, 1, 0, 1)), (q_d, qst, (0, 0, 1, 1))):
                        for i, s in enumerate(order):
                            a = src[s, hp, :].rearrange("(h e) (b t) -> b e h t", e=D1, b=BATCH)[b]
                            pool.dma_start(dst[8 * i:8 * i + 8, g], a).then_inc(stack_in[g], 16)
                    pool.dma_start(vb[:, g], v_d.rearrange("(b t p) (g n) -> b g p t n", p=P, t=LT, g=NHG)[b, g])\
                        .then_inc(side_in[g], 16)
                    pool.dma_start(rbb[:, g], rb_d.rearrange("(b t p) (g n) -> b g p t n", p=P, t=LT, g=NHG)[b, g])\
                        .then_inc(side_in[g], 16)

                def spread(i, g):
                    pool.wait_ge(spread_in, 16 * 32 * (i + 1))
                    for d in (kd, qd):
                        v = d[:, g].rearrange("p h (a j) -> p (h a) j", j=JG)
                        nc.gpsimd.tensor_tensor(v, v, bc_mid(gm[:, :], HG * SEQ // JG), ALU.mult).then_inc(spread_ok, 1)

                with pool.Fori(0, BATCH) as b:
                    for g in range(NHG):
                        pool.wait_ge(c_ready, b * UPB)
                        load(b, g)
                        spread(b * NHG + g, g)
                    pool.wait_ge(c_ready, (b + 1) * UPB)
                    for g in range(NHG):
                        pool.dma_start(ctx_d.rearrange("(b t p) (g n) -> b g p t n", p=P, t=LT, g=NHG)[b, g],
                                       cb[:, g]).then_inc(c_out, 16)
                    pool.wait_ge(c_out, (b + 1) * 16 * NHG)

            @block.tensor
            def _(pe):
                with pe.Fori(0, BATCH) as b:
                    def first(u):
                        g, t = u // LT, u % LT
                        if t == 0:
                            pe.wait_ge(stack_in[g], (b + 1) * 16 * 8)
                            pe.wait_ge(spread_ok, (b * NHG + g + 1) * 2)
                        for c in range(RC):
                            n = u * RC + c
                            if n >= 3:
                                m = n - 3
                                pe.wait_ge(a_even if m % 2 == 0 else a_odd, b * (UPB * RC // 2) + m // 2 + 1)
                            v = v3(A[n % 3])
                            for h in range(HG):
                                nc.tensor.matmul(v[:, h, :], qst[:, g, h, t * P:(t + 1) * P],
                                                 kst[:, g, h, c * 64:(c + 1) * 64],
                                                 start=(h == 0), stop=False, skip_group_check=True)
                            for a in range(NG):
                                r = c * 64 + a * JG
                                y = t * P - r + TOFF
                                for tab in (fwd_hi, fwd_lo):
                                    mm = nc.tensor.matmul(v[:, :, a * JG:(a + 1) * JG], tab[:, y:y + P],
                                                          kd[:, g, :, r:r + JG], start=False,
                                                          stop=(a == NG - 1 and tab is fwd_lo), skip_group_check=True)
                            mm.then_inc(a_ready, 1)

                    def second(u):
                        g, t = u // LT, u % LT
                        pe.wait_ge(dm_ok, b * UPB + u + 1)
                        for k in range(HALVES):
                            n = u * HALVES + k
                            if n >= 3:
                                pe.wait_ge(p_ready, b * (UPB * HALVES) + n - 2)
                            half, r = k // LT, k % LT
                            v = v3(B[n % 3])
                            nc.tensor.matmul(B[n % 3][:, :], ones_bf[:, :], dm[:, u % 2, :, half * 64:(half + 1) * 64],
                                             start=True, stop=False, skip_group_check=True)
                            for a in range(NG):
                                l = t * P + half * 64 + a * JG
                                y = r * P - l + TOFF
                                for tab in (bwd_hi, bwd_lo):
                                    nc.tensor.matmul(v[:, :, a * JG:(a + 1) * JG], tab[:, y:y + P],
                                                     qd[:, g, :, l:l + JG], start=False, stop=False,
                                                     skip_group_check=True)
                            for h in range(HG):
                                mm = nc.tensor.matmul(v[:, h, :], S1[:, u % 2, h, r * P:(r + 1) * P],
                                                      ident[:, half * 64:(half + 1) * 64], start=False,
                                                      stop=(h == HG - 1), skip_group_check=True)
                            mm.then_inc(b_ready, 1)

                    def values(u):
                        g, t = u // LT, u % LT
                        pe.wait_ge(p_ready, (b * UPB + u + 1) * HALVES)
                        if u >= 2:
                            pe.wait_ge(c_ready, b * UPB + u - 1)
                        if t == 0:
                            pe.wait_ge(side_in[g], (b + 1) * 32)
                        for h in range(HG):
                            for r in range(LT):
                                mm = nc.tensor.matmul(O[u % 2][:, h * DE:(h + 1) * DE], PT[:, u % 2, r, h, :],
                                                      vb[:, g, r, h * DE:(h + 1) * DE], start=(r == 0), stop=(r == LT - 1))
                        mm.then_inc(o_ready, 1)

                    for u in range(UPB + 2):
                        if u < UPB:
                            first(u)
                        if u >= 2:
                            values(u - 2)
                        if 1 <= u <= UPB:
                            second(u - 1)

            @block.scalar
            def _(act):
                with act.Fori(0, BATCH) as b:
                    for u in range(UPB + 1):
                        if u < UPB:
                            for c in range(0, RC, 2):
                                act.wait_ge(a_ready, (b * UPB + u) * RC + c + 1)
                                nc.scalar.copy(S1[:, u % 2, :, c * 64:(c + 1) * 64], v3(A[(u * RC + c) % 3])).then_inc(a_even, 1)
                        if u >= 1:
                            for k in range(HALVES):
                                act.wait_ge(b_ready, (b * UPB + u - 1) * HALVES + k + 1)
                                half, r = k // LT, k % LT
                                nc.scalar.activation(PT[:, (u - 1) % 2, r, :, half * 64:(half + 1) * 64],
                                                     v3(B[((u - 1) * HALVES + k) % 3]), ACT.Exp, scale=SM1).then_inc(p_ready, 1)

            @block.vector
            def _(dve):
                with dve.Fori(0, BATCH) as b:
                    for u in range(UPB + 2):
                        if u < UPB:
                            g, t = u // LT, u % LT
                            for c in range(1, RC, 2):
                                dve.wait_ge(a_ready, (b * UPB + u) * RC + c + 1)
                                nc.vector.tensor_copy(S1[:, u % 2, :, c * 64:(c + 1) * 64], v3(A[(u * RC + c) % 3])).then_inc(a_odd, 1)
                            dve.wait_ge(a_even, (b * UPB + u + 1) * (RC // 2))
                            dve.wait_ge(a_odd, (b * UPB + u + 1) * (RC // 2))
                            nc.vector.tensor_reduce(mx[:, u % 2, :], S1[:, u % 2, :, :], AX.X, ALU.max).then_inc(mx_step, 1)
                            if t == 0:
                                dve.wait_ge(side_in[g], (b + 1) * 32)
                            dve.wait_ge(mx_step, (b * UPB + u) * 2 + 1)
                            nc.vector.scalar_tensor_tensor(out=mx[:, u % 2, :], in0=mx[:, u % 2, :], scalar=-1.0,
                                                           in1=rbb[:, g, t, :], op0=ALU.mult, op1=ALU.subtract).then_inc(mx_step, 1)
                            dve.wait_ge(mx_step, (b * UPB + u) * 2 + 2)
                            nc.vector.tensor_tensor(dm[:, u % 2, :, :], bc_mid(ident_bf[:, :], HG),
                                                    bc_last(mx[:, u % 2, :], P), ALU.mult).then_inc(dm_ok, 1)
                        if u >= 2:
                            w = u - 2
                            g, t = w // LT, w % LT
                            dve.wait_ge(o_ready, b * UPB + w + 1)
                            if w == 0:
                                dve.wait_ge(c_out, b * 16 * NHG)
                            dve.wait_ge(c_ready, b * UPB + w)
                            o = O[w % 2][:, 0:HG * DE].rearrange("p (h e) -> p h e", h=HG)
                            nc.vector.reciprocal(rz[:, :], o[:, :, D1]).then_inc(rz_step, 1)
                            dve.wait_ge(rz_step, b * UPB + w + 1)
                            nc.vector.tensor_tensor(cb[:, g, t, :].rearrange("p (h e) -> p h e", h=HG), o[:, :, 0:D1],
                                                    bc_last(rz[:, :], D1), ALU.mult).then_inc(c_ready, 1)


def l1_project(nc, sb, pb, sem, ins, XN, S, ident, ctx_d):
    with ExitStack() as st:
        C = sb("C", [P, TILES, DIM], F32, st)
        CTt = sb("CTt", [P, 2, 512], F32, st)
        wo = sb("wo1", [P, P], F32, st)
        rows = sb("rows", [P, 3, P], F32, st)
        sq = sb("sq2", [P, CT, DIM], F32, st)
        mean = sb("mean2", [P, TILES], F32, st)
        var = sb("var2", [P, TILES], F32, st)
        rstd = sb("rstd2", [P, TILES], F32, st)
        eps = sb("eps2", [P, 1], F32, st)
        TPp = [pb(f"tc{i}", [P, 512], F32, st) for i in range(2)]
        PR = [pb(f"pc{i}", [P, 512], F32, st) for i in range(2)]
        c_in, w_in = [sem(f"ctx_in{c}") for c in range(CH)], sem("wo_in")
        step_s, var_ok, std_ok, eps_ok = sem("p2_step"), sem("var2_ok"), sem("std2_ok"), sem("eps2_ok")
        tp_ok, ct_ok, pr_ok, h_ok = sem("tc_ok"), sem("ct_ok"), sem("pc_ok"), sem("h_ok")
        NCK = TOK // 512
        with nc.Block() as block:
            @block.sync
            def _(sp):
                for c in range(CH):
                    t = slice(c * CT, (c + 1) * CT)
                    sp.dma_start(C[:, t, :], ctx_d.rearrange("(t p) n -> p t n", p=P)[:, t, :]).then_inc(c_in[c], 16)
                sp.dma_start(wo[:, :], ins["wo"]).then_inc(w_in, 16)
                for k, n in enumerate(("bo", "ln_g", "ln_b")):
                    sp.dma_start(rows[:, k, :], ins[n].partition_broadcast(P)).then_inc(w_in, 16)

            @block.tensor
            def _(pe):
                for n in range(NCK + 1):
                    if n < NCK:
                        pe.wait_ge(c_in[n // 2], 16)
                        if n >= 2:
                            pe.wait_ge(ct_ok, n - 1)
                        for k in range(4):
                            mm = nc.tensor.transpose(TPp[n % 2][:, k * P:(k + 1) * P], C[:, 4 * n + k, :], ident[:, :])
                        mm.then_inc(tp_ok, 1)
                    if n >= 1:
                        m = n - 1
                        if m == 0:
                            pe.wait_ge(w_in, 64)
                        pe.wait_ge(ct_ok, m + 1)
                        if m >= 2:
                            pe.wait_ge(h_ok, m - 1)
                        for k in range(4):
                            mm = nc.tensor.matmul(PR[m % 2][:, k * P:(k + 1) * P], CTt[:, m % 2, k * P:(k + 1) * P],
                                                  wo[:, :], start=True, stop=True)
                        mm.then_inc(pr_ok, 1)

            @block.scalar
            def _(act):
                for n in range(NCK):
                    act.wait_ge(tp_ok, n + 1)
                    if n >= 2:
                        act.wait_ge(pr_ok, n - 1)
                    nc.scalar.copy(CTt[:, n % 2, :], TPp[n % 2][:, :]).then_inc(ct_ok, 1)
                act.wait_ge(eps_ok, 1)
                for c in range(CH):
                    t = slice(c * CT, (c + 1) * CT)
                    act.wait_ge(var_ok, c + 1)
                    nc.scalar.activation(rstd[:, t], var[:, t], ACT.Sqrt, bias=eps[:, 0:1]).then_inc(std_ok, 1)

            @block.vector
            def _(dve):
                step = Chain(dve, step_s)
                nc.vector.memset(eps[:, :], 1e-12).then_inc(eps_ok, 1)
                dve.wait_ge(w_in, 64)
                step(nc.vector.tensor_tensor(XN[:, :, :], XN[:, :, :], bc_mid(rows[:, 0, :], TILES), ALU.add))
                for n in range(NCK):
                    dve.wait_ge(pr_ok, n + 1)
                    t = slice(4 * n, 4 * n + 4)
                    nc.vector.tensor_tensor(S[:, t, :], PR[n % 2][:, :].rearrange("p (t c) -> p t c", t=4),
                                            XN[:, t, :], ALU.add).then_inc(h_ok, 1)
                dve.wait_ge(h_ok, NCK)
                for c in range(CH):
                    t = slice(c * CT, (c + 1) * CT)
                    norm_stats(dve, nc, step, S, S, sq, mean, var, c)
                    nc.vector.tensor_scalar(var[:, t], var[:, t], 1.0 / DIM, None, ALU.mult).then_inc(var_ok, 1)
                    dve.wait_ge(std_ok, c + 1)
                    step(nc.vector.reciprocal(rstd[:, t], rstd[:, t]))
                    step(nc.vector.tensor_tensor(S[:, t, :], S[:, t, :], bc_last(rstd[:, t], DIM), ALU.mult))
                    step(nc.vector.tensor_tensor(S[:, t, :], S[:, t, :], bc_mid(rows[:, 1, :], CT), ALU.mult))
                    step(nc.vector.tensor_tensor(S[:, t, :], S[:, t, :], bc_mid(rows[:, 2, :], CT), ALU.add))


def l1_experts(nc, sb, pb, sem, ins, out, X, XT, S, ident):
    with ExitStack() as st:
        wr = sb("wr", [P, NEXP], F32, st)
        wg = sb("wg", [P, PAIRS + 1, P], F32, st)
        wu = sb("wu", [P, PAIRS + 1, P], F32, st)
        wd = sb("wd", [P, PAIRS + 1, P], F32, st)
        pkf = sb("pkf", [2 * NEXP, PAIRS, P], F32, st)
        pk = sb("pk", [2 * NEXP, PAIRS, P], F16, st)
        L = sb("L", [P, TILES, NEXP + 6], F32, st)
        best = sb("best", [P, TILES, 8], F32, st)
        rest = sb("rest", [P, TILES, NEXP + 6], F32, st)
        lm = sb("lm", [P, TILES], F32, st)
        cwT = sb("cwT", [2 * NEXP, TOK], F16, st)
        cl = sb("cl", [P, TILES, 2 * NEXP], F16, st)
        idh = sb("idh", [P, P], F16, st)
        sg = sb("sgs", [P, 2, 512], F32, st)
        hb = sb("hb", [P, 2, 512], F32, st)
        Y = sb("Y1", [P, TILES, P], F32, st)
        G = [pb(f"G{i}", [P, 512], F32, st) for i in range(2)]
        U = [pb(f"U{i}", [P, 512], F32, st) for i in range(2)]
        W = [pb(f"W{i}", [P, 512], F32, st) for i in range(2)]
        Dn = [pb(f"D{i}", [P, 512], F32, st) for i in range(2)]
        w_in, r_in = sem("we_in"), sem("wr_in")
        step_s, log_ok, log_used = sem("p3_step"), sem("log_ok"), sem("log_used")
        exp_in, exp_ok, best_ok, cw_ok = sem("exp_in"), sem("exp_ok"), sem("best_ok"), sem("cw_ok")
        ct_ok, ct_used, pk_ok, idh_ok = sem("cwt_ok"), sem("cwt_used"), sem("pk_ok"), sem("idh_ok")
        gu_ok, silu_ok, h2_ok = sem("gu_ok"), sem("sg_ok"), sem("h2_ok")
        dn_ok, y_ok, s_ok, out_ok, stored = sem("dn2_ok"), sem("y2_ok"), sem("s2_ok"), sem("out_ok"), sem("stored")
        NCK, NP = TOK // 512, PAIRS + 1
        out_v = out.rearrange("b (t p) c -> p (b t) c", p=P)
        with nc.Block() as block:
            @block.sync
            def _(sp):
                sp.dma_start(wr[:, :], ins["wr"]).then_inc(r_in, 16)
                for d, n, s in ((wg, "wg", "sg"), (wu, "wu", "su")):
                    sp.dma_start(d[:, 0:PAIRS, :].rearrange("p k (e f) -> p (k e) f", e=2),
                                 ins[n].rearrange("e d f -> d e f")).then_inc(w_in, 16)
                    sp.dma_start(d[:, PAIRS, :], ins[s]).then_inc(w_in, 16)
                sp.dma_start(wd[:, 0:PAIRS, :], ins["wd"].rearrange("(k e) f d -> (e f) k d", e=2)).then_inc(w_in, 16)
                sp.dma_start(wd[:, PAIRS, :], ins["sd"]).then_inc(w_in, 16)
                sp.dma_start(pkf[:, :, :], ins["pick"]).then_inc(w_in, 16)
                for c in range(CH):
                    t = slice(c * CT, (c + 1) * CT)
                    sp.wait_ge(out_ok, c + 1)
                    sp.dma_start(out_v[:, t, :], Y[:, t, :]).then_inc(stored, 16)
                sp.wait_ge(stored, 16 * CH)

            @block.gpsimd
            def _(pool):
                nc.gpsimd.tensor_copy(idh[:, :], ident[:, :]).then_inc(idh_ok, 1)
                pool.wait_ge(w_in, 16 * 7)
                nc.gpsimd.tensor_copy(pk[:, :, :], pkf[:, :, :]).then_inc(pk_ok, 1)

            @block.tensor
            def _(pe):
                pe.wait_ge(r_in, 16)
                for t in range(TILES):
                    mm = nc.tensor.matmul(G[0][:, t * NEXP:(t + 1) * NEXP], XT[:, t * P:(t + 1) * P], wr[:, :],
                                          start=True, stop=True)
                mm.then_inc(log_ok, 1)
                pe.wait_ge(idh_ok, 1)
                pe.wait_ge(cw_ok, 1)
                for n in range(NCK):
                    if n >= 2:
                        pe.wait_ge(ct_used, n - 1)
                    for k in range(4):
                        mm = nc.tensor.matmul(W[n % 2][0:2 * NEXP, k * P:(k + 1) * P], cl[:, 4 * n + k, :],
                                              idh[:, :], start=True, stop=True)
                    mm.then_inc(ct_ok, 1)
                pe.wait_ge(w_in, 16 * 7)
                pe.wait_ge(pk_ok, 1)
                pe.wait_ge(ct_used, NCK)

                def up(n):
                    c, p = n // NP, n % NP
                    x = XT[:, c * 512:(c + 1) * 512]
                    if n >= 2:
                        pe.wait_ge(h2_ok, n - 1)
                    nc.tensor.matmul(G[n % 2][:, :], wg[:, p, :], x, start=True, stop=True)
                    if p < PAIRS:
                        nc.tensor.matmul(W[n % 2][:, :], pk[:, p, :], cwT[:, c * 512:(c + 1) * 512],
                                         start=True, stop=True)
                    nc.tensor.matmul(U[n % 2][:, :], wu[:, p, :], x, start=True, stop=True).then_inc(gu_ok, 1)

                def down(n):
                    c, p = n // NP, n % NP
                    pe.wait_ge(h2_ok, n + 1)
                    if p == 0 and c >= 2:
                        pe.wait_ge(y_ok, c - 1)
                    for k in range(4):
                        mm = nc.tensor.matmul(Dn[c % 2][:, k * P:(k + 1) * P], hb[:, n % 2, k * P:(k + 1) * P],
                                              wd[:, p, :], start=(p == 0 and k == 0), stop=(p == NP - 1),
                                              skip_group_check=True)
                    mm.then_inc(dn_ok, 1)

                for n in range(NCK * NP + 1):
                    if n < NCK * NP:
                        up(n)
                    if n >= 1:
                        down(n - 1)

            @block.scalar
            def _(act):
                act.wait_ge(exp_in, 1)
                nc.scalar.activation(L[:, :, 0:NEXP], L[:, :, 0:NEXP], ACT.Exp).then_inc(exp_ok, 1)
                for n in range(NCK):
                    act.wait_ge(ct_ok, n + 1)
                    nc.scalar.copy(cwT[:, n * 512:(n + 1) * 512], W[n % 2][0:2 * NEXP, :]).then_inc(ct_used, 1)
                for n in range(NCK * NP):
                    act.wait_ge(gu_ok, n + 1)
                    if n >= 2:
                        act.wait_ge(h2_ok, n - 1)
                    nc.scalar.activation(sg[:, n % 2, :], G[n % 2][:, :], ACT.Silu).then_inc(silu_ok, 1)
                for c in range(CH):
                    t = slice(c * CT, (c + 1) * CT)
                    act.wait_ge(y_ok, 2 * c + 2)
                    nc.scalar.activation(Y[:, t, :], Y[:, t, :], ACT.Silu).then_inc(s_ok, 1)

            @block.vector
            def _(dve):
                step = Chain(dve, step_s)
                step(nc.vector.memset(L[:, :, NEXP:NEXP + 6], -1.0))
                dve.wait_ge(log_ok, 1)
                lv = L[:, :, 0:NEXP]
                lp = G[0][:, :].rearrange("p (t e) -> p t e", e=NEXP)
                step(nc.vector.tensor_reduce(lm[:, :], lp, AX.X, ALU.max))
                nc.vector.tensor_tensor(lv, lp, bc_last(lm[:, :], NEXP), ALU.subtract).then_inc(exp_in, 1)
                dve.wait_ge(exp_ok, 1)
                step(nc.vector.tensor_reduce(lm[:, :], lv, AX.X, ALU.add))
                step(nc.vector.reciprocal(lm[:, :], lm[:, :]))
                step(nc.vector.tensor_tensor(lv, lv, bc_last(lm[:, :], NEXP), ALU.mult))
                for t in range(TILES):
                    i = nc.vector.max(best[:, t, :], L[:, t, :])
                    i.then_inc(best_ok, 1)
                dve.wait_ge(best_ok, TILES)
                step(nc.vector.memset(best[:, :, 2:8], -1.0))
                for t in range(TILES):
                    nc.vector.match_replace(rest[:, t, :], best[:, t, :], L[:, t, :], 0.0).then_inc(best_ok, 1)
                dve.wait_ge(best_ok, 2 * TILES)
                step(nc.vector.tensor_tensor(lv, lv, rest[:, :, 0:NEXP], ALU.subtract))
                step(nc.vector.tensor_copy(cl[:, :, 0:NEXP], lv))
                nc.vector.tensor_tensor(cl[:, :, NEXP:2 * NEXP], lv, cl[:, :, 0:NEXP], ALU.subtract).then_inc(cw_ok, 1)
                for n in range(NCK * NP):
                    c, p = n // NP, n % NP
                    dve.wait_ge(silu_ok, n + 1)
                    if n >= 2:
                        dve.wait_ge(dn_ok, n - 1)
                    if p == PAIRS:
                        nc.vector.tensor_tensor(hb[:, n % 2, :], U[n % 2][:, :], sg[:, n % 2, :], ALU.mult).then_inc(h2_ok, 1)
                    else:
                        step(nc.vector.tensor_tensor(hb[:, n % 2, :], U[n % 2][:, :], sg[:, n % 2, :], ALU.mult))
                        nc.vector.tensor_tensor(hb[:, n % 2, :], hb[:, n % 2, :], W[n % 2][:, :], ALU.mult).then_inc(h2_ok, 1)
                    if p == 0 and c >= 1:
                        keep2(nc, dve, dn_ok, y_ok, Y, Dn, c - 1, NP)
                keep2(nc, dve, dn_ok, y_ok, Y, Dn, NCK - 1, NP)
                for c in range(CH):
                    t = slice(c * CT, (c + 1) * CT)
                    dve.wait_ge(s_ok, c + 1)
                    step(nc.vector.tensor_tensor(Y[:, t, :], Y[:, t, :], S[:, t, :], ALU.mult))
                    nc.vector.tensor_tensor(Y[:, t, :], Y[:, t, :], X[:, t, :], ALU.add).then_inc(out_ok, 1)


def keep2(nc, dve, dn_ok, y_ok, Y, Dn, c, NP):
    dve.wait_ge(dn_ok, (c + 1) * NP)
    nc.vector.tensor_copy(Y[:, 4 * c:4 * c + 4, :], Dn[c % 2][:, :].rearrange("p (t c) -> p t c", t=4)).then_inc(y_ok, 1)


def kernel(**inputs):
    import numpy as _np
    import concourse.bacc as _bacc
    from concourse import mybir as _mybir
    from concourse.bass_utils import run_bass_kernel_spmd as _run

    a = {k: _np.asarray(v) for k, v in inputs.items()}
    dist = a["L1_attn_dist_emb"]
    delta = _np.arange(-(SEQ - 1), SEQ) + M_REL - 1
    row = _np.clip(_np.where(delta < 0, delta + NDIST, delta), 0, NDIST - 1)
    y = _np.arange(TW)
    e_of, j_of = _np.repeat(_np.arange(D1), JG), _np.tile(_np.arange(JG), D1)
    fwd = row[(y[None, :] - TOFF - j_of[:, None]) + SEQ - 1]
    bwd = row[(j_of[:, None] - (y[None, :] - TOFF)) + SEQ - 1]
    eye = _np.eye(P, dtype=_np.float32)
    key_after = _np.triu(_np.ones((P, P), _np.float32), k=1) * _np.float32(NEG)
    group = _np.zeros((P, JG), _np.float32)
    group[_np.arange(P), _np.arange(P) % JG] = 1.0
    head = _np.zeros((P, H1), _np.float32)
    head[_np.arange(P), _np.arange(P) // D1] = 1.0
    pick = _np.zeros((2 * NEXP, PAIRS, P), _np.float32)
    for e in range(NEXP):
        pick[[e, NEXP + e], e // 2, (e % 2) * FE:(e % 2 + 1) * FE] = 1.0
    host = {
        "x": a["L0_attn_x"], "gamma": a["L0_attn_gamma"], "w_qkv": a["L0_attn_w_qkv"],
        "w_outT": a["L0_attn_w_out"].T, "w_upT": a["L0_ffn_w_up"].T, "w_downT": a["L0_ffn_w_down"].T,
        "wq": a["L1_attn_Wq"], "bq": a["L1_attn_bq"], "wk": a["L1_attn_Wk"], "bk": a["L1_attn_bk"],
        "wv": a["L1_attn_Wv"], "bv": a["L1_attn_bv"], "wo": a["L1_attn_Wo"], "bo": a["L1_attn_bo"],
        "ln_g": a["L1_attn_ln_gamma"], "ln_b": a["L1_attn_ln_beta"],
        "toep_f": dist[fwd, e_of[:, None]], "toep_b": dist[bwd, e_of[:, None]], "distT": dist.T,
        "wr": a["L1_ffn_Wr"], "wg": a["L1_ffn_Wg"], "wu": a["L1_ffn_Wu"], "wd": a["L1_ffn_Wd"],
        "sg": a["L1_ffn_Sg"], "su": a["L1_ffn_Su"], "sd": a["L1_ffn_Sd"],
        "identity": eye, "causal": _np.stack([key_after, key_after.T]), "group": group, "head": head,
        "pick": pick,
    }
    nc = _bacc.Bacc("TRN2", target_bir_lowering=False, num_devices=1)
    arrays, ins = {}, {}
    for name, value in host.items():
        value = _np.ascontiguousarray(value)
        arrays[f"in_{name}"] = value
        ins[name] = nc.dram_tensor(f"in_{name}", value.shape, _mybir.dt.from_np(value.dtype),
                                   kind="ExternalInput").ap()
    out = nc.dram_tensor("out_x", (BATCH, SEQ, DIM), F32, kind="ExternalOutput").ap()
    build(nc, ins, out)
    r = _run(nc, [arrays], core_ids=[0])
    return r.results[0]["out_x"]
```

```python
from contextlib import ExitStack

import concourse.bass as bass
from concourse import mybir

F32 = mybir.dt.float32
F16 = mybir.dt.float16
BF16 = mybir.dt.bfloat16
ALU = mybir.AluOpType
ACT = mybir.ActivationFunctionType
AX = mybir.AxisListType

P = 128
BATCH, SEQ, DIM = 8, 512, 128
TOK = BATCH * SEQ
TILES = TOK // P
LT = SEQ // P
CH = 4
CT = TILES // CH
H0 = 8
FF = 512
FT = FF // P
H1, D1 = 16, 8
HG = 8
NHG = H1 // HG
DE = D1 + 1
DV = DE + D1
Q_STACK = (0, 1, 1, 0)
K_STACK = (0, 1, 0, 1)
M_REL = 128
NDIST = 2 * M_REL - 1
JG = 8
NG = 64 // JG
TW = 2 * SEQ - JG
TOFF = SEQ - JG
NEXP, FE, PAIRS = 16, 64, 8
QK_SCALE = 64.0
SM0 = float(P) ** -0.5
SM1 = float(D1) ** -0.5
NEG = -1.0e30


def flat(ap):
    return ap.rearrange("p a b -> p (a b)")


def bc_last(col, n):
    return col.unsqueeze(2).to_broadcast([col.shape[0], col.shape[1], n])


def bc_mid(row, a):
    return row.unsqueeze(1).to_broadcast([row.shape[0], a, row.shape[1]])


def build(nc, ins, out):
    ctx = ExitStack()
    with ctx:
        def sb(name, shape, dt=F32, stack=ctx):
            return stack.enter_context(nc.sbuf_tensor(name, shape, dt))

        def pb(name, shape, dt=F32, stack=ctx):
            return stack.enter_context(nc.psum_tensor(name, shape, dt))

        live = []

        def sem(name):
            live.append(nc.alloc_semaphore(name=name))
            return live[-1]

        def renew_semaphores():
            nc.all_engine_barrier()
            nc.clear_and_free_semaphores(list(live))
            live.clear()
            nc.all_engine_barrier()

        def scratch(name, shape, dt):
            return nc.dram_tensor(name, shape, dt, kind="Internal").ap()

        X = sb("X", [P, TILES, DIM])
        S = sb("S", [P, TILES, DIM])
        ident = sb("ident", [P, P])
        ident_bf = sb("ident_bf", [P, P], BF16)
        ones_bf = sb("ones_bf", [P, P], BF16)
        q_d = scratch("q_stack", (H1, 4, D1, TOK), F16)
        k_d = scratch("k_stack", (H1, 4, D1, TOK), F16)
        v_d = scratch("v_split", (TOK, H1 * DV), F16)
        rb_d = scratch("rel_bound", (TOK, H1), F32)
        ctx_d = scratch("context", (TOK, DIM), F32)

        layer0(nc, sb, pb, sem, ins, X, S, ident, ident_bf, ones_bf)
        renew_semaphores()
        layer1(nc, sb, pb, sem, ins, out, X, S, ident, ident_bf, ones_bf, (q_d, k_d, v_d, rb_d, ctx_d))


def norm_stats(dve, nc, step, src, dst, sq, mean, var, c):
    t = slice(c * CT, (c + 1) * CT)
    step(nc.vector.tensor_reduce(mean[:, t], src[:, t, :], AX.X, ALU.add))
    step(nc.vector.tensor_scalar(mean[:, t], mean[:, t], 1.0 / DIM, None, ALU.mult))
    step(nc.vector.tensor_tensor(dst[:, t, :], src[:, t, :], bc_last(mean[:, t], DIM), ALU.subtract))
    step(nc.vector.tensor_tensor(sq[:, :, :], dst[:, t, :], dst[:, t, :], ALU.mult))
    step(nc.vector.tensor_reduce(var[:, t], sq[:, :, :], AX.X, ALU.add))


def wait_for(eng, s, value):
    if not isinstance(value, int) or value > 0:
        eng.wait_ge(s, value)


class Chain:

    def __init__(self, eng, s):
        self.eng, self.s, self.n = eng, s, 0

    def __call__(self, ins):
        self.n += 1
        ins.then_inc(self.s, 1)
        self.eng.wait_ge(self.s, self.n)


def layer0(nc, sb, pb, sem, ins, X, S, ident, ident_bf, ones_bf):
    with ExitStack() as st:
        ZH = sb("ZH", [P, TOK], F16, st)
        ZL = sb("ZL", [P, TOK], F16, st)
        UH = sb("UH", [P, TOK], F16, st)
        UL = sb("UL", [P, TOK], F16, st)
        MH = sb("MH", [P, H0, P], F16, st)
        ML = sb("ML", [P, H0, P], F16, st)
        NH = sb("NH", [P, H0, P], F16, st)
        NL = sb("NL", [P, H0, P], F16, st)
        cmask = sb("cmask", [P, 2, P], BF16, st)
        wupT = sb("wupT", [P, FF], F32, st)
        wdnT = sb("wdnT", [P, FT, P], F32, st)
        l0_prepare(nc, sb, pb, sem, ins, X, S, ident, ident_bf, ones_bf,
                   ZH, ZL, UH, UL, MH, ML, NH, NL, cmask, wupT, wdnT)
        l0_attention(nc, sb, pb, sem, S, ident_bf, ones_bf, ZH, ZL, MH, ML, NH, NL, cmask)
        l0_ffn(nc, sb, pb, sem, X, S, UH, UL, wupT, wdnT)


def l0_prepare(nc, sb, pb, sem, ins, X, S, ident, ident_bf, ones_bf,
               ZH, ZL, UH, UL, MH, ML, NH, NL, cmask, wupT, wdnT):
    with ExitStack() as st:
        XC = sb("XC", [P, TILES, DIM], F32, st)
        Z = sb("Z", [P, 2, CT, DIM], F32, st)
        U = sb("U", [P, 2, CT, DIM], F32, st)
        sq = sb("sq0", [P, CT, DIM], F32, st)
        mean = sb("mean0", [P, TILES], F32, st)
        var = sb("var0", [P, TILES], F32, st)
        rstd = sb("rstd0", [P, TILES], F32, st)
        l2 = sb("l2", [P, TILES], F32, st)
        za = sb("za", [P, TILES], F32, st)
        ub = sb("ub", [P, TILES], F32, st)
        gamma = sb("gamma", [P, DIM], F32, st)
        wqkv = sb("wqkv", [P, 3 * H0, P], F32, st)
        woT = sb("woT", [P, H0, P], F32, st)
        cmf = sb("cmf", [P, 2, P], F32, st)
        eps = sb("eps0", [P, 1], F32, st)
        tp = [pb(f"tp{i}", [P, 512], F32, st) for i in range(4)]
        wp = [pb(f"wp{i}", [P, 512], F32, st) for i in range(2)]
        x_in = [sem(f"x_in{c}") for c in range(CH)]
        w_in, g_in, k_in = sem("w_in"), sem("g_in"), sem("k_in")
        dve_step, act_step = sem("p0_dve_step"), sem("p0_act_step")
        var_ok, rstd_ok, l2_ok, zu_ok = sem("var_ok"), sem("std_ok"), sem("l2_ok"), sem("zu_ok")
        l2_in = sem("l2_in")
        tp_ok, tp_hi, tp_lo = sem("tp_ok"), sem("tp_hi"), sem("tp_lo")
        wp_ok, wp_hi, wp_lo = sem("wp_ok"), sem("wp_hi"), sem("wp_lo")
        eps_ok, s_zero = sem("eps_ok"), sem("s_zero")
        pool_ok = sem("p0_pool")
        x_v = ins["x"].rearrange("b (t p) c -> p (b t) c", p=P)

        with nc.Block() as block:
            @block.sync
            def _(sp):
                for c in range(CH):
                    t = slice(c * CT, (c + 1) * CT)
                    sp.dma_start(X[:, t, :], x_v[:, t, :]).then_inc(x_in[c], 16)
                sp.dma_start(wqkv[:, :, :], ins["w_qkv"].rearrange("(k d) c -> d k c", d=P)).then_inc(w_in, 16)
                sp.dma_start(woT[:, :, :], ins["w_outT"].rearrange("(k d) c -> d k c", d=P)).then_inc(w_in, 16)
                sp.dma_start(wupT[:, :], ins["w_upT"]).then_inc(k_in, 16)
                sp.dma_start(wdnT[:, :, :], ins["w_downT"].rearrange("(k f) c -> f k c", f=P)).then_inc(k_in, 16)

            @block.gpsimd
            def _(pool):
                nc.gpsimd.memset(ones_bf[:, :], 1.0).then_inc(pool_ok, 1)
                nc.gpsimd.memset(S[:, :, :], 0.0).then_inc(s_zero, 1)
                pool.wait_ge(k_in, 16 * 4)
                nc.gpsimd.tensor_copy(ident_bf[:, :], ident[:, :]).then_inc(pool_ok, 1)
                nc.gpsimd.tensor_copy(cmask[:, :, :], cmf[:, :, :]).then_inc(pool_ok, 1)

            @block.vector
            def _(dve):
                step = Chain(dve, dve_step)
                nc.vector.memset(eps[:, :], 1e-5).then_inc(eps_ok, 1)
                for c in range(CH):
                    t = slice(c * CT, (c + 1) * CT)
                    dve.wait_ge(x_in[c], 16)
                    norm_stats(dve, nc, step, X, XC, sq, mean, var, c)
                    nc.vector.tensor_scalar(var[:, t], var[:, t], 1.0 / DIM, None, ALU.mult).then_inc(var_ok, 1)
                    dve.wait_ge(rstd_ok, c + 1)
                    step(nc.vector.reciprocal(rstd[:, t], rstd[:, t]))
                    step(nc.vector.tensor_tensor(XC[:, t, :], XC[:, t, :], bc_last(rstd[:, t], DIM), ALU.mult))
                    step(nc.vector.tensor_tensor(sq[:, :, :], XC[:, t, :], XC[:, t, :], ALU.mult))
                    nc.vector.tensor_reduce(l2[:, t], sq[:, :, :], AX.X, ALU.add).then_inc(l2_in, 1)
                    dve.wait_ge(l2_ok, c + 1)
                    step(nc.vector.tensor_scalar(za[:, t], l2[:, t], 1e-12, DIM ** -0.5, ALU.max, ALU.mult))
                    step(nc.vector.tensor_scalar(ub[:, t], l2[:, t], DIM ** -0.5, 1e-8, ALU.mult, ALU.add))
                    step(nc.vector.reciprocal(za[:, t], za[:, t]))
                    step(nc.vector.reciprocal(ub[:, t], ub[:, t]))
                    if c == 0:
                        dve.wait_ge(g_in, 16)
                    if c >= 2:
                        dve.wait_ge(tp_ok, 4 * (c - 1))
                    step(nc.vector.tensor_tensor(Z[:, c % 2], XC[:, t, :], bc_last(za[:, t], DIM), ALU.mult))
                    step(nc.vector.tensor_tensor(Z[:, c % 2], Z[:, c % 2], bc_mid(gamma[:, :], CT), ALU.mult))
                    nc.vector.tensor_tensor(U[:, c % 2], XC[:, t, :], bc_last(ub[:, t], DIM),
                                            ALU.mult).then_inc(zu_ok, 1)
                    dve.wait_ge(zu_ok, c + 1)
                    for i in range(4):
                        n = 4 * c + i
                        lo, hi = (ZL, ZH) if i < 2 else (UL, UH)
                        o = c * CT * P + (i % 2) * 512
                        dve.wait_ge(tp_hi, n + 1)
                        nc.vector.tensor_tensor(lo[:, o:o + 512], tp[i][:, :], hi[:, o:o + 512],
                                                ALU.subtract).then_inc(tp_lo, 1)
                for n in range(4):
                    lo, hi = (ML, MH) if n < 2 else (NL, NH)
                    h = 4 * (n % 2)
                    dve.wait_ge(wp_hi, n + 1)
                    nc.vector.scalar_tensor_tensor(out=flat(lo[:, h:h + 4, :]), in0=wp[n % 2][:, :],
                                                   scalar=QK_SCALE, in1=flat(hi[:, h:h + 4, :]),
                                                   op0=ALU.mult, op1=ALU.subtract).then_inc(wp_lo, 1)

            @block.scalar
            def _(act):
                act.dma_start(ident[:, :], ins["identity"]).then_inc(k_in, 16)
                act.dma_start(cmf[:, :, :], ins["causal"].rearrange("k p c -> p k c")).then_inc(k_in, 16)
                act.dma_start(gamma[:, :], ins["gamma"].partition_broadcast(P)).then_inc(g_in, 16)
                act.wait_ge(eps_ok, 1)
                for c in range(CH):
                    t = slice(c * CT, (c + 1) * CT)
                    act.wait_ge(var_ok, c + 1)
                    nc.scalar.activation(rstd[:, t], var[:, t], ACT.Sqrt, bias=eps[:, 0:1]).then_inc(rstd_ok, 1)
                    act.wait_ge(l2_in, c + 1)
                    nc.scalar.activation(l2[:, t], l2[:, t], ACT.Sqrt).then_inc(l2_ok, 1)
                    for i in range(4):
                        n = 4 * c + i
                        hi = ZH if i < 2 else UH
                        o = c * CT * P + (i % 2) * 512
                        act.wait_ge(tp_ok, n + 1)
                        nc.scalar.copy(hi[:, o:o + 512], tp[i][:, :]).then_inc(tp_hi, 1)
                for n in range(4):
                    hi = MH if n < 2 else NH
                    h = 4 * (n % 2)
                    act.wait_ge(wp_ok, n + 1)
                    nc.scalar.mul(flat(hi[:, h:h + 4, :]), wp[n % 2][:, :], QK_SCALE).then_inc(wp_hi, 1)

            @block.tensor
            def _(pe):
                pe.wait_ge(k_in, 64)
                for c in range(CH):
                    pe.wait_ge(zu_ok, c + 1)
                    for i in range(4):
                        if c >= 1:
                            pe.wait_ge(tp_lo, 4 * (c - 1) + i + 1)
                        src = Z if i < 2 else U
                        for k in range(4):
                            mm = nc.tensor.transpose(tp[i][:, k * P:(k + 1) * P],
                                                     src[:, c % 2, 4 * (i % 2) + k, :], ident[:, :])
                        mm.then_inc(tp_ok, 1)
                pe.wait_ge(w_in, 32)
                for n in range(4):
                    if n >= 2:
                        pe.wait_ge(wp_lo, n - 1)
                    for k in range(4):
                        h = 4 * (n % 2) + k
                        a, b = (wqkv[:, h, :], wqkv[:, H0 + h, :]) if n < 2 else (wqkv[:, 2 * H0 + h, :], woT[:, h, :])
                        mm = nc.tensor.matmul(wp[n % 2][:, k * P:(k + 1) * P], a, b, start=True, stop=True)
                    mm.then_inc(wp_ok, 1)


def l0_attention(nc, sb, pb, sem, S, ident_bf, ones_bf, ZH, ZL, MH, ML, NH, NL, cmask):
    with ExitStack() as st:
        zbH = sb("zbH", [P, SEQ], F16, st)
        zbL = sb("zbL", [P, SEQ], F16, st)
        qH = sb("qH", [P, 2, SEQ], F16, st)
        qL = sb("qL", [P, 2, SEQ], F16, st)
        V = sb("V0", [P, LT, H0, P + 1], F32, st)
        mx = sb("mx0", [P, 2, LT], F32, st)
        dmx = sb("dmx0", [P, 2, LT, P], BF16, st)
        PT = sb("PT0", [P, 2, LT, SEQ], F32, st)
        rz = sb("rz0", [P, LT], F32, st)
        Sb = sb("Sb", [P, LT, P], F32, st)
        QP = pb("QP", [P, 512], F32, st)
        AX_ = [pb(f"AXP{i}", [P, 512], F32, st) for i in range(2)]
        ST = [pb(f"STP{i}", [P, 512], F32, st) for i in range(3)]
        OPB = [pb(f"OP{i}", [P, 512], F32, st) for i in range(2)]
        OP = [o[:, 0:2 * (P + 1)].rearrange("p (t c) -> p t c", t=2) for o in OPB]
        VPS = [ST[i][:, :].rearrange("p (h c) -> p h c", h=4) for i in range(2)]
        z_ready, z_used = sem("z_ready"), sem("z_used")
        v_ready, v_even, v_odd = sem("v_ready"), sem("v_even"), sem("v_odd")
        ones_col = sem("ones_col")
        q_ready, q_hi, q_lo = sem("q_ready"), sem("q_hi"), sem("q_lo")
        aux_ready, aux_max = sem("aux_ready"), sem("aux_max")
        dmx_ready = sem("dmx_ready")
        st_ready, p_ready = sem("st_ready"), sem("p_ready")
        o_ready, o_used, rz_ready = sem("o_ready"), sem("o_used"), sem("rz_ready")
        acc_step, acc_zero, s_kept = sem("acc_step"), sem("acc_zero"), sem("s_kept")
        NV = 2 * LT

        with nc.Block() as block:
            @block.gpsimd
            def _(pool):
                nc.gpsimd.memset(V[:, :, :, P:P + 1], 1.0).then_inc(ones_col, 1)
                with pool.Fori(0, BATCH) as b:
                    pool.wait_ge(z_used, b)
                    nc.gpsimd.tensor_copy(zbH[:, :], ZH[:, bass.ds(b * SEQ, SEQ)]).then_inc(z_ready, 1)
                    nc.gpsimd.tensor_copy(zbL[:, :], ZL[:, bass.ds(b * SEQ, SEQ)]).then_inc(z_ready, 1)
                    for h in range(H0):
                        pool.wait_ge(aux_max, (b * H0 + h + 1) * LT)
                        nc.gpsimd.tensor_tensor(dmx[:, h % 2, :, :], bc_mid(ident_bf[:, :], LT),
                                                bc_last(mx[:, h % 2, :], P), ALU.mult).then_inc(dmx_ready, 1)
                    pool.wait_ge(acc_step, (b + 1) * H0 * LT)
                    nc.gpsimd.tensor_copy(S[:, bass.ds(b * LT, LT), :], Sb[:, :, :]).then_inc(s_kept, 1)

            @block.scalar
            def _(act):
                with act.Fori(0, BATCH) as b:
                    for n in range(0, NV, 2):
                        act.wait_ge(v_ready, b * NV + n + 1)
                        nc.scalar.copy(V[:, n // 2, 0:4, 0:P], VPS[n % 2]).then_inc(v_even, 1)
                    for h in range(H0 + 1):
                        if h < H0:
                            act.wait_ge(q_ready, b * H0 + h + 1)
                            nc.scalar.copy(qH[:, h % 2, :], QP[:, :]).then_inc(q_hi, 1)
                        if h >= 1:
                            g = h - 1
                            for r in range(LT):
                                act.wait_ge(st_ready, (b * H0 + g) * LT + r + 1)
                                nc.scalar.activation(PT[:, g % 2, r, r * P:SEQ], ST[(g * LT + r) % 3][:, r * P:SEQ],
                                                     ACT.Exp, scale=1.0 / QK_SCALE * SM0).then_inc(p_ready, 1)

            @block.vector
            def _(dve):
                with dve.Fori(0, BATCH) as b:
                    for n in range(1, NV, 2):
                        dve.wait_ge(v_ready, b * NV + n + 1)
                        nc.vector.tensor_copy(V[:, n // 2, 4:8, 0:P], VPS[n % 2]).then_inc(v_odd, 1)
                    for h in range(H0 + 2):
                        if h < H0:
                            dve.wait_ge(q_hi, b * H0 + h + 1)
                            nc.vector.tensor_tensor(qL[:, h % 2, :], QP[:, :], qH[:, h % 2, :],
                                                    ALU.subtract).then_inc(q_lo, 1)
                            for t in range(LT):
                                dve.wait_ge(aux_ready, (b * H0 + h) * LT + t + 1)
                                if t == 0:
                                    if h >= 2:
                                        dve.wait_ge(dmx_ready, b * H0 + h - 1)
                                    else:
                                        dve.wait_ge(dmx_ready, b * H0)
                                i = nc.vector.tensor_reduce(mx[:, h % 2, t:t + 1], AX_[t % 2][:, 0:(t + 1) * P],
                                                            AX.X, ALU.max, negate=True)
                                i.then_inc(aux_max, 1)
                        if h == 0:
                            dve.wait_ge(s_kept, b)
                            nc.vector.memset(Sb[:, :, :], 0.0).then_inc(acc_zero, 1)
                            dve.wait_ge(acc_zero, b + 1)
                        if h >= 2:
                            g = h - 2
                            for k in range(2):
                                dve.wait_ge(o_ready, (b * H0 + g) * 2 + k + 1)
                                if g >= 1:
                                    dve.wait_ge(acc_step, (b * H0 + g) * LT)
                                nc.vector.tensor_scalar(rz[:, 2 * k:2 * k + 2], OP[k][:, :, P], QK_SCALE, None,
                                                        ALU.mult).then_inc(rz_ready, 1)
                                dve.wait_ge(rz_ready, ((b * H0 + g) * 2 + k) * 2 + 1)
                                nc.vector.reciprocal(rz[:, 2 * k:2 * k + 2], rz[:, 2 * k:2 * k + 2]).then_inc(rz_ready, 1)
                                dve.wait_ge(rz_ready, ((b * H0 + g) * 2 + k) * 2 + 2)
                                for t in range(2 * k, 2 * k + 2):
                                    i = nc.vector.scalar_tensor_tensor(
                                        out=Sb[:, t, :], in0=OP[k][:, t - 2 * k, 0:P], scalar=rz[:, t:t + 1],
                                        in1=Sb[:, t, :], op0=ALU.mult, op1=ALU.add)
                                    i.then_inc(acc_step, 1)

            @block.tensor
            def _(pe):
                pe.wait_ge(ones_col, 1)
                with pe.Fori(0, BATCH) as b:
                    pe.wait_ge(z_ready, 2 * b + 2)
                    for n in range(NV):
                        if n >= 2:
                            pe.wait_ge(v_odd if n % 2 else v_even, b * LT + n // 2)
                        r, h = n // 2, 4 * (n % 2)
                        for j, (a, w) in enumerate(((zbH, NH), (zbH, NL), (zbL, NH))):
                            mm = nc.tensor.matmul(ST[n % 2][:, :], a[:, r * P:(r + 1) * P], flat(w[:, h:h + 4, :]),
                                                  start=(j == 0), stop=(j == 2))
                        mm.then_inc(v_ready, 1)

                    def query(h):
                        for j, (a, w) in enumerate(((MH, zbH), (MH, zbL), (ML, zbH))):
                            mm = nc.tensor.matmul(QP[:, :], a[:, h, :], w[:, :], start=(j == 0), stop=(j == 2))
                        mm.then_inc(q_ready, 1)

                    def aux(h):
                        pe.wait_ge(q_hi, b * H0 + h + 1)
                        for t in range(LT):
                            if t >= 2 or h >= 1:
                                pe.wait_ge(aux_max, (b * H0 + h) * LT + t - 1)
                            nc.tensor.matmul(AX_[t % 2][:, 0:(t + 1) * P], qH[:, h % 2, t * P:(t + 1) * P],
                                             zbH[:, 0:(t + 1) * P], start=True, stop=False)
                            nc.tensor.matmul(AX_[t % 2][:, t * P:(t + 1) * P], ident_bf[:, :], cmask[:, 0, :],
                                             start=False, stop=True).then_inc(aux_ready, 1)

                    def scores(h):
                        pe.wait_ge(q_lo, b * H0 + h + 1)
                        pe.wait_ge(dmx_ready, b * H0 + h + 1)
                        if h == 0:
                            pe.wait_ge(v_even, (b + 1) * LT)
                            pe.wait_ge(v_odd, (b + 1) * LT)
                        for r in range(LT):
                            o = slice(r * P, SEQ)
                            k = (h * LT + r) % 3
                            if h * LT + r >= 3:
                                pe.wait_ge(p_ready, (b * H0 + h) * LT + r - 2)
                            bank = ST[k]
                            nc.tensor.matmul(bank[:, o], zbH[:, r * P:(r + 1) * P], qH[:, h % 2, o],
                                             start=True, stop=False)
                            nc.tensor.matmul(bank[:, o], zbL[:, r * P:(r + 1) * P], qH[:, h % 2, o],
                                             start=False, stop=False)
                            nc.tensor.matmul(bank[:, o], zbH[:, r * P:(r + 1) * P], qL[:, h % 2, o],
                                             start=False, stop=False)
                            nc.tensor.matmul(bank[:, r * P:(r + 1) * P], ident_bf[:, :], cmask[:, 1, :],
                                             start=False, stop=False)
                            mm = nc.tensor.matmul(bank[:, o], ones_bf[:, :], flat(dmx[:, h % 2, r:LT, :]),
                                                  start=False, stop=True)
                            mm.then_inc(st_ready, 1)

                    def values(h):
                        pe.wait_ge(p_ready, (b * H0 + h + 1) * LT)
                        if h >= 1:
                            pe.wait_ge(acc_step, (b * H0 + h) * LT)
                        for t in range(LT):
                            for r in range(t + 1):
                                mm = nc.tensor.matmul(OP[t // 2][:, t % 2, :], PT[:, h % 2, r, t * P:(t + 1) * P],
                                                      V[:, r, h, :], start=(r == 0), stop=(r == t))
                            if t % 2:
                                mm.then_inc(o_ready, 1)

                    query(0)
                    aux(0)
                    for h in range(H0):
                        if h + 1 < H0:
                            pe.wait_ge(q_lo, b * H0 + h + 1)
                            query(h + 1)
                            aux(h + 1)
                        scores(h)
                        if h >= 1:
                            values(h - 1)
                    values(H0 - 1)
                    nc.tensor.matmul(QP[:, 0:1], ident_bf[:, :], ident_bf[:, 0:1], start=True, stop=True)\
                        .then_inc(z_used, 1)


def l0_ffn(nc, sb, pb, sem, X, S, UH, UL, wupT, wdnT):
    with ExitStack() as st:
        tu = sb("tu", [P, FF], F16, st)
        td = sb("td", [P, FT, P], F32, st)
        ta = sb("ta", [P, FF], F32, st)
        tb = sb("tb", [P, FF], F32, st)
        ones_f = sb("ones_f", [P, P], F32, st)
        rs = sb("rs", [P, 2], F32, st)
        thr = sb("thr", [P, 2], F32, st)
        nthr = sb("nthr", [P, 2], F32, st)
        Hb = sb("Hb", [P, 2, FT, 512], F32, st)
        H2 = sb("H2", [P, 2, FT, 512], F32, st)
        Y = sb("Y", [P, TILES, P], F32, st)
        ss = sb("ss", [P, TILES], F32, st)
        rr = sb("rr", [P, TILES], F32, st)
        UP = [pb(f"UP{i}", [P, 512], F32, st) for i in range(3)]
        DP = [pb(f"DP{i}", [P, 512], F32, st) for i in range(2)]
        QP = [pb(f"QQ{i}", [P, 512], F32, st) for i in range(2)]
        TP = pb("TPs", [P, 512], F32, st)
        w_step, wsum_ok, tot_ok, tern_ok = sem("w_step"), sem("wsum_ok"), sem("tot_ok"), sem("tern_ok")
        onef_ok = sem("onef_ok")
        up_ok, gelu_ok, sq_ok = sem("up_ok"), sem("gelu_ok"), sem("sq_ok")
        dn_ok, y_ok = sem("dn_ok"), sem("y_ok")
        rms_in, rms_ok, pre_ok, silu_ok, res_step = (sem(n) for n in ("rms_in", "rms_ok", "pre_ok", "silu_ok", "res_step"))
        NCK = TOK // 512

        with nc.Block() as block:
            @block.gpsimd
            def _(pool):
                nc.gpsimd.memset(ones_f[:, :], 1.0).then_inc(onef_ok, 1)

            @block.tensor
            def _(pe):
                pe.wait_ge(onef_ok, 1)
                pe.wait_ge(wsum_ok, 2)
                nc.tensor.matmul(TP[:, 0:2], ones_f[:, :], rs[:, :], start=True, stop=True).then_inc(tot_ok, 1)
                pe.wait_ge(tern_ok, 2)

                def up(c):
                    for f in range(FT):
                        n = c * FT + f
                        if n >= 3:
                            pe.wait_ge(gelu_ok, n - 2)
                        nc.tensor.matmul(UP[n % 3][:, :], tu[:, f * P:(f + 1) * P], UH[:, c * 512:(c + 1) * 512],
                                         start=True, stop=False)
                        nc.tensor.matmul(UP[n % 3][:, :], tu[:, f * P:(f + 1) * P], UL[:, c * 512:(c + 1) * 512],
                                         start=False, stop=True).then_inc(up_ok, 1)

                def down(c):
                    pe.wait_ge(sq_ok, (c + 1) * FT)
                    if c >= 2:
                        pe.wait_ge(y_ok, 2 * (c - 1))
                    for k in range(4):
                        for f in range(FT):
                            nc.tensor.matmul(DP[c % 2][:, k * P:(k + 1) * P], Hb[:, c % 2, f, k * P:(k + 1) * P],
                                             td[:, f, :], start=(f == 0), stop=(f == FT - 1))
                    for k in range(4):
                        for f in range(FT):
                            mm = nc.tensor.matmul(QP[c % 2][:, k:k + 1], H2[:, c % 2, f, k * P:(k + 1) * P],
                                                  ones_f[:, 0:1], start=(f == 0), stop=(f == FT - 1))
                    mm.then_inc(dn_ok, 1)

                for c in range(NCK + 1):
                    if c < NCK:
                        up(c)
                    if c >= 1:
                        down(c - 1)

            @block.scalar
            def _(act):
                for c in range(NCK):
                    for f in range(FT):
                        n = c * FT + f
                        act.wait_ge(up_ok, n + 1)
                        if c >= 2:
                            act.wait_ge(dn_ok, c - 1)
                        nc.scalar.activation(Hb[:, c % 2, f, :], UP[n % 3][:, :], ACT.Gelu).then_inc(gelu_ok, 1)
                act.wait_ge(rms_in, 1)
                nc.scalar.activation(rr[:, :], ss[:, :], ACT.Sqrt).then_inc(rms_ok, 1)
                for c in range(CH):
                    t = slice(c * CT, (c + 1) * CT)
                    act.wait_ge(pre_ok, c + 1)
                    nc.scalar.activation(Y[:, t, :], Y[:, t, :], ACT.Silu).then_inc(silu_ok, 1)

            @block.vector
            def _(dve):
                step = Chain(dve, w_step)
                wd = wdnT[:, :, :].rearrange("p f c -> p (f c)")
                nc.vector.tensor_reduce(rs[:, 0:1], wupT[:, :], AX.X, ALU.add, apply_absolute_value=True).then_inc(wsum_ok, 1)
                nc.vector.tensor_reduce(rs[:, 1:2], wd, AX.X, ALU.add, apply_absolute_value=True).then_inc(wsum_ok, 1)
                dve.wait_ge(tot_ok, 1)
                step(nc.vector.tensor_scalar(thr[:, :], TP[:, 0:2], 0.5 / (FF * DIM), None, ALU.mult))
                step(nc.vector.tensor_scalar(nthr[:, :], thr[:, :], -1.0, None, ALU.mult))
                for k, (w, d) in enumerate(((wupT[:, :], tu[:, :]), (wd, td[:, :, :].rearrange("p f c -> p (f c)")))):
                    step(nc.vector.tensor_scalar(ta[:, :], w, thr[:, k:k + 1], None, ALU.is_gt))
                    step(nc.vector.tensor_scalar(tb[:, :], w, nthr[:, k:k + 1], None, ALU.is_lt))
                    nc.vector.tensor_tensor(d, ta[:, :], tb[:, :], ALU.subtract).then_inc(tern_ok, 1)
                    dve.wait_ge(tern_ok, k + 1)

                def keep(c):
                    dve.wait_ge(dn_ok, c + 1)
                    nc.vector.tensor_copy(Y[:, 4 * c:4 * c + 4, :], DP[c % 2][:, :].rearrange("p (t c) -> p t c", t=4))\
                        .then_inc(y_ok, 1)
                    nc.vector.tensor_copy(ss[:, 4 * c:4 * c + 4], QP[c % 2][:, 0:4]).then_inc(y_ok, 1)

                for c in range(NCK):
                    for f in range(FT):
                        dve.wait_ge(gelu_ok, c * FT + f + 1)
                        if c >= 2:
                            dve.wait_ge(dn_ok, c - 1)
                        nc.vector.tensor_tensor(H2[:, c % 2, f, :], Hb[:, c % 2, f, :], Hb[:, c % 2, f, :],
                                                ALU.mult).then_inc(sq_ok, 1)
                    if c >= 1:
                        keep(c - 1)
                keep(NCK - 1)
                dve.wait_ge(y_ok, 2 * NCK)
                nc.vector.tensor_scalar(ss[:, :], ss[:, :], 1.0 / FF, None, ALU.mult).then_inc(rms_in, 1)
                dve.wait_ge(rms_ok, 1)
                step(nc.vector.tensor_scalar(rr[:, :], rr[:, :], 1e-8, None, ALU.add))
                step(nc.vector.reciprocal(rr[:, :], rr[:, :]))
                for c in range(CH):
                    t = slice(c * CT, (c + 1) * CT)
                    nc.vector.tensor_tensor(Y[:, t, :], Y[:, t, :], bc_last(rr[:, t], P), ALU.mult).then_inc(pre_ok, 1)
                for c in range(CH):
                    t = slice(c * CT, (c + 1) * CT)
                    dve.wait_ge(silu_ok, c + 1)
                    step(nc.vector.tensor_tensor(Y[:, t, :], Y[:, t, :], S[:, t, :], ALU.mult))
                    step(nc.vector.tensor_tensor(X[:, t, :], X[:, t, :], Y[:, t, :], ALU.add))


def layer1(nc, sb, pb, sem, ins, out, X, S, ident, ident_bf, ones_bf, dram):
    with ExitStack() as st:
        XN = sb("XN", [P, TILES, DIM], F32, st)
        XH = sb("XH", [P, TOK], F16, st)
        XL = sb("XL", [P, TOK], F16, st)
        toep = [sb(n, [P, TW], F16, st) for n in ("fwd_hi", "fwd_lo", "bwd_hi", "bwd_lo")]
        l1_prepare(nc, sb, pb, sem, ins, X, XN, XH, XL, toep, ident, dram)
        l1_attention(nc, sb, pb, sem, ins, S, toep, ident_bf, ones_bf, dram)
        l1_project(nc, sb, pb, sem, ins, XN, S, ident, dram)
        l1_experts(nc, sb, pb, sem, ins, out, X, XH, XL, S, ident)


def l1_prepare(nc, sb, pb, sem, ins, X, XN, XH, XL, toep, ident, dram):
    q_d, k_d, v_d, rb_d, ctx_d = dram
    with ExitStack() as st:
        sq = sb("sq1", [P, CT, DIM], F32, st)
        mean = sb("mean1", [P, TILES], F32, st)
        var = sb("var1", [P, TILES], F32, st)
        rstd = sb("rstd1", [P, TILES], F32, st)
        eps = sb("eps1", [P, 1], F32, st)
        w3 = sb("w3", [P, 3, P], F32, st)
        wh = sb("w3h", [P, 3, P], F16, st)
        wl = sb("w3l", [P, 3, P], F16, st)
        bqk = sb("bqk", [P, 2], F32, st)
        bvr = sb("bvr", [P, P], F32, st)
        tf = sb("tf", [P, 2, TW], F32, st)
        dT = sb("dT", [P, NDIST], F32, st)
        dmax = sb("dmax", [P, 1], F32, st)
        headm = sb("headm", [P, H1], F32, st)
        bound = sb("bound", [P, H1], F16, st)
        qf = sb("qf", [P, 2, 512], F32, st)
        qa = sb("qa", [P, 2, 512], F16, st)
        hs = sb("hs", [P, 4, 2, 512], F16, st)
        vf = sb("vf", [P, 2, 4, H1, D1], F32, st)
        vo = sb("vo", [P, 2, 4, H1, DV], F16, st)
        rb = sb("rb", [P, TILES, H1], F32, st)
        TPp = [pb(f"tq{i}", [P, 512], F32, st) for i in range(2)]
        PR = [pb(f"pr{i}", [P, 512], F32, st) for i in range(2)]
        VP = [pb(f"vp{i}", [P, 512], F32, st) for i in range(2)]
        RP = pb("rp", [P, 512], F32, st)
        w_in, t_in, d_in = sem("w1_in"), sem("t_in"), sem("d_in")
        step_s, var_ok, std_ok = sem("p1_step"), sem("var1_ok"), sem("std1_ok")
        eps_ok, wh_ok, wl_ok = sem("eps1_ok"), sem("w3h_ok"), sem("w3l_ok")
        xn_ok, tp_ok, xh_ok, xl_ok = sem("xn_ok"), sem("tq_ok"), sem("xh_ok"), sem("xl_ok")
        pr_ok, qf_ok, hi_ok, lo_ok = (sem(n) for n in ("pr_ok", "qf_ok", "hi_ok", "lo_ok"))
        qk_out = [sem(f"qk_out{i}") for i in range(4)]
        abs_ok, rp_ok, rb_ok, rb_out = (sem(n) for n in ("abs_ok", "rp_ok", "rb_ok", "rb_out"))
        vp_ok, vf_ok, vh_ok, vo_ok, vones = (sem(n) for n in ("vp_ok", "vf_ok", "vh_ok", "vo_ok", "vones"))
        v_out = [sem("v_out0"), sem("v_out1")]
        tab_ok, bound_ok = sem("tab_ok"), sem("bound_ok")
        NCK = TOK // 512

        with nc.Block() as block:
            @block.sync
            def _(sp):
                for k, n in enumerate(("wq", "wk", "wv")):
                    sp.dma_start(w3[:, k, :], ins[n]).then_inc(w_in, 16)
                sp.dma_start(bqk[:, 0:1], ins["bq"].unsqueeze(1)).then_inc(w_in, 16)
                sp.dma_start(bqk[:, 1:2], ins["bk"].unsqueeze(1)).then_inc(w_in, 16)
                sp.dma_start(bvr[:, :], ins["bv"].partition_broadcast(P)).then_inc(w_in, 16)
                sp.dma_start(headm[:, :], ins["head"]).then_inc(w_in, 16)
                for s in range(2):
                    for k, n in enumerate(("toep_f", "toep_b")):
                        sp.dma_start(tf[64 * s:64 * s + 64, k, :], ins[n]).then_inc(t_in, 16)
                for h in range(H1):
                    sp.dma_start(dT[h * D1:(h + 1) * D1, :], ins["distT"]).then_inc(d_in, 16)
                for c in range(NCK):
                    for k, (d, order) in enumerate(((q_d, Q_STACK), (k_d, K_STACK))):
                        n = 2 * c + k
                        sp.wait_ge(lo_ok, n + 1)
                        for i, half in enumerate(order):
                            sp.dma_start(d[:, i, :, c * 512:(c + 1) * 512], hs[:, n % 4, half, :])\
                              .then_inc(qk_out[n % 4], 16)
                    sp.wait_ge(vo_ok, c + 1)
                    sp.dma_start(v_d[c * 512:(c + 1) * 512, :].rearrange("(t p) n -> p t n", p=P),
                                 vo[:, c % 2].rearrange("p t h e -> p t (h e)")).then_inc(v_out[c % 2], 16)
                sp.wait_ge(rb_ok, NCK)
                sp.dma_start(rb_d.rearrange("(t p) h -> p t h", p=P), rb[:, :, :]).then_inc(rb_out, 16)
                for k in range(4):
                    sp.wait_ge(qk_out[k], 16 * 4 * NCK // 2)
                for k in range(2):
                    sp.wait_ge(v_out[k], 8 * NCK)
                sp.wait_ge(rb_out, 16)

            @block.gpsimd
            def _(pool):
                nc.gpsimd.memset(vo[:, :, :, :, D1:DE], 1.0).then_inc(vones, 1)

            @block.scalar
            def _(act):
                act.wait_ge(w_in, 16 * 7)
                nc.scalar.copy(wh[:, :, :], w3[:, :, :]).then_inc(wh_ok, 1)
                act.wait_ge(t_in, 64)
                for k in range(2):
                    nc.scalar.copy(toep[2 * k][:, :], tf[:, k, :]).then_inc(tab_ok, 1)
                act.wait_ge(eps_ok, 1)
                for c in range(CH):
                    t = slice(c * CT, (c + 1) * CT)
                    act.wait_ge(var_ok, c + 1)
                    nc.scalar.activation(rstd[:, t], var[:, t], ACT.Sqrt, bias=eps[:, 0:1]).then_inc(std_ok, 1)
                    for i in range(2):
                        n = 2 * c + i
                        act.wait_ge(tp_ok, n + 1)
                        nc.scalar.copy(XH[:, n * 512:(n + 1) * 512], TPp[n % 2][:, :]).then_inc(xh_ok, 1)
                for n in range(2 * NCK):
                    act.wait_ge(pr_ok, n + 1)
                    if n >= 2:
                        act.wait_ge(lo_ok, n - 1)
                    if n % 2 == 0 and n >= 2:
                        act.wait_ge(abs_ok, n // 2)
                    nc.scalar.activation(qf[:, n % 2, :], PR[n % 2][:, :], ACT.Identity,
                                         bias=bqk[:, n % 2:n % 2 + 1]).then_inc(qf_ok, 1)
                    act.wait_ge(qf_ok, n + 1)
                    if n >= 4:
                        act.wait_ge(qk_out[n % 4], 64 * (n // 4))
                    nc.scalar.copy(hs[:, n % 4, 0, :], qf[:, n % 2, :]).then_inc(hi_ok, 1)
                    if n % 2 == 0:
                        if n >= 4:
                            act.wait_ge(rp_ok, n // 2 - 1)
                        nc.scalar.activation(qa[:, (n // 2) % 2, :], qf[:, 0, :], ACT.Abs).then_inc(abs_ok, 1)
                    else:
                        c = n // 2
                        act.wait_ge(vf_ok, c + 1)
                        if c == 0:
                            act.wait_ge(vones, 1)
                        if c >= 2:
                            act.wait_ge(v_out[c % 2], 16 * (c // 2))
                        nc.scalar.copy(vo[:, c % 2, :, :, 0:D1], vf[:, c % 2]).then_inc(vh_ok, 1)

            @block.vector
            def _(dve):
                step = Chain(dve, step_s)
                nc.vector.memset(eps[:, :], 1e-5).then_inc(eps_ok, 1)
                dve.wait_ge(wh_ok, 1)
                nc.vector.tensor_tensor(wl[:, :, :], w3[:, :, :], wh[:, :, :], ALU.subtract).then_inc(wl_ok, 1)

                def x_low(n):
                    dve.wait_ge(xh_ok, n + 1)
                    nc.vector.tensor_tensor(XL[:, n * 512:(n + 1) * 512], TPp[n % 2][:, :],
                                            XH[:, n * 512:(n + 1) * 512], ALU.subtract).then_inc(xl_ok, 1)

                for c in range(CH):
                    t = slice(c * CT, (c + 1) * CT)
                    norm_stats(dve, nc, step, X, XN, sq, mean, var, c)
                    nc.vector.tensor_scalar(var[:, t], var[:, t], 1.0 / DIM, None, ALU.mult).then_inc(var_ok, 1)
                    dve.wait_ge(std_ok, c + 1)
                    step(nc.vector.reciprocal(rstd[:, t], rstd[:, t]))
                    nc.vector.tensor_tensor(XN[:, t, :], XN[:, t, :], bc_last(rstd[:, t], DIM), ALU.mult).then_inc(xn_ok, 1)
                    if c >= 1:
                        x_low(2 * c - 2)
                        x_low(2 * c - 1)
                x_low(2 * CH - 2)
                x_low(2 * CH - 1)
                dve.wait_ge(tab_ok, 2)
                for k in range(2):
                    nc.vector.tensor_tensor(toep[2 * k + 1][:, :], tf[:, k, :], toep[2 * k][:, :], ALU.subtract)
                dve.wait_ge(d_in, 16 * H1)
                step(nc.vector.tensor_reduce(dmax[:, :], dT[:, :], AX.X, ALU.max, apply_absolute_value=True))
                dve.wait_ge(w_in, 16 * 7)
                nc.vector.tensor_scalar(bound[:, :], headm[:, :], dmax[:, 0:1], 1.01, ALU.mult, ALU.mult).then_inc(bound_ok, 1)
                bv = bvr[:, :].rearrange("p (h e) -> p h e", h=H1).unsqueeze(1).to_broadcast([P, 4, H1, D1])
                for c in range(NCK):
                    for k in range(2):
                        n = 2 * c + k
                        dve.wait_ge(hi_ok, n + 1)
                        nc.vector.tensor_tensor(hs[:, n % 4, 1, :], qf[:, n % 2, :], hs[:, n % 4, 0, :],
                                                ALU.subtract).then_inc(lo_ok, 1)
                        if k == 0:
                            dve.wait_ge(vp_ok, c + 1)
                            if c >= 2:
                                dve.wait_ge(vo_ok, c - 1)
                            nc.vector.tensor_tensor(vf[:, c % 2],
                                                    VP[c % 2][:, :].rearrange("p (t h e) -> p t h e", t=4, h=H1),
                                                    bv, ALU.add).then_inc(vf_ok, 1)
                    dve.wait_ge(vh_ok, c + 1)
                    nc.vector.tensor_tensor(vo[:, c % 2, :, :, DE:DV], vf[:, c % 2], vo[:, c % 2, :, :, 0:D1],
                                            ALU.subtract).then_inc(vo_ok, 1)
                    dve.wait_ge(rp_ok, c + 1)
                    nc.vector.tensor_copy(rb[:, 4 * c:4 * c + 4, :],
                                          RP[:, 0:4 * H1].rearrange("p (t h) -> p t h", t=4)).then_inc(rb_ok, 1)

            @block.tensor
            def _(pe):
                for n in range(NCK):
                    pe.wait_ge(xn_ok, n // 2 + 1)
                    if n >= 2:
                        pe.wait_ge(xl_ok, n - 1)
                    for k in range(4):
                        mm = nc.tensor.transpose(TPp[n % 2][:, k * P:(k + 1) * P], XN[:, 4 * n + k, :], ident[:, :])
                    mm.then_inc(tp_ok, 1)
                pe.wait_ge(wl_ok, 1)
                pe.wait_ge(xl_ok, NCK)
                pe.wait_ge(bound_ok, 1)
                for c in range(NCK):
                    x = slice(c * 512, (c + 1) * 512)
                    for k in range(2):
                        n = 2 * c + k
                        if n >= 2:
                            pe.wait_ge(qf_ok, n - 1)
                        nc.tensor.matmul(PR[n % 2][:, :], wh[:, k, :], XH[:, x], start=True, stop=False)
                        nc.tensor.matmul(PR[n % 2][:, :], wl[:, k, :], XH[:, x], start=False, stop=False)
                        nc.tensor.matmul(PR[n % 2][:, :], wh[:, k, :], XL[:, x], start=False, stop=True).then_inc(pr_ok, 1)
                    if c >= 2:
                        pe.wait_ge(vf_ok, c - 1)
                    for k in range(4):
                        o = slice(k * P, (k + 1) * P)
                        xs = slice(c * 512 + k * P, c * 512 + (k + 1) * P)
                        nc.tensor.matmul(VP[c % 2][:, o], XH[:, xs], wh[:, 2, :], start=True, stop=False)
                        nc.tensor.matmul(VP[c % 2][:, o], XH[:, xs], wl[:, 2, :], start=False, stop=False)
                        mm = nc.tensor.matmul(VP[c % 2][:, o], XL[:, xs], wh[:, 2, :], start=False, stop=True)
                    mm.then_inc(vp_ok, 1)
                    pe.wait_ge(abs_ok, c + 1)
                    if c >= 1:
                        pe.wait_ge(rb_ok, c)
                    for k in range(4):
                        mm = nc.tensor.matmul(RP[:, k * H1:(k + 1) * H1], qa[:, c % 2, k * P:(k + 1) * P], bound[:, :],
                                              start=True, stop=True)
                    mm.then_inc(rp_ok, 1)


def l1_attention(nc, sb, pb, sem, ins, S, toep, ident_bf, ones_bf, dram):
    fwd_hi, fwd_lo, bwd_hi, bwd_lo = toep
    q_d, k_d, v_d, rb_d, ctx_d = dram
    UPB = NHG * LT
    RC = SEQ // 64
    SC = 2 * LT
    NA, NB, NP32 = 4, 2, 4
    with ExitStack() as st:
        kbd = sb("kbd", [P, NHG, 2, 4, SEQ], F16, st)
        qst = sb("qst", [P, NHG, 2, SEQ], F16, st)
        kd = sb("kd", [P, NHG, HG, SEQ], F16, st)
        qd = sb("qd", [P, NHG, HG, SEQ], F16, st)
        rbb = sb("rbb", [P, NHG, LT, HG], F32, st)
        gm = sb("gm", [P, JG], F16, st)
        gmf = sb("gmf", [P, JG], F32, st)
        idh = sb("idh1", [P, P], F16, st)
        S1H = sb("S1H", [P, 2, HG, SEQ], F16, st)
        S1L = sb("S1L", [P, 2, HG, SEQ], F16, st)
        PF = sb("PF", [P, NP32, HG, 64], F32, st)
        PH = sb("PH", [P, 2, LT, HG, P], F16, st)
        PL = sb("PL", [P, 2, LT, HG, P], F16, st)
        dm = sb("dm", [P, 2, HG, P], BF16, st)
        mx = sb("mx1", [P, 2, HG], F32, st)
        rz = sb("rz1", [P, HG], F32, st)
        ol = sb("ol", [P, HG, D1], F32, st)
        spare = S[:, :, :].rearrange("p t c -> p (t c)")
        nv = NHG * LT * HG * DV // 2
        ncx = NHG * LT * HG * D1
        vb = spare[:, 0:nv].bitcast(F16).rearrange("p (g t n) -> p g t n", g=NHG, t=LT)
        cb = spare[:, nv:nv + ncx].rearrange("p (g t n) -> p g t n", g=NHG, t=LT)
        A = [pb(f"A{i}", [P, 512], F32, st) for i in range(NA)]
        B = [pb(f"B{i}", [P, 512], F32, st) for i in range(NB)]
        O = [pb(f"O{i}", [P, 512], F32, st) for i in range(2)]
        gm_in, gm_ok, bd_zero, idh_ok = sem("gm_in"), sem("gm_ok"), sem("bd_zero"), sem("idh1_ok")
        kd_in, qd_in, stack_in, side_in = ([sem(f"{n}{g}") for g in range(NHG)]
                                           for n in ("kd_in", "qd_in", "stack_in", "side_in"))
        kd_ok, qd_ok = [sem(f"kd_ok{g}") for g in range(NHG)], [sem(f"qd_ok{g}") for g in range(NHG)]
        a_ready, s1_hi, s1_lo = sem("a_ready"), sem("s1_hi"), sem("s1_lo")
        mx_step, dm_ok = sem("mx_step"), sem("dm_ok")
        b_ready, p_ready, pl_ok = sem("b_ready"), sem("p_ready1"), sem("pl_ok")
        o_ready, o_step, c_ready = sem("o_ready1"), sem("o_step"), sem("c_ready")
        c_out = [sem(f"c_out{g}") for g in range(NHG)]

        def v3(bank):
            return bank[:, :].rearrange("p (h c) -> p h c", h=HG)

        with nc.Block() as block:
            @block.sync
            def _(sp):
                sp.wait_ge(bd_zero, 1)

                def load(b):
                    for g in range(NHG):
                        last = (b - 1) * UPB + (g + 1) * LT
                        heads = slice(g * HG, (g + 1) * HG)
                        kb = k_d.rearrange("h s e (b t) -> b h (s e) t", b=BATCH)[b, heads]
                        qb = q_d.rearrange("h s e (b t) -> b h (s e) t", b=BATCH)[b, heads]
                        wait_for(sp, a_ready, last * RC)
                        for j in range(JG):
                            sp.dma_start(kd[j:P:JG, g], kb[:, 0:2 * D1, :].rearrange("h r t -> r h t"))\
                              .then_inc(kd_in[g], 16)
                        for h in range(HG):
                            sp.dma_start(kbd[32 * (h % 4):32 * (h % 4) + 32, g, h // 4, h % 4, :], kb[h])\
                              .then_inc(stack_in[g], 16)
                        for i in range(2):
                            sp.dma_start(qst[:, g, i, :], qb[4 * i:4 * i + 4].rearrange("h r t -> (h r) t"))\
                              .then_inc(stack_in[g], 16)
                        wait_for(sp, b_ready, last * SC)
                        for j in range(JG):
                            sp.dma_start(qd[j:P:JG, g], qb[:, 0:2 * D1, :].rearrange("h r t -> r h t"))\
                              .then_inc(qd_in[g], 16)
                        wait_for(sp, o_ready, last)
                        sp.dma_start(vb[:, g], v_d.rearrange("(b t p) (g n) -> b g p t n", p=P, t=LT, g=NHG)[b, g])\
                            .then_inc(side_in[g], 16)
                        sp.dma_start(rbb[:, g], rb_d.rearrange("(b t p) (g n) -> b g p t n", p=P, t=LT, g=NHG)[b, g])\
                            .then_inc(side_in[g], 16)

                load(0)
                with sp.Fori(1, BATCH) as b:
                    load(b)

            @block.gpsimd
            def _(pool):
                pool.dma_start(gmf[:, :], ins["group"]).then_inc(gm_in, 16)
                nc.gpsimd.memset(kbd[:, :, :, :, :], 0.0).then_inc(bd_zero, 1)
                nc.gpsimd.tensor_copy(idh[:, :], ident_bf[:, :]).then_inc(idh_ok, 1)
                pool.wait_ge(gm_in, 16)
                nc.gpsimd.tensor_copy(gm[:, :], gmf[:, :]).then_inc(gm_ok, 1)
                pool.wait_ge(gm_ok, 1)

                def spread(b, g, d, landed, done):
                    pool.wait_ge(landed[g], (b + 1) * 16 * JG)
                    v = d[:, g].rearrange("p h (a j) -> p (h a) j", j=JG)
                    nc.gpsimd.tensor_tensor(v, v, bc_mid(gm[:, :], HG * SEQ // JG), ALU.mult).then_inc(done[g], 1)

                def low(b, u):
                    for k in range(SC):
                        half, r = k // LT, k % LT
                        o = slice(half * 64, (half + 1) * 64)
                        pool.wait_ge(p_ready, (b * UPB + u) * SC + k + 1)
                        nc.gpsimd.tensor_tensor(PL[:, u % 2, r, :, o], PF[:, k % NP32], PH[:, u % 2, r, :, o],
                                                ALU.subtract).then_inc(pl_ok, 1)

                def store(b, g):
                    pool.wait_ge(c_ready, b * UPB + (g + 1) * LT)
                    pool.dma_start(ctx_d.rearrange("(b t p) (g n) -> b g p t n", p=P, t=LT, g=NHG)[b, g],
                                   cb[:, g]).then_inc(c_out[g], 16)

                def most(b, u0, u1):
                    for u in range(u0, u1):
                        if u == 2:
                            if u0 == 0 and not (isinstance(b, int) and b == 0):
                                store(b - 1, 1)
                            spread(b, 1, kd, kd_in, kd_ok)
                        if u == 3:
                            spread(b, 1, qd, qd_in, qd_ok)
                        if u == 6:
                            store(b, 0)
                        if u >= 1:
                            low(b, u - 1)
                        elif not (isinstance(b, int) and b == 0):
                            low(b - 1, UPB - 1)

                def turn(b):
                    store(b - 1, 0)
                    spread(b, 0, kd, kd_in, kd_ok)
                    low(b - 1, UPB - 3)
                    spread(b, 0, qd, qd_in, qd_ok)
                    low(b - 1, UPB - 2)

                spread(0, 0, kd, kd_in, kd_ok)
                spread(0, 0, qd, qd_in, qd_ok)
                most(0, 0, 6)
                with pool.Fori(1, BATCH) as b:
                    turn(b)
                    most(b, 0, 6)
                most(BATCH - 1, 6, UPB)
                low(BATCH - 1, UPB - 1)
                store(BATCH - 1, 1)
                for g in range(NHG):
                    pool.wait_ge(c_out[g], 16 * BATCH)

            @block.tensor
            def _(pe):
                pe.wait_ge(idh_ok, 1)

                def first(b, u):
                    g, t = u // LT, u % LT
                    if t == 0:
                        pe.wait_ge(stack_in[g], (b + 1) * 16 * (HG + 2))
                        pe.wait_ge(kd_ok[g], b + 1)
                    for c in range(RC):
                        n = u * RC + c
                        v = v3(A[n % NA])
                        wait_for(pe, s1_lo, b * (UPB * RC) + n + 1 - NA)
                        for i in range(2):
                            nc.tensor.matmul(v[:, 4 * i:4 * i + 4, :], qst[:, g, i, t * P:(t + 1) * P],
                                             kbd[:, g, i, :, c * 64:(c + 1) * 64],
                                             start=(i == 0), stop=False, skip_group_check=True)
                        for a in range(NG):
                            r = c * 64 + a * JG
                            y = t * P - r + TOFF
                            for tab in (fwd_hi, fwd_lo):
                                mm = nc.tensor.matmul(v[:, :, a * JG:(a + 1) * JG], tab[:, y:y + P],
                                                      kd[:, g, :, r:r + JG], start=False,
                                                      stop=(a == NG - 1 and tab is fwd_lo), skip_group_check=True)
                        mm.then_inc(a_ready, 1)

                def second(b, u):
                    g, t = u // LT, u % LT
                    if t == 0:
                        pe.wait_ge(qd_ok[g], b + 1)
                    pe.wait_ge(dm_ok, b * UPB + u + 1)
                    for k in range(SC):
                        n = u * SC + k
                        half, r = k // LT, k % LT
                        bank = B[n % NB]
                        v = v3(bank)
                        wait_for(pe, p_ready, b * (UPB * SC) + n + 1 - NB)
                        nc.tensor.matmul(bank[:, :], ones_bf[:, :], dm[:, u % 2, :, half * 64:(half + 1) * 64],
                                         start=True, stop=False, skip_group_check=True)
                        for a in range(NG):
                            l = t * P + half * 64 + a * JG
                            y = r * P - l + TOFF
                            for tab in (bwd_hi, bwd_lo):
                                nc.tensor.matmul(v[:, :, a * JG:(a + 1) * JG], tab[:, y:y + P],
                                                 qd[:, g, :, l:l + JG], start=False, stop=False,
                                                 skip_group_check=True)
                        for h in range(HG):
                            for part in (S1H, S1L):
                                mm = nc.tensor.matmul(v[:, h, :], part[:, u % 2, h, r * P:(r + 1) * P],
                                                      idh[:, half * 64:(half + 1) * 64], start=False,
                                                      stop=(h == HG - 1 and part is S1L), skip_group_check=True)
                        mm.then_inc(b_ready, 1)

                def values(b, u):
                    g, t = u // LT, u % LT
                    if t == 0:
                        pe.wait_ge(side_in[g], (b + 1) * 32)
                    pe.wait_ge(pl_ok, (b * UPB + u + 1) * SC)
                    wait_for(pe, c_ready, b * UPB + u - 1)
                    for h in range(HG):
                        for r in range(LT):
                            o, w = h * DV, vb[:, g, r, h * DV:(h + 1) * DV]
                            nc.tensor.matmul(O[u % 2][:, o:o + DV], PH[:, u % 2, r, h, :], w,
                                             start=(r == 0), stop=False, skip_group_check=True)
                            mm = nc.tensor.matmul(O[u % 2][:, o:o + DE], PL[:, u % 2, r, h, :], w[:, 0:DE],
                                                  start=False, stop=(r == LT - 1), skip_group_check=True)
                    mm.then_inc(o_ready, 1)

                def batch(b):
                    for u in range(UPB):
                        first(b, u)
                        if u >= 2:
                            values(b, u - 2)
                        elif not (isinstance(b, int) and b == 0):
                            values(b - 1, UPB + u - 2)
                        if u >= 1:
                            second(b, u - 1)
                        elif not (isinstance(b, int) and b == 0):
                            second(b - 1, UPB - 1)

                batch(0)
                with pe.Fori(1, BATCH) as b:
                    batch(b)
                values(BATCH - 1, UPB - 2)
                second(BATCH - 1, UPB - 1)
                values(BATCH - 1, UPB - 1)

            @block.scalar
            def _(act):
                def high(b, u):
                    for c in range(RC):
                        act.wait_ge(a_ready, (b * UPB + u) * RC + c + 1)
                        nc.scalar.copy(S1H[:, u % 2, :, c * 64:(c + 1) * 64], v3(A[(u * RC + c) % NA])).then_inc(s1_hi, 1)

                def exponentials(b, u):
                    for k in range(SC):
                        half, r = k // LT, k % LT
                        bank = v3(B[(u * SC + k) % NB])
                        act.wait_ge(b_ready, (b * UPB + u) * SC + k + 1)
                        nc.scalar.activation(PH[:, u % 2, r, :, half * 64:(half + 1) * 64], bank, ACT.Exp, scale=SM1)
                        wait_for(act, pl_ok, (b * UPB + u) * SC + k + 1 - NP32)
                        nc.scalar.activation(PF[:, k % NP32], bank, ACT.Exp, scale=SM1).then_inc(p_ready, 1)

                def batch(b):
                    for u in range(UPB):
                        high(b, u)
                        if u >= 1:
                            exponentials(b, u - 1)
                        elif not (isinstance(b, int) and b == 0):
                            exponentials(b - 1, UPB - 1)

                batch(0)
                with act.Fori(1, BATCH) as b:
                    batch(b)
                exponentials(BATCH - 1, UPB - 1)

            @block.vector
            def _(dve):
                def low(b, u):
                    for c in range(RC):
                        dve.wait_ge(s1_hi, (b * UPB + u) * RC + c + 1)
                        o = slice(c * 64, (c + 1) * 64)
                        nc.vector.tensor_tensor(S1L[:, u % 2, :, o], v3(A[(u * RC + c) % NA]), S1H[:, u % 2, :, o],
                                                ALU.subtract).then_inc(s1_lo, 1)

                def shift(b, u):
                    g, t = u // LT, u % LT
                    if t == 0:
                        dve.wait_ge(side_in[g], (b + 1) * 32)
                    nc.vector.tensor_reduce(mx[:, u % 2, :], S1H[:, u % 2, :, :], AX.X, ALU.max).then_inc(mx_step, 1)
                    dve.wait_ge(mx_step, (b * UPB + u) * 2 + 1)
                    nc.vector.scalar_tensor_tensor(out=mx[:, u % 2, :], in0=mx[:, u % 2, :], scalar=-1.0,
                                                   in1=rbb[:, g, t, :], op0=ALU.mult, op1=ALU.subtract).then_inc(mx_step, 1)
                    dve.wait_ge(mx_step, (b * UPB + u) * 2 + 2)
                    nc.vector.tensor_tensor(dm[:, u % 2, :, :], bc_mid(ident_bf[:, :], HG),
                                            bc_last(mx[:, u % 2, :], P), ALU.mult).then_inc(dm_ok, 1)

                def divide(b, u):
                    g, t = u // LT, u % LT
                    dve.wait_ge(o_ready, b * UPB + u + 1)
                    wait_for(dve, c_ready, b * UPB + u)
                    if t == 0:
                        wait_for(dve, c_out[g], b * 16)
                    o = O[u % 2][:, 0:HG * DV].rearrange("p (h e) -> p h e", h=HG)
                    c = cb[:, g, t, :].rearrange("p (h e) -> p h e", h=HG)
                    nc.vector.reciprocal(rz[:, :], o[:, :, D1]).then_inc(o_step, 1)
                    nc.vector.tensor_copy(ol[:, :, :], o[:, :, DE:DV]).then_inc(o_step, 1)
                    dve.wait_ge(o_step, (b * UPB + u) * 3 + 2)
                    nc.vector.tensor_tensor(ol[:, :, :], o[:, :, 0:D1], ol[:, :, :], ALU.add).then_inc(o_step, 1)
                    dve.wait_ge(o_step, (b * UPB + u) * 3 + 3)
                    nc.vector.tensor_tensor(c, ol[:, :, :], bc_last(rz[:, :], D1), ALU.mult).then_inc(c_ready, 1)

                def batch(b):
                    for u in range(UPB):
                        low(b, u)
                        shift(b, u)
                        if u >= 2:
                            divide(b, u - 2)
                        elif not (isinstance(b, int) and b == 0):
                            divide(b - 1, UPB + u - 2)

                batch(0)
                with dve.Fori(1, BATCH) as b:
                    batch(b)
                divide(BATCH - 1, UPB - 2)
                divide(BATCH - 1, UPB - 1)


def l1_project(nc, sb, pb, sem, ins, XN, S, ident, dram):
    ctx_d = dram[4]
    with ExitStack() as st:
        C = sb("C", [P, TILES, DIM], F32, st)
        CTt = sb("CTt", [P, 2, 512], F32, st)
        wo = sb("wo1", [P, P], F32, st)
        rows = sb("rows", [P, 3, P], F32, st)
        sq = sb("sq2", [P, CT, DIM], F32, st)
        mean = sb("mean2", [P, TILES], F32, st)
        var = sb("var2", [P, TILES], F32, st)
        rstd = sb("rstd2", [P, TILES], F32, st)
        eps = sb("eps2", [P, 1], F32, st)
        TPp = [pb(f"tc{i}", [P, 512], F32, st) for i in range(2)]
        PR = [pb(f"pc{i}", [P, 512], F32, st) for i in range(2)]
        c_in, w_in = [sem(f"ctx_in{c}") for c in range(CH)], sem("wo_in")
        step_s, var_ok, std_ok, eps_ok = sem("p2_step"), sem("var2_ok"), sem("std2_ok"), sem("eps2_ok")
        tp_ok, ct_ok, pr_ok, h_ok = sem("tc_ok"), sem("ct_ok"), sem("pc_ok"), sem("h_ok")
        NCK = TOK // 512
        with nc.Block() as block:
            @block.sync
            def _(sp):
                for c in range(CH):
                    t = slice(c * CT, (c + 1) * CT)
                    sp.dma_start(C[:, t, :], ctx_d.rearrange("(t p) n -> p t n", p=P)[:, t, :]).then_inc(c_in[c], 16)
                sp.dma_start(wo[:, :], ins["wo"]).then_inc(w_in, 16)
                for k, n in enumerate(("bo", "ln_g", "ln_b")):
                    sp.dma_start(rows[:, k, :], ins[n].partition_broadcast(P)).then_inc(w_in, 16)

            @block.tensor
            def _(pe):
                for n in range(NCK + 1):
                    if n < NCK:
                        pe.wait_ge(c_in[n // 2], 16)
                        if n >= 2:
                            pe.wait_ge(ct_ok, n - 1)
                        for k in range(4):
                            mm = nc.tensor.transpose(TPp[n % 2][:, k * P:(k + 1) * P], C[:, 4 * n + k, :], ident[:, :])
                        mm.then_inc(tp_ok, 1)
                    if n >= 1:
                        m = n - 1
                        if m == 0:
                            pe.wait_ge(w_in, 64)
                        pe.wait_ge(ct_ok, m + 1)
                        if m >= 2:
                            pe.wait_ge(h_ok, m - 1)
                        for k in range(4):
                            mm = nc.tensor.matmul(PR[m % 2][:, k * P:(k + 1) * P], CTt[:, m % 2, k * P:(k + 1) * P],
                                                  wo[:, :], start=True, stop=True)
                        mm.then_inc(pr_ok, 1)

            @block.scalar
            def _(act):
                for n in range(NCK):
                    act.wait_ge(tp_ok, n + 1)
                    if n >= 2:
                        act.wait_ge(pr_ok, n - 1)
                    nc.scalar.copy(CTt[:, n % 2, :], TPp[n % 2][:, :]).then_inc(ct_ok, 1)
                act.wait_ge(eps_ok, 1)
                for c in range(CH):
                    t = slice(c * CT, (c + 1) * CT)
                    act.wait_ge(var_ok, c + 1)
                    nc.scalar.activation(rstd[:, t], var[:, t], ACT.Sqrt, bias=eps[:, 0:1]).then_inc(std_ok, 1)

            @block.vector
            def _(dve):
                step = Chain(dve, step_s)
                nc.vector.memset(eps[:, :], 1e-12).then_inc(eps_ok, 1)
                dve.wait_ge(w_in, 64)
                step(nc.vector.tensor_tensor(XN[:, :, :], XN[:, :, :], bc_mid(rows[:, 0, :], TILES), ALU.add))
                for n in range(NCK):
                    dve.wait_ge(pr_ok, n + 1)
                    t = slice(4 * n, 4 * n + 4)
                    nc.vector.tensor_tensor(S[:, t, :], PR[n % 2][:, :].rearrange("p (t c) -> p t c", t=4),
                                            XN[:, t, :], ALU.add).then_inc(h_ok, 1)
                dve.wait_ge(h_ok, NCK)
                for c in range(CH):
                    t = slice(c * CT, (c + 1) * CT)
                    norm_stats(dve, nc, step, S, S, sq, mean, var, c)
                    nc.vector.tensor_scalar(var[:, t], var[:, t], 1.0 / DIM, None, ALU.mult).then_inc(var_ok, 1)
                    dve.wait_ge(std_ok, c + 1)
                    step(nc.vector.reciprocal(rstd[:, t], rstd[:, t]))
                    step(nc.vector.tensor_tensor(S[:, t, :], S[:, t, :], bc_last(rstd[:, t], DIM), ALU.mult))
                    step(nc.vector.tensor_tensor(S[:, t, :], S[:, t, :], bc_mid(rows[:, 1, :], CT), ALU.mult))
                    step(nc.vector.tensor_tensor(S[:, t, :], S[:, t, :], bc_mid(rows[:, 2, :], CT), ALU.add))


def l1_experts(nc, sb, pb, sem, ins, out, X, XH, XL, S, ident):
    with ExitStack() as st:
        wr = sb("wr", [P, NEXP], F32, st)
        wrh = sb("wrh", [P, NEXP], F16, st)
        wrl = sb("wrl", [P, NEXP], F16, st)
        wf = sb("wf", [P, 3, PAIRS + 1, P], F32, st)
        wh = sb("wh", [P, 3, PAIRS + 1, P], F16, st)
        wl = sb("wl", [P, 3, PAIRS + 1, P], F16, st)
        pkf = sb("pkf", [2 * NEXP, PAIRS, P], F32, st)
        pk = sb("pk", [2 * NEXP, PAIRS, P], F16, st)
        L = sb("L", [P, TILES, NEXP + 6], F32, st)
        best = sb("best", [P, TILES, 8], F32, st)
        rest = sb("rest", [P, TILES, NEXP + 6], F32, st)
        lm = sb("lm", [P, TILES], F32, st)
        cwT = sb("cwT", [2 * NEXP, TOK], F16, st)
        cl = sb("cl", [P, TILES, 2 * NEXP], F16, st)
        idh = sb("idh", [P, P], F16, st)
        sg = sb("sgs", [P, 2, 512], F32, st)
        hb = sb("hb", [P, 2, 512], F32, st)
        hh = sb("hh", [P, 2, 512], F16, st)
        hl = sb("hl", [P, 2, 512], F16, st)
        Y = sb("Y1", [P, TILES, P], F32, st)
        G = [pb(f"G{i}", [P, 512], F32, st) for i in range(2)]
        U = [pb(f"U{i}", [P, 512], F32, st) for i in range(2)]
        W = [pb(f"W{i}", [P, 512], F32, st) for i in range(2)]
        Dn = [pb(f"D{i}", [P, 512], F32, st) for i in range(2)]
        w_in, r_in = sem("we_in"), sem("wr_in")
        step_s, log_ok, log_used = sem("p3_step"), sem("log_ok"), sem("log_used")
        exp_in, exp_ok, best_ok, cw_ok = sem("exp_in"), sem("exp_ok"), sem("best_ok"), sem("cw_ok")
        ct_ok, ct_used, pk_ok, idh_ok = sem("cwt_ok"), sem("cwt_used"), sem("pk_ok"), sem("idh_ok")
        gu_ok, silu_ok, h2_ok, hh_ok, hl_ok = (sem(n) for n in ("gu_ok", "sg_ok", "h2_ok", "hh_ok", "hl_ok"))
        wrh_ok, wrl_ok, wh_ok, wl_ok = (sem(n) for n in ("wrh_ok", "wrl_ok", "wh_ok", "wl_ok"))
        dn_ok, y_ok, s_ok, out_ok, stored = sem("dn2_ok"), sem("y2_ok"), sem("s2_ok"), sem("out_ok"), sem("stored")
        NCK, NP = TOK // 512, PAIRS + 1
        out_v = out.rearrange("b (t p) c -> p (b t) c", p=P)
        with nc.Block() as block:
            @block.sync
            def _(sp):
                sp.dma_start(wr[:, :], ins["wr"]).then_inc(r_in, 16)
                for i, n, s in ((0, "wg", "sg"), (1, "wu", "su")):
                    d = wf[:, i]
                    sp.dma_start(d[:, 0:PAIRS, :].rearrange("p k (e f) -> p (k e) f", e=2),
                                 ins[n].rearrange("e d f -> d e f")).then_inc(w_in, 16)
                    sp.dma_start(d[:, PAIRS, :], ins[s]).then_inc(w_in, 16)
                sp.dma_start(wf[:, 2, 0:PAIRS, :], ins["wd"].rearrange("(k e) f d -> (e f) k d", e=2)).then_inc(w_in, 16)
                sp.dma_start(wf[:, 2, PAIRS, :], ins["sd"]).then_inc(w_in, 16)
                sp.dma_start(pkf[:, :, :], ins["pick"]).then_inc(w_in, 16)
                for c in range(CH):
                    t = slice(c * CT, (c + 1) * CT)
                    sp.wait_ge(out_ok, c + 1)
                    sp.dma_start(out_v[:, t, :], Y[:, t, :]).then_inc(stored, 16)
                sp.wait_ge(stored, 16 * CH)

            @block.gpsimd
            def _(pool):
                nc.gpsimd.tensor_copy(idh[:, :], ident[:, :]).then_inc(idh_ok, 1)
                pool.wait_ge(w_in, 16 * 7)
                nc.gpsimd.tensor_copy(pk[:, :, :], pkf[:, :, :]).then_inc(pk_ok, 1)

            @block.tensor
            def _(pe):
                pe.wait_ge(wrl_ok, 1)
                for t in range(TILES):
                    o, x = slice(t * NEXP, (t + 1) * NEXP), slice(t * P, (t + 1) * P)
                    nc.tensor.matmul(G[0][:, o], XH[:, x], wrh[:, :], start=True, stop=False)
                    nc.tensor.matmul(G[0][:, o], XH[:, x], wrl[:, :], start=False, stop=False)
                    mm = nc.tensor.matmul(G[0][:, o], XL[:, x], wrh[:, :], start=False, stop=True)
                mm.then_inc(log_ok, 1)
                pe.wait_ge(idh_ok, 1)
                pe.wait_ge(cw_ok, 1)
                for n in range(NCK):
                    if n >= 2:
                        pe.wait_ge(ct_used, n - 1)
                    for k in range(4):
                        mm = nc.tensor.matmul(W[n % 2][0:2 * NEXP, k * P:(k + 1) * P], cl[:, 4 * n + k, :],
                                              idh[:, :], start=True, stop=True)
                    mm.then_inc(ct_ok, 1)
                pe.wait_ge(wl_ok, 1)
                pe.wait_ge(pk_ok, 1)
                pe.wait_ge(ct_used, NCK)

                def up(n):
                    c, p = n // NP, n % NP
                    x = slice(c * 512, (c + 1) * 512)

                    def halves(bank, i):
                        nc.tensor.matmul(bank[:, :], wh[:, i, p, :], XH[:, x], start=True, stop=False)
                        nc.tensor.matmul(bank[:, :], wl[:, i, p, :], XH[:, x], start=False, stop=False)
                        return nc.tensor.matmul(bank[:, :], wh[:, i, p, :], XL[:, x], start=False, stop=True)

                    if n >= 2:
                        pe.wait_ge(h2_ok, n - 1)
                    halves(G[n % 2], 0)
                    if p < PAIRS:
                        nc.tensor.matmul(W[n % 2][:, :], pk[:, p, :], cwT[:, c * 512:(c + 1) * 512],
                                         start=True, stop=True)
                    halves(U[n % 2], 1).then_inc(gu_ok, 1)

                def down(n):
                    c, p = n // NP, n % NP
                    pe.wait_ge(hl_ok, n + 1)
                    if p == 0 and c >= 2:
                        pe.wait_ge(y_ok, c - 1)
                    for k in range(4):
                        o = slice(k * P, (k + 1) * P)
                        for i, (a, w) in enumerate(((hh, wh), (hh, wl), (hl, wh))):
                            mm = nc.tensor.matmul(Dn[c % 2][:, o], a[:, n % 2, o], w[:, 2, p, :],
                                                  start=(p == 0 and k == 0 and i == 0),
                                                  stop=(p == NP - 1 and i == 2), skip_group_check=True)
                    mm.then_inc(dn_ok, 1)

                for n in range(NCK * NP + 2):
                    if n < NCK * NP:
                        up(n)
                    if n >= 2:
                        down(n - 2)

            @block.scalar
            def _(act):
                act.wait_ge(r_in, 16)
                nc.scalar.copy(wrh[:, :], wr[:, :]).then_inc(wrh_ok, 1)
                act.wait_ge(w_in, 16 * 7)
                for i in range(3):
                    nc.scalar.copy(wh[:, i], wf[:, i]).then_inc(wh_ok, 1)
                act.wait_ge(exp_in, 1)
                nc.scalar.activation(L[:, :, 0:NEXP], L[:, :, 0:NEXP], ACT.Exp).then_inc(exp_ok, 1)
                for n in range(NCK):
                    act.wait_ge(ct_ok, n + 1)
                    nc.scalar.copy(cwT[:, n * 512:(n + 1) * 512], W[n % 2][0:2 * NEXP, :]).then_inc(ct_used, 1)
                for n in range(NCK * NP + 1):
                    if n < NCK * NP:
                        act.wait_ge(gu_ok, n + 1)
                        if n >= 2:
                            act.wait_ge(h2_ok, n - 1)
                        nc.scalar.activation(sg[:, n % 2, :], G[n % 2][:, :], ACT.Silu).then_inc(silu_ok, 1)
                    if n >= 1:
                        act.wait_ge(h2_ok, n)
                        if n >= 3:
                            act.wait_ge(dn_ok, n - 2)
                        nc.scalar.copy(hh[:, (n - 1) % 2, :], hb[:, (n - 1) % 2, :]).then_inc(hh_ok, 1)
                for c in range(CH):
                    t = slice(c * CT, (c + 1) * CT)
                    act.wait_ge(y_ok, 2 * c + 2)
                    nc.scalar.activation(Y[:, t, :], Y[:, t, :], ACT.Silu).then_inc(s_ok, 1)

            @block.vector
            def _(dve):
                step = Chain(dve, step_s)
                dve.wait_ge(wrh_ok, 1)
                nc.vector.tensor_tensor(wrl[:, :], wr[:, :], wrh[:, :], ALU.subtract).then_inc(wrl_ok, 1)
                step(nc.vector.memset(L[:, :, NEXP:NEXP + 6], -1.0))
                dve.wait_ge(wh_ok, 3)
                nc.vector.tensor_tensor(wl[:, :, :, :], wf[:, :, :, :], wh[:, :, :, :], ALU.subtract).then_inc(wl_ok, 1)
                dve.wait_ge(log_ok, 1)
                lv = L[:, :, 0:NEXP]
                lp = G[0][:, :].rearrange("p (t e) -> p t e", e=NEXP)
                step(nc.vector.tensor_reduce(lm[:, :], lp, AX.X, ALU.max))
                nc.vector.tensor_tensor(lv, lp, bc_last(lm[:, :], NEXP), ALU.subtract).then_inc(exp_in, 1)
                dve.wait_ge(exp_ok, 1)
                step(nc.vector.tensor_reduce(lm[:, :], lv, AX.X, ALU.add))
                step(nc.vector.reciprocal(lm[:, :], lm[:, :]))
                step(nc.vector.tensor_tensor(lv, lv, bc_last(lm[:, :], NEXP), ALU.mult))
                for t in range(TILES):
                    i = nc.vector.max(best[:, t, :], L[:, t, :])
                    i.then_inc(best_ok, 1)
                dve.wait_ge(best_ok, TILES)
                step(nc.vector.memset(best[:, :, 2:8], -1.0))
                for t in range(TILES):
                    nc.vector.match_replace(rest[:, t, :], best[:, t, :], L[:, t, :], 0.0).then_inc(best_ok, 1)
                dve.wait_ge(best_ok, 2 * TILES)
                step(nc.vector.tensor_tensor(lv, lv, rest[:, :, 0:NEXP], ALU.subtract))
                step(nc.vector.tensor_copy(cl[:, :, 0:NEXP], lv))
                nc.vector.tensor_tensor(cl[:, :, NEXP:2 * NEXP], lv, cl[:, :, 0:NEXP], ALU.subtract).then_inc(cw_ok, 1)
                for n in range(NCK * NP + 1):
                    c, p = n // NP, n % NP
                    if n < NCK * NP:
                        dve.wait_ge(silu_ok, n + 1)
                        if n >= 2:
                            dve.wait_ge(hl_ok, n - 1)
                        m = nc.vector.tensor_tensor(hb[:, n % 2, :], U[n % 2][:, :], sg[:, n % 2, :], ALU.mult)
                        if p < PAIRS:
                            step(m)
                            m = nc.vector.tensor_tensor(hb[:, n % 2, :], hb[:, n % 2, :], W[n % 2][:, :], ALU.mult)
                        m.then_inc(h2_ok, 1)
                    if n >= 1:
                        dve.wait_ge(hh_ok, n)
                        nc.vector.tensor_tensor(hl[:, (n - 1) % 2, :], hb[:, (n - 1) % 2, :], hh[:, (n - 1) % 2, :],
                                                ALU.subtract).then_inc(hl_ok, 1)
                    if p == 1 and 1 <= c < NCK:
                        keep2(nc, dve, dn_ok, y_ok, Y, Dn, c - 1, NP)
                keep2(nc, dve, dn_ok, y_ok, Y, Dn, NCK - 1, NP)
                for c in range(CH):
                    t = slice(c * CT, (c + 1) * CT)
                    dve.wait_ge(s_ok, c + 1)
                    step(nc.vector.tensor_tensor(Y[:, t, :], Y[:, t, :], S[:, t, :], ALU.mult))
                    nc.vector.tensor_tensor(Y[:, t, :], Y[:, t, :], X[:, t, :], ALU.add).then_inc(out_ok, 1)


def keep2(nc, dve, dn_ok, y_ok, Y, Dn, c, NP):
    dve.wait_ge(dn_ok, (c + 1) * NP)
    nc.vector.tensor_copy(Y[:, 4 * c:4 * c + 4, :], Dn[c % 2][:, :].rearrange("p (t c) -> p t c", t=4)).then_inc(y_ok, 1)


def kernel(**inputs):
    import numpy as _np
    import concourse.bacc as _bacc
    from concourse import mybir as _mybir
    from concourse.bass_utils import run_bass_kernel_spmd as _run

    a = {k: _np.asarray(v) for k, v in inputs.items()}
    dist = a["L1_attn_dist_emb"]
    delta = _np.arange(-(SEQ - 1), SEQ) + M_REL - 1
    row = _np.clip(_np.where(delta < 0, delta + NDIST, delta), 0, NDIST - 1)
    y = _np.arange(TW)
    e_of, j_of = _np.repeat(_np.arange(D1), JG), _np.tile(_np.arange(JG), D1)
    fwd = row[(y[None, :] - TOFF - j_of[:, None]) + SEQ - 1]
    bwd = row[(j_of[:, None] - (y[None, :] - TOFF)) + SEQ - 1]
    eye = _np.eye(P, dtype=_np.float32)
    key_after = _np.triu(_np.ones((P, P), _np.float32), k=1) * _np.float32(NEG)
    group = _np.zeros((P, JG), _np.float32)
    group[_np.arange(P), _np.arange(P) % JG] = 1.0
    head = _np.zeros((P, H1), _np.float32)
    head[_np.arange(P), _np.arange(P) // D1] = 1.0
    pick = _np.zeros((2 * NEXP, PAIRS, P), _np.float32)
    for e in range(NEXP):
        pick[[e, NEXP + e], e // 2, (e % 2) * FE:(e % 2 + 1) * FE] = 1.0
    host = {
        "x": a["L0_attn_x"], "gamma": a["L0_attn_gamma"], "w_qkv": a["L0_attn_w_qkv"],
        "w_outT": a["L0_attn_w_out"].T, "w_upT": a["L0_ffn_w_up"].T, "w_downT": a["L0_ffn_w_down"].T,
        "wq": a["L1_attn_Wq"], "bq": a["L1_attn_bq"], "wk": a["L1_attn_Wk"], "bk": a["L1_attn_bk"],
        "wv": a["L1_attn_Wv"], "bv": a["L1_attn_bv"], "wo": a["L1_attn_Wo"], "bo": a["L1_attn_bo"],
        "ln_g": a["L1_attn_ln_gamma"], "ln_b": a["L1_attn_ln_beta"],
        "toep_f": dist[fwd, e_of[:, None]], "toep_b": dist[bwd, e_of[:, None]], "distT": dist.T,
        "wr": a["L1_ffn_Wr"], "wg": a["L1_ffn_Wg"], "wu": a["L1_ffn_Wu"], "wd": a["L1_ffn_Wd"],
        "sg": a["L1_ffn_Sg"], "su": a["L1_ffn_Su"], "sd": a["L1_ffn_Sd"],
        "identity": eye, "causal": _np.stack([key_after, key_after.T]), "group": group, "head": head,
        "pick": pick,
    }
    nc = _bacc.Bacc("TRN2", target_bir_lowering=False, num_devices=1)
    arrays, ins = {}, {}
    for name, value in host.items():
        value = _np.ascontiguousarray(value)
        arrays[f"in_{name}"] = value
        ins[name] = nc.dram_tensor(f"in_{name}", value.shape, _mybir.dt.from_np(value.dtype),
                                   kind="ExternalInput").ap()
    out = nc.dram_tensor("out_x", (BATCH, SEQ, DIM), F32, kind="ExternalOutput").ap()
    build(nc, ins, out)
    r = _run(nc, [arrays], core_ids=[0])
    return r.results[0]["out_x"]
```

```python
from contextlib import ExitStack

import concourse.bass as bass
from concourse import mybir

F32 = mybir.dt.float32
F16 = mybir.dt.float16
BF16 = mybir.dt.bfloat16
ALU = mybir.AluOpType
ACT = mybir.ActivationFunctionType
AX = mybir.AxisListType

P = 128
BATCH, SEQ, DIM = 8, 512, 128
TOK = BATCH * SEQ
TILES = TOK // P
LT = SEQ // P
CH = 4
CT = TILES // CH
H0 = 8
FF = 512
FT = FF // P
H1, D1 = 16, 8
HG = 8
NHG = H1 // HG
DE = D1 + 1
DV = DE + D1
Q_STACK = (0, 0, 1, 1)
K_STACK = (0, 1, 0, 1)
M_REL = 128
NDIST = 2 * M_REL - 1
JG = 4
NA_ = SEQ // JG
TW = 2 * SEQ - JG
TOFF = SEQ - JG
NEXP, FE, PAIRS = 16, 64, 8
QK_SCALE = 64.0
SM0 = float(P) ** -0.5
SM1 = float(D1) ** -0.5
NEG = -1.0e30


def flat(ap):
    return ap.rearrange("p a b -> p (a b)")


def bc_last(col, n):
    return col.unsqueeze(2).to_broadcast([col.shape[0], col.shape[1], n])


def bc_mid(row, a):
    return row.unsqueeze(1).to_broadcast([row.shape[0], a, row.shape[1]])


def build(nc, ins, out):
    ctx = ExitStack()
    with ctx:
        def sb(name, shape, dt=F32, stack=ctx):
            return stack.enter_context(nc.sbuf_tensor(name, shape, dt))

        def pb(name, shape, dt=F32, stack=ctx):
            return stack.enter_context(nc.psum_tensor(name, shape, dt))

        live = []

        def sem(name):
            live.append(nc.alloc_semaphore(name=name))
            return live[-1]

        def finished():
            old = list(live)
            live.clear()
            return old

        def scratch(name, shape, dt):
            return nc.dram_tensor(name, shape, dt, kind="Internal").ap()

        X = sb("X", [P, TILES, DIM])
        S = sb("S", [P, TILES, DIM])
        ident = sb("ident", [P, P])
        ident_bf = sb("ident_bf", [P, P], BF16)
        ones_bf = sb("ones_bf", [P, P], BF16)
        q_d = scratch("q_stack", (H1, D1, 4, TOK), F16)
        k_d = scratch("k_stack", (H1, D1, 4, TOK), F16)
        qx_d = scratch("q_groups", (H1, D1, 4, BATCH, SEQ), F16)
        kx_d = scratch("k_groups", (H1, D1, 4, BATCH, SEQ), F16)
        xn_d = scratch("xn_keep", (TOK, DIM), F32)
        v_d = scratch("v_split", (TOK, H1 * DV), F16)
        rb_d = scratch("rel_bound", (TOK, H1), F32)
        ctx_d = scratch("context", (TOK, DIM), F32)

        layer0(nc, sb, pb, sem, finished, ins, X, S, ident, ident_bf, ones_bf)
        layer1(nc, sb, pb, sem, ins, out, X, S, ident, ident_bf, ones_bf, (q_d, k_d, qx_d, kx_d, v_d, rb_d, ctx_d, xn_d))


def norm_stats(nc, step, src, stats, mv, c):
    for i in range(CT):
        step.more(nc.vector.bn_stats(stats[:, c * CT + i, :], src[:, c * CT + i, :]))
    step.wait()
    for i in range(CT - 1):
        step.more(nc.vector.bn_aggr(mv[:, c * CT + i, :], stats[:, c * CT + i, :]))
    return nc.vector.bn_aggr(mv[:, c * CT + CT - 1, :], stats[:, c * CT + CT - 1, :])


def normalise(nc, src, dst, mv, rstd, c):
    for t in range(c * CT, (c + 1) * CT):
        yield nc.vector.tensor_scalar(dst[:, t, :], src[:, t, :], mv[:, t, 0:1], rstd[:, t:t + 1], ALU.subtract, ALU.mult)


def wait_for(eng, s, value):
    if not isinstance(value, int) or value > 0:
        eng.wait_ge(s, value)


class Chain:

    def __init__(self, eng, s):
        self.eng, self.s, self.n = eng, s, 0

    def more(self, ins):
        self.n += 1
        ins.then_inc(self.s, 1)

    def wait(self):
        self.eng.wait_ge(self.s, self.n)

    def __call__(self, ins):
        self.more(ins)
        self.wait()


def layer0(nc, sb, pb, sem, finished, ins, X, S, ident, ident_bf, ones_bf):
    with ExitStack() as st:
        ZH = sb("ZH", [P, TOK], F16, st)
        ZL = sb("ZL", [P, TOK], F16, st)
        UH = sb("UH", [P, TOK], F16, st)
        UL = sb("UL", [P, TOK], F16, st)
        MH = sb("MH", [P, H0, P], F16, st)
        ML = sb("ML", [P, H0, P], F16, st)
        NH = sb("NH", [P, H0, P], F16, st)
        NL = sb("NL", [P, H0, P], F16, st)
        cmask = sb("cmask", [P, 2, P], BF16, st)
        wupT = sb("wupT", [P, FF], F32, st)
        wdnT = sb("wdnT", [P, FT, P], F32, st)
        l0_prepare(nc, sb, pb, sem, ins, X, S, ident, ident_bf, ones_bf,
                   ZH, ZL, UH, UL, MH, ML, NH, NL, cmask, wupT, wdnT)
        l0_attention(nc, sb, pb, sem, S, ident_bf, ones_bf, ZH, ZL, MH, ML, NH, NL, cmask)
        l0_ffn(nc, sb, pb, sem, finished, X, S, UH, UL, wupT, wdnT)


def l0_prepare(nc, sb, pb, sem, ins, X, S, ident, ident_bf, ones_bf,
               ZH, ZL, UH, UL, MH, ML, NH, NL, cmask, wupT, wdnT):
    with ExitStack() as st:
        XC = sb("XC", [P, TILES, DIM], F32, st)
        Z = sb("Z", [P, 2, CT, DIM], F32, st)
        U = sb("U", [P, 2, CT, DIM], F32, st)
        stats = sb("stats0", [P, TILES, 6], F32, st)
        statsn = sb("statsn", [P, TILES, 6], F32, st)
        mv = sb("mv0", [P, TILES, 2], F32, st)
        mvn = sb("mvn0", [P, TILES, 2], F32, st)
        rstd = sb("rstd0", [P, TILES], F32, st)
        l2 = sb("l2", [P, TILES], F32, st)
        za = sb("za", [P, TILES], F32, st)
        ub = sb("ub", [P, TILES], F32, st)
        gamma = sb("gamma", [P, DIM], F32, st)
        wqkv = sb("wqkv", [P, 3 * H0, P], F32, st)
        woT = sb("woT", [P, H0, P], F32, st)
        cmf = sb("cmf", [P, 2, P], F32, st)
        eps = sb("eps0", [P, 1], F32, st)
        tp = [pb(f"tp{i}", [P, 512], F32, st) for i in range(4)]
        wp = [pb(f"wp{i}", [P, 512], F32, st) for i in range(2)]
        x_in = [sem(f"x_in{c}") for c in range(CH)]
        w_in, g_in, k_in = sem("w_in"), sem("g_in"), sem("k_in")
        dve_step, act_step = sem("p0_dve_step"), sem("p0_act_step")
        var_ok, rstd_ok, l2_ok, zu_ok = sem("var_ok"), sem("std_ok"), sem("l2_ok"), sem("zu_ok")
        l2_in = sem("l2_in")
        tp_ok, tp_hi, tp_lo = sem("tp_ok"), sem("tp_hi"), sem("tp_lo")
        wp_ok, wp_hi, wp_lo = sem("wp_ok"), sem("wp_hi"), sem("wp_lo")
        eps_ok, s_zero = sem("eps_ok"), sem("s_zero")
        pool_ok = sem("p0_pool")
        x_v = ins["x"].rearrange("b (t p) c -> p (b t) c", p=P)

        with nc.Block() as block:
            @block.sync
            def _(sp):
                for c in range(CH):
                    t = slice(c * CT, (c + 1) * CT)
                    sp.dma_start(X[:, t, :], x_v[:, t, :]).then_inc(x_in[c], 16)
                sp.dma_start(wqkv[:, :, :], ins["w_qkv"].rearrange("(k d) c -> d k c", d=P)).then_inc(w_in, 16)
                sp.dma_start(woT[:, :, :], ins["w_outT"].rearrange("(k d) c -> d k c", d=P)).then_inc(w_in, 16)
                sp.dma_start(wupT[:, :], ins["w_upT"]).then_inc(k_in, 16)
                sp.dma_start(wdnT[:, :, :], ins["w_downT"].rearrange("(k f) c -> f k c", f=P)).then_inc(k_in, 16)

            @block.gpsimd
            def _(pool):
                nc.gpsimd.memset(ones_bf[:, :], 1.0).then_inc(pool_ok, 1)
                nc.gpsimd.memset(S[:, :, :], 0.0).then_inc(s_zero, 1)
                pool.wait_ge(k_in, 16 * 4)
                nc.gpsimd.tensor_copy(ident_bf[:, :], ident[:, :]).then_inc(pool_ok, 1)
                nc.gpsimd.tensor_copy(cmask[:, :, :], cmf[:, :, :]).then_inc(pool_ok, 1)

            @block.vector
            def _(dve):
                step = Chain(dve, dve_step)
                nc.vector.memset(eps[:, :], 1e-5).then_inc(eps_ok, 1)

                def lows(c):
                    for i in range(4):
                        n = 4 * c + i
                        lo, hi = (ZL, ZH) if i < 2 else (UL, UH)
                        o = c * CT * P + (i % 2) * 512
                        dve.wait_ge(tp_hi, n + 1)
                        nc.vector.tensor_tensor(lo[:, o:o + 512], tp[i][:, :], hi[:, o:o + 512],
                                                ALU.subtract).then_inc(tp_lo, 1)

                for c in range(CH):
                    t = slice(c * CT, (c + 1) * CT)
                    dve.wait_ge(x_in[c], 16)
                    norm_stats(nc, step, X, stats, mv, c).then_inc(var_ok, 1)
                    if c >= 1:
                        lows(c - 1)
                    dve.wait_ge(rstd_ok, c + 1)
                    step(nc.vector.reciprocal(rstd[:, t], rstd[:, t]))
                    for i in normalise(nc, X, XC, mv, rstd, c):
                        step.more(i)
                    step.wait()
                    step(norm_stats(nc, step, XC, statsn, mvn, c))
                    step(nc.vector.tensor_tensor(l2[:, t], mvn[:, t, 0], mvn[:, t, 0], ALU.mult))
                    nc.vector.tensor_tensor(l2[:, t], l2[:, t], mvn[:, t, 1], ALU.add).then_inc(l2_in, 1)
                    dve.wait_ge(l2_ok, c + 1)
                    step(nc.vector.tensor_scalar(za[:, t], l2[:, t], 1e-12, DIM ** -0.5, ALU.max, ALU.mult))
                    step(nc.vector.tensor_scalar(ub[:, t], l2[:, t], DIM ** -0.5, 1e-8, ALU.mult, ALU.add))
                    step(nc.vector.reciprocal(za[:, t], za[:, t]))
                    step(nc.vector.reciprocal(ub[:, t], ub[:, t]))
                    if c == 0:
                        dve.wait_ge(g_in, 16)
                    if c >= 2:
                        dve.wait_ge(tp_ok, 4 * (c - 1))
                    for i in range(CT):
                        k = c * CT + i
                        nc.vector.scalar_tensor_tensor(out=Z[:, c % 2, i], in0=XC[:, k, :], scalar=za[:, k:k + 1],
                                                       in1=gamma[:, :], op0=ALU.mult, op1=ALU.mult)
                        u = nc.vector.tensor_scalar(U[:, c % 2, i], XC[:, k, :], ub[:, k:k + 1], None, ALU.mult)
                    u.then_inc(zu_ok, 1)
                lows(CH - 1)
                for n in range(4):
                    lo, hi = (ML, MH) if n < 2 else (NL, NH)
                    h = 4 * (n % 2)
                    dve.wait_ge(wp_hi, n + 1)
                    nc.vector.scalar_tensor_tensor(out=flat(lo[:, h:h + 4, :]), in0=wp[n % 2][:, :],
                                                   scalar=QK_SCALE, in1=flat(hi[:, h:h + 4, :]),
                                                   op0=ALU.mult, op1=ALU.subtract).then_inc(wp_lo, 1)

            @block.scalar
            def _(act):
                act.dma_start(ident[:, :], ins["identity"]).then_inc(k_in, 16)
                act.dma_start(cmf[:, :, :], ins["causal"].rearrange("k p c -> p k c")).then_inc(k_in, 16)
                act.dma_start(gamma[:, :], ins["gamma"].partition_broadcast(P)).then_inc(g_in, 16)
                act.wait_ge(eps_ok, 1)
                for c in range(CH):
                    t = slice(c * CT, (c + 1) * CT)
                    act.wait_ge(var_ok, c + 1)
                    nc.scalar.activation(rstd[:, t], mv[:, t, 1], ACT.Sqrt, bias=eps[:, 0:1]).then_inc(rstd_ok, 1)
                    act.wait_ge(l2_in, c + 1)
                    nc.scalar.activation(l2[:, t], l2[:, t], ACT.Sqrt, scale=float(DIM)).then_inc(l2_ok, 1)
                    for i in range(4):
                        n = 4 * c + i
                        hi = ZH if i < 2 else UH
                        o = c * CT * P + (i % 2) * 512
                        act.wait_ge(tp_ok, n + 1)
                        nc.scalar.copy(hi[:, o:o + 512], tp[i][:, :]).then_inc(tp_hi, 1)
                for n in range(4):
                    hi = MH if n < 2 else NH
                    h = 4 * (n % 2)
                    act.wait_ge(wp_ok, n + 1)
                    nc.scalar.mul(flat(hi[:, h:h + 4, :]), wp[n % 2][:, :], QK_SCALE).then_inc(wp_hi, 1)

            @block.tensor
            def _(pe):
                pe.wait_ge(k_in, 64)
                for c in range(CH):
                    pe.wait_ge(zu_ok, c + 1)
                    for i in range(4):
                        if c >= 1:
                            pe.wait_ge(tp_lo, 4 * (c - 1) + i + 1)
                        src = Z if i < 2 else U
                        for k in range(4):
                            mm = nc.tensor.transpose(tp[i][:, k * P:(k + 1) * P],
                                                     src[:, c % 2, 4 * (i % 2) + k, :], ident[:, :])
                        mm.then_inc(tp_ok, 1)
                pe.wait_ge(w_in, 32)
                for n in range(4):
                    if n >= 2:
                        pe.wait_ge(wp_lo, n - 1)
                    for k in range(4):
                        h = 4 * (n % 2) + k
                        a, b = (wqkv[:, h, :], wqkv[:, H0 + h, :]) if n < 2 else (wqkv[:, 2 * H0 + h, :], woT[:, h, :])
                        mm = nc.tensor.matmul(wp[n % 2][:, k * P:(k + 1) * P], a, b, start=True, stop=True)
                    mm.then_inc(wp_ok, 1)


def l0_attention(nc, sb, pb, sem, S, ident_bf, ones_bf, ZH, ZL, MH, ML, NH, NL, cmask):
    AUX = ((3,), (0, 2), (1,))
    AUX_OFF = {3: 0, 0: 0, 2: P, 1: 0}
    AUX_DONE = (1, 3, 4)
    KEYS = ((2, 3), (1,), (0,))
    NGRP = len(KEYS)
    BASE = {2: 0, 3: 2 * P, 1: 3 * P, 0: 6 * P}
    GRP = ((0, 3 * P), (3 * P, 6 * P), (6 * P, 10 * P))
    NB = 4
    with ExitStack() as st:
        qH = sb("qH", [P, 2, SEQ], F16, st)
        qL = sb("qL", [P, 2, SEQ], F16, st)
        VH = sb("V0H", [P, NB, LT, P + 1], F16, st)
        VL = sb("V0L", [P, NB, LT, P], F16, st)
        mx = sb("mx0", [P, 2, LT], F32, st)
        dmx = sb("dmx0", [P, 2, LT, P], BF16, st)
        PF = sb("PF0", [P, 2, 10 * P], F32, st)
        PH = sb("PH0", [P, 2, 10 * P], F16, st)
        PL = sb("PL0", [P, 2, 10 * P], F16, st)
        rz = sb("rz0", [P, LT], F32, st)
        Sb = sb("Sb", [P, LT, P], F32, st)
        QP = pb("QP", [P, 512], F32, st)
        VP = pb("VP0", [P, 512], F32, st)
        AX_ = [pb(f"AXP{i}", [P, 512], F32, st) for i in range(2)]
        ST = [pb(f"STP{i}", [P, 512], F32, st) for i in range(2)]
        OPB = [pb(f"OP{i}", [P, 512], F32, st) for i in range(2)]
        OP = [o[:, 0:2 * (P + 1)].rearrange("p (t c) -> p t c", t=2) for o in OPB]
        VPV = VP[:, :].rearrange("p (t c) -> p t c", t=LT)
        ones_col = sem("ones_col")
        q_ready, q_hi, q_lo = sem("q_ready"), sem("q_hi"), sem("q_lo")
        v_ready, v_hi, v_lo = sem("v_ready"), sem("v_hi"), sem("v_lo")
        aux_ready, aux_max, dmx_ready = sem("aux_ready"), sem("aux_max"), sem("dmx_ready")
        st_ready, p_ready, p_low = sem("st_ready"), sem("p_ready"), sem("p_low")
        o_ready, rz_ready = sem("o_ready"), sem("rz_ready")
        acc_step, s_kept = sem("acc_step"), sem("s_kept")

        def back(b, h, n):
            if h >= n:
                return b, h - n
            return None if isinstance(b, int) and b == 0 else (b - 1, h - n + H0)

        def count(b, h):
            return b * H0 + h

        with nc.Block() as block:
            @block.gpsimd
            def _(pool):
                nc.gpsimd.memset(VH[:, :, :, P:P + 1], 1.0).then_inc(ones_col, 1)

                def diagonal(b, h):
                    pool.wait_ge(aux_max, (count(b, h) + 1) * LT)
                    nc.gpsimd.tensor_tensor(dmx[:, h % 2, :, :], bc_mid(ident_bf[:, :], LT),
                                            bc_last(mx[:, h % 2, :], P), ALU.mult).then_inc(dmx_ready, 1)

                def low(b, h):
                    for k, (o0, o1) in enumerate(GRP):
                        pool.wait_ge(p_ready, count(b, h) * NGRP + k + 1)
                        nc.gpsimd.tensor_tensor(PL[:, h % 2, o0:o1], PF[:, h % 2, o0:o1], PH[:, h % 2, o0:o1],
                                                ALU.subtract).then_inc(p_low, 1)

                def keep(b):
                    pool.wait_ge(acc_step, (b + 1) * H0 * LT)
                    nc.gpsimd.tensor_copy(S[:, bass.ds(b * LT, LT), :], Sb[:, :, :]).then_inc(s_kept, 1)

                def batch(b):
                    for h in range(H0):
                        diagonal(b, h)
                        if back(b, h, 1):
                            low(*back(b, h, 1))
                        if h == 1 and back(b, h, 2):
                            keep(b - 1)

                batch(0)
                with pool.Fori(1, BATCH) as b:
                    batch(b)
                low(BATCH - 1, H0 - 1)
                keep(BATCH - 1)

            @block.scalar
            def _(act):
                def high(b, h):
                    act.wait_ge(q_ready, count(b, h) + 1)
                    nc.scalar.copy(qH[:, h % 2, :], QP[:, :]).then_inc(q_hi, 1)
                    act.wait_ge(v_ready, count(b, h) + 1)
                    wait_for(act, o_ready, (count(b, h) - NB + 1) * 2)
                    nc.scalar.copy(VH[:, h % NB, :, 0:P], VPV).then_inc(v_hi, 1)

                def exponentials(b, h):
                    for k, (o0, o1) in enumerate(GRP):
                        n = h * NGRP + k
                        bank = ST[n % 2][:, 0:o1 - o0]
                        act.wait_ge(st_ready, b * (H0 * NGRP) + n + 1)
                        nc.scalar.activation(PH[:, h % 2, o0:o1], bank, ACT.Exp, scale=1.0 / QK_SCALE * SM0)
                        wait_for(act, p_low, (count(b, h) - 2) * NGRP + k + 1)
                        nc.scalar.activation(PF[:, h % 2, o0:o1], bank, ACT.Exp,
                                             scale=1.0 / QK_SCALE * SM0).then_inc(p_ready, 1)

                def batch(b):
                    for h in range(H0):
                        high(b, h)
                        if back(b, h, 1):
                            exponentials(*back(b, h, 1))

                batch(0)
                with act.Fori(1, BATCH) as b:
                    batch(b)
                exponentials(BATCH - 1, H0 - 1)

            @block.vector
            def _(dve):
                def low(b, h):
                    dve.wait_ge(q_hi, count(b, h) + 1)
                    nc.vector.tensor_tensor(qL[:, h % 2, :], QP[:, :], qH[:, h % 2, :], ALU.subtract).then_inc(q_lo, 1)
                    dve.wait_ge(v_hi, count(b, h) + 1)
                    nc.vector.tensor_tensor(VL[:, h % NB], VPV, VH[:, h % NB, :, 0:P], ALU.subtract).then_inc(v_lo, 1)

                def maxima(b, h):
                    wait_for(dve, dmx_ready, count(b, h) - 1)
                    for k, tiles in enumerate(AUX):
                        dve.wait_ge(aux_ready, count(b, h) * len(AUX) + k + 1)
                        for t in tiles:
                            o = AUX_OFF[t]
                            nc.vector.tensor_reduce(mx[:, h % 2, t:t + 1],
                                                    AX_[(h * len(AUX) + k) % 2][:, o:o + (t + 1) * P],
                                                    AX.X, ALU.max, negate=True).then_inc(aux_max, 1)

                def accumulate(b, h):
                    wait_for(dve, acc_step, count(b, h) * LT)
                    if h == 0:
                        wait_for(dve, s_kept, b)
                    for k in range(2):
                        n = (h * 2 + k) * 2
                        r = slice(2 * k, 2 * k + 2)
                        dve.wait_ge(o_ready, count(b, h) * 2 + k + 1)
                        nc.vector.tensor_scalar(rz[:, r], OP[k][:, :, P], QK_SCALE, None, ALU.mult).then_inc(rz_ready, 1)
                        dve.wait_ge(rz_ready, b * (H0 * 4) + n + 1)
                        nc.vector.reciprocal(rz[:, r], rz[:, r]).then_inc(rz_ready, 1)
                        dve.wait_ge(rz_ready, b * (H0 * 4) + n + 2)
                        for t in range(2 * k, 2 * k + 2):
                            o = OP[k][:, t - 2 * k, 0:P]
                            if h == 0:
                                i = nc.vector.tensor_scalar(Sb[:, t, :], o, rz[:, t:t + 1], None, ALU.mult)
                            else:
                                i = nc.vector.scalar_tensor_tensor(out=Sb[:, t, :], in0=o, scalar=rz[:, t:t + 1],
                                                                   in1=Sb[:, t, :], op0=ALU.mult, op1=ALU.add)
                            i.then_inc(acc_step, 1)

                def batch(b):
                    for h in range(H0):
                        low(b, h)
                        maxima(b, h)
                        if back(b, h, 2):
                            accumulate(*back(b, h, 2))

                batch(0)
                with dve.Fori(1, BATCH) as b:
                    batch(b)
                accumulate(BATCH - 1, H0 - 2)
                accumulate(BATCH - 1, H0 - 1)

            @block.tensor
            def _(pe):
                pe.wait_ge(ones_col, 1)

                def z(half, b, o, n):
                    return half[:, bass.ds(b * SEQ + o, n)]

                def query(b, h):
                    wait_for(pe, q_lo, count(b, h))
                    for j, (a, w) in enumerate(((MH, ZH), (MH, ZL), (ML, ZH))):
                        mm = nc.tensor.matmul(QP[:, :], a[:, h, :], z(w, b, 0, SEQ), start=(j == 0), stop=(j == 2))
                    mm.then_inc(q_ready, 1)

                def project(b, h):
                    wait_for(pe, v_lo, count(b, h))
                    for r in range(LT):
                        for j, (a, w) in enumerate(((ZH, NH), (ZH, NL), (ZL, NH))):
                            mm = nc.tensor.matmul(VP[:, r * P:(r + 1) * P], z(a, b, r * P, P), w[:, h, :],
                                                  start=(j == 0), stop=(j == 2))
                    mm.then_inc(v_ready, 1)

                def aux(b, h, k):
                    n = h * len(AUX) + k
                    wait_for(pe, aux_max, count(b, h) * LT + (AUX_DONE[1] - LT, 0, AUX_DONE[0])[k])
                    for t in AUX[k]:
                        o = AUX_OFF[t]
                        nc.tensor.matmul(AX_[n % 2][:, o:o + (t + 1) * P], qH[:, h % 2, t * P:(t + 1) * P],
                                         z(ZH, b, 0, (t + 1) * P), start=True, stop=False)
                        mm = nc.tensor.matmul(AX_[n % 2][:, o + t * P:o + (t + 1) * P], ident_bf[:, :], cmask[:, 0, :],
                                              start=False, stop=True)
                    mm.then_inc(aux_ready, 1)

                def scores(b, h):
                    pe.wait_ge(q_lo, count(b, h) + 1)
                    pe.wait_ge(dmx_ready, count(b, h) + 1)
                    for k, tiles in enumerate(KEYS):
                        n = h * NGRP + k
                        wait_for(pe, p_ready, b * (H0 * NGRP) + n - 1)
                        for r in tiles:
                            o = slice(r * P, SEQ)
                            c = BASE[r] - GRP[k][0]
                            bank = ST[n % 2][:, c:c + SEQ - r * P]
                            nc.tensor.matmul(bank, z(ZH, b, r * P, P), qH[:, h % 2, o], start=True, stop=False)
                            nc.tensor.matmul(bank, z(ZL, b, r * P, P), qH[:, h % 2, o], start=False, stop=False)
                            nc.tensor.matmul(bank, z(ZH, b, r * P, P), qL[:, h % 2, o], start=False, stop=False)
                            nc.tensor.matmul(bank[:, 0:P], ident_bf[:, :], cmask[:, 1, :], start=False, stop=False)
                            mm = nc.tensor.matmul(bank, ones_bf[:, :], flat(dmx[:, h % 2, r:LT, :]),
                                                  start=False, stop=True)
                        mm.then_inc(st_ready, 1)

                def values(b, h):
                    pe.wait_ge(v_lo, count(b, h) + 1)
                    pe.wait_ge(p_low, (count(b, h) + 1) * NGRP)
                    wait_for(pe, acc_step, count(b, h) * LT)
                    for t in range(LT):
                        o = OP[t // 2][:, t % 2, :]
                        for r in range(t + 1):
                            p = slice(BASE[r] + (t - r) * P, BASE[r] + (t - r + 1) * P)
                            nc.tensor.matmul(o, PH[:, h % 2, p], VH[:, h % NB, r, :], start=(r == 0), stop=False)
                            nc.tensor.matmul(o[:, 0:P], PH[:, h % 2, p], VL[:, h % NB, r, :], start=False, stop=False)
                            mm = nc.tensor.matmul(o, PL[:, h % 2, p], VH[:, h % NB, r, :], start=False, stop=(r == t))
                        if t % 2:
                            mm.then_inc(o_ready, 1)

                def batch(b):
                    for h in range(H0):
                        query(b, h)
                        project(b, h)
                        pe.wait_ge(q_hi, count(b, h) + 1)
                        aux(b, h, 0)
                        aux(b, h, 1)
                        if back(b, h, 2):
                            values(*back(b, h, 2))
                        aux(b, h, 2)
                        if back(b, h, 1):
                            scores(*back(b, h, 1))

                batch(0)
                with pe.Fori(1, BATCH) as b:
                    batch(b)
                values(BATCH - 1, H0 - 2)
                scores(BATCH - 1, H0 - 1)
                values(BATCH - 1, H0 - 1)


def l0_ffn(nc, sb, pb, sem, finished, X, S, UH, UL, wupT, wdnT):
    old_semaphores = finished()
    with ExitStack() as st:
        tu = sb("tu", [P, FF], F16, st)
        td = sb("td", [P, FT, P], F16, st)
        ta = sb("ta", [P, FF], F32, st)
        tb = sb("tb", [P, FF], F32, st)
        ones_f = sb("ones_f", [P, P], F32, st)
        rs = sb("rs", [P, 2], F32, st)
        thr = sb("thr", [P, 2], F32, st)
        nthr = sb("nthr", [P, 2], F32, st)
        Hb = sb("Hb", [P, 2, FT, 512], F32, st)
        Hh = sb("Hh", [P, 2, FT, 512], F16, st)
        Hl = sb("Hl", [P, 2, FT, 512], F16, st)
        H2 = sb("H2", [P, 2, FT, 512], F32, st)
        Y = sb("Y", [P, TILES, P], F32, st)
        ss = sb("ss", [P, TILES], F32, st)
        rr = sb("rr", [P, TILES], F32, st)
        UP = [pb(f"UP{i}", [P, 512], F32, st) for i in range(3)]
        DP = [pb(f"DP{i}", [P, 512], F32, st) for i in range(2)]
        QP = [pb(f"QQ{i}", [P, 512], F32, st) for i in range(2)]
        TP = pb("TPs", [P, 512], F32, st)
        w_step, wsum_ok, tot_ok, tern_ok = sem("w_step"), sem("wsum_ok"), sem("tot_ok"), sem("tern_ok")
        onef_ok = sem("onef_ok")
        up_ok, gelu_ok, sq_ok, hl_ok = sem("up_ok"), sem("gelu_ok"), sem("sq_ok"), sem("hl0_ok")
        dn_ok, y_ok = sem("dn_ok"), sem("y_ok")
        rms_in, rms_ok, pre_ok, silu_ok, res_step = (sem(n) for n in ("rms_in", "rms_ok", "pre_ok", "silu_ok", "res_step"))
        NCK = TOK // 512

        with nc.Block() as block:
            @block.gpsimd
            def _(pool):
                nc.gpsimd.memset(ones_f[:, :], 1.0).then_inc(onef_ok, 1)
                nc.clear_and_free_semaphores(old_semaphores)
                for c in range(NCK):
                    for f in range(FT):
                        n = c * FT + f
                        pool.wait_ge(gelu_ok, n + 1)
                        if c >= 2:
                            pool.wait_ge(dn_ok, c - 1)
                        nc.gpsimd.tensor_tensor(Hl[:, c % 2, f, :], Hb[:, c % 2, f, :], Hh[:, c % 2, f, :],
                                                ALU.subtract).then_inc(hl_ok, 1)
                for k in range(2 * CH):
                    t = slice(k * CT // 2, (k + 1) * CT // 2)
                    pool.wait_ge(res_step, k // 2 + 1)
                    nc.gpsimd.tensor_tensor(X[:, t, :], X[:, t, :], Y[:, t, :], ALU.add)

            @block.tensor
            def _(pe):
                pe.wait_ge(onef_ok, 1)
                pe.wait_ge(wsum_ok, 2)
                nc.tensor.matmul(TP[:, 0:2], ones_f[:, :], rs[:, :], start=True, stop=True).then_inc(tot_ok, 1)
                pe.wait_ge(tern_ok, 2)

                def up(c):
                    for f in range(FT):
                        n = c * FT + f
                        if n >= 3:
                            pe.wait_ge(gelu_ok, n - 2)
                        nc.tensor.matmul(UP[n % 3][:, :], tu[:, f * P:(f + 1) * P], UH[:, c * 512:(c + 1) * 512],
                                         start=True, stop=False)
                        nc.tensor.matmul(UP[n % 3][:, :], tu[:, f * P:(f + 1) * P], UL[:, c * 512:(c + 1) * 512],
                                         start=False, stop=True).then_inc(up_ok, 1)

                def down(c):
                    pe.wait_ge(hl_ok, (c + 1) * FT)
                    if c >= 2:
                        pe.wait_ge(y_ok, 2 * (c - 1))
                    for k in range(4):
                        for f in range(FT):
                            for half in (Hh, Hl):
                                nc.tensor.matmul(DP[c % 2][:, k * P:(k + 1) * P], half[:, c % 2, f, k * P:(k + 1) * P],
                                                 td[:, f, :], start=(f == 0 and half is Hh),
                                                 stop=(f == FT - 1 and half is Hl))
                    pe.wait_ge(sq_ok, (c + 1) * (2 * FT - 1))
                    for k in range(4):
                        mm = nc.tensor.matmul(QP[c % 2][:, k:k + 1], H2[:, c % 2, 0, k * P:(k + 1) * P],
                                              ones_f[:, 0:1], start=True, stop=True)
                    mm.then_inc(dn_ok, 1)

                for c in range(NCK + 1):
                    if c < NCK:
                        up(c)
                    if c >= 1:
                        down(c - 1)

            @block.scalar
            def _(act):
                for c in range(NCK):
                    for f in range(FT):
                        n = c * FT + f
                        act.wait_ge(up_ok, n + 1)
                        if c >= 2:
                            act.wait_ge(dn_ok, c - 1)
                            act.wait_ge(hl_ok, (c - 1) * FT)
                            act.wait_ge(sq_ok, (c - 1) * (2 * FT - 1))
                        nc.scalar.activation(Hh[:, c % 2, f, :], UP[n % 3][:, :], ACT.Gelu)
                        nc.scalar.activation(Hb[:, c % 2, f, :], UP[n % 3][:, :], ACT.Gelu).then_inc(gelu_ok, 1)
                act.wait_ge(rms_in, 1)
                nc.scalar.activation(rr[:, :], ss[:, :], ACT.Sqrt).then_inc(rms_ok, 1)
                for c in range(CH):
                    t = slice(c * CT, (c + 1) * CT)
                    act.wait_ge(pre_ok, 1)
                    for k in range(c * CT, (c + 1) * CT):
                        i = nc.scalar.activation(Y[:, k, :], Y[:, k, :], ACT.Silu, scale=rr[:, k:k + 1])
                    i.then_inc(silu_ok, 1)

            @block.vector
            def _(dve):
                step = Chain(dve, w_step)
                wd = wdnT[:, :, :].rearrange("p f c -> p (f c)")
                nc.vector.tensor_reduce(rs[:, 0:1], wupT[:, :], AX.X, ALU.add, apply_absolute_value=True).then_inc(wsum_ok, 1)
                nc.vector.tensor_reduce(rs[:, 1:2], wd, AX.X, ALU.add, apply_absolute_value=True).then_inc(wsum_ok, 1)
                dve.wait_ge(tot_ok, 1)
                step(nc.vector.tensor_scalar(thr[:, :], TP[:, 0:2], 0.5 / (FF * DIM), None, ALU.mult))
                step(nc.vector.tensor_scalar(nthr[:, :], thr[:, :], -1.0, None, ALU.mult))
                for k, (w, d) in enumerate(((wupT[:, :], tu[:, :]), (wd, td[:, :, :].rearrange("p f c -> p (f c)")))):
                    step(nc.vector.tensor_scalar(ta[:, :], w, thr[:, k:k + 1], None, ALU.is_gt))
                    step(nc.vector.tensor_scalar(tb[:, :], w, nthr[:, k:k + 1], None, ALU.is_lt))
                    nc.vector.tensor_tensor(d, ta[:, :], tb[:, :], ALU.subtract).then_inc(tern_ok, 1)
                    dve.wait_ge(tern_ok, k + 1)

                def keep(c):
                    dve.wait_ge(dn_ok, c + 1)
                    nc.vector.tensor_copy(Y[:, 4 * c:4 * c + 4, :], DP[c % 2][:, :].rearrange("p (t c) -> p t c", t=4))\
                        .then_inc(y_ok, 1)
                    nc.vector.tensor_copy(ss[:, 4 * c:4 * c + 4], QP[c % 2][:, 0:4]).then_inc(y_ok, 1)

                for c in range(NCK):
                    for f in range(FT):
                        dve.wait_ge(gelu_ok, c * FT + f + 1)
                        if c >= 2:
                            dve.wait_ge(dn_ok, c - 1)
                        nc.vector.tensor_tensor(H2[:, c % 2, f, :], Hb[:, c % 2, f, :], Hb[:, c % 2, f, :],
                                                ALU.mult).then_inc(sq_ok, 1)
                    base = c * (2 * FT - 1) + FT
                    for k, (x, y) in enumerate(((0, 1), (2, 3), (0, 2))):
                        dve.wait_ge(sq_ok, base if k < 2 else base + 2)
                        nc.vector.tensor_tensor(H2[:, c % 2, x, :], H2[:, c % 2, x, :], H2[:, c % 2, y, :],
                                                ALU.add).then_inc(sq_ok, 1)
                    if c >= 1:
                        keep(c - 1)
                keep(NCK - 1)
                dve.wait_ge(y_ok, 2 * NCK)
                nc.vector.tensor_scalar(ss[:, :], ss[:, :], 1.0 / FF, None, ALU.mult).then_inc(rms_in, 1)
                dve.wait_ge(rms_ok, 1)
                step(nc.vector.tensor_scalar(rr[:, :], rr[:, :], 1e-8, None, ALU.add))
                nc.vector.reciprocal(rr[:, :], rr[:, :]).then_inc(pre_ok, 1)
                for c in range(CH):
                    t = slice(c * CT, (c + 1) * CT)
                    dve.wait_ge(silu_ok, c + 1)
                    nc.vector.tensor_tensor(Y[:, t, :], Y[:, t, :], S[:, t, :], ALU.mult).then_inc(res_step, 1)


def layer1(nc, sb, pb, sem, ins, out, X, S, ident, ident_bf, ones_bf, dram):
    with ExitStack() as st:
        XH = sb("XH", [P, TOK], F16, st)
        XL = sb("XL", [P, TOK], F16, st)
        toep = [sb(n, [P, TW], F16, st) for n in ("toep_fwd", "toep_bwd")]
        kbd = sb("kbd", [P, H1 // 4, 4, SEQ], F16, st)
        l1_prepare(nc, sb, pb, sem, ins, X, XH, XL, toep, kbd, ident, dram)
        l1_attention(nc, sb, pb, sem, ins, S, toep, kbd, ident_bf, ones_bf, dram)
        l1_project(nc, sb, pb, sem, ins, S, ident, dram)
        l1_experts(nc, sb, pb, sem, ins, out, X, XH, XL, S, ident)


def l1_prepare(nc, sb, pb, sem, ins, X, XH, XL, toep, kbd, ident, dram):
    q_d, k_d, qx_d, kx_d, v_d, rb_d, ctx_d, xn_d = dram
    with ExitStack() as st:
        XN = sb("XN", [P, TILES, DIM], F32, st)
        stats = sb("stats1", [P, TILES, 6], F32, st)
        mv = sb("mv1", [P, TILES, 2], F32, st)
        rstd = sb("rstd1", [P, TILES], F32, st)
        eps = sb("eps1", [P, 1], F32, st)
        w3 = sb("w3", [P, 3, P], F32, st)
        wh = sb("w3h", [P, 3, P], F16, st)
        wl = sb("w3l", [P, 3, P], F16, st)
        bqk = sb("bqk", [P, 2], F32, st)
        bvr = sb("bvr", [P, P], F32, st)
        tf = sb("tf", [P, 2, TW], F32, st)
        th = sb("th", [P, 2, TW], F16, st)
        tl = sb("tl", [P, 2, TW], F16, st)
        side = sb("side", [P, 2, 2], F32, st)
        dT = sb("dT", [P, NDIST], F32, st)
        dmax = sb("dmax", [P, 1], F32, st)
        headm = sb("headm", [P, H1], F32, st)
        bound = sb("bound", [P, H1], F16, st)
        qf = sb("qf", [P, 2, 512], F32, st)
        qa = sb("qa", [P, 2, 512], F16, st)
        hs = sb("hs", [P, 4, 2, 512], F16, st)
        hx = sb("hx", [P, 4, 2, 512], F16, st)
        vf = sb("vf", [P, 2, 4, H1, D1], F32, st)
        vo = sb("vo", [P, 2, 4, H1, DV], F16, st)
        rb = sb("rb", [P, TILES, H1], F32, st)
        TPp = [pb(f"tq{i}", [P, 512], F32, st) for i in range(2)]
        PR = [pb(f"pr{i}", [P, 512], F32, st) for i in range(2)]
        VP = [pb(f"vp{i}", [P, 512], F32, st) for i in range(2)]
        RP = pb("rp", [P, 512], F32, st)
        w_in, t_in, d_in = sem("w1_in"), sem("t_in"), sem("d_in")
        step_s, var_ok, std_ok = sem("p1_step"), sem("var1_ok"), sem("std1_ok")
        eps_ok, wh_ok, wl_ok = sem("eps1_ok"), sem("w3h_ok"), sem("w3l_ok")
        xn_ok, tp_ok, xh_ok, xl_ok = sem("xn_ok"), sem("tq_ok"), sem("xh_ok"), sem("xl_ok")
        pr_ok, qf_ok, hi_ok, lo_ok = (sem(n) for n in ("pr_ok", "qf_ok", "hi_ok", "lo_ok"))
        qk_out = [sem(f"qk_out{i}") for i in range(4)]
        hx_hi, hx_ok, hx_out, xn_out = sem("hx_hi"), sem("hx_ok"), [sem(f"hx_out{i}") for i in range(4)], sem("xn_out")
        abs_ok, rp_ok, rb_ok, rb_out = (sem(n) for n in ("abs_ok", "rp_ok", "rb_ok", "rb_out"))
        vp_ok, vf_ok, vh_ok, vo_ok, vones = (sem(n) for n in ("vp_ok", "vf_ok", "vh_ok", "vo_ok", "vones"))
        v_out = [sem("v_out0"), sem("v_out1")]
        tab_ok, bound_ok, bd_zero = sem("tab_ok"), sem("bound_ok"), sem("bd_zero")
        NCK = TOK // 512

        def grouped(i, half):
            return (hx[:, i, half].rearrange("p (j a) -> p j a", j=JG),
                    hs[:, i, half].rearrange("p (a j) -> p j a", j=JG))

        with nc.Block() as block:
            @block.sync
            def _(sp):
                for k, n in enumerate(("wq", "wk", "wv")):
                    sp.dma_start(w3[:, k, :], ins[n]).then_inc(w_in, 16)
                sp.dma_start(bqk[:, 0:1], ins["bq"].unsqueeze(1)).then_inc(w_in, 16)
                sp.dma_start(bqk[:, 1:2], ins["bk"].unsqueeze(1)).then_inc(w_in, 16)
                sp.dma_start(bvr[:, :], ins["bv"].partition_broadcast(P)).then_inc(w_in, 16)
                sp.dma_start(headm[:, :], ins["head"]).then_inc(w_in, 16)
                for k, n in enumerate(("toep_f", "toep_b")):
                    sp.dma_start(tf[:, k, :], ins[n]).then_inc(t_in, 16)
                sp.dma_start(side[:, :, :], ins["side"]).then_inc(t_in, 16)
                for h in range(H1):
                    sp.dma_start(dT[h * D1:(h + 1) * D1, :], ins["distT"]).then_inc(d_in, 16)
                def halves(d, src, order, c, done):
                    for i in range(2):
                        places = slice(2 * i, 2 * i + 2) if order is K_STACK else slice(i, 4, 2)
                        sp.dma_start(d.rearrange("h e s t -> (h e) s t")[:, places], src).then_inc(done, 16)

                for c in range(NCK):
                    for k, (d, dx, order) in enumerate(((q_d, qx_d, Q_STACK), (k_d, kx_d, K_STACK))):
                        n = 2 * c + k
                        sp.wait_ge(lo_ok, n + 1)
                        halves(d[:, :, :, c * 512:(c + 1) * 512], hs[:, n % 4], order, c, qk_out[n % 4])
                        sp.wait_ge(hx_hi, n + 1)
                        sp.wait_ge(hx_ok, n + 1)
                        halves(dx[:, :, :, c, :], hx[:, n % 4], order, c, hx_out[n % 4])
                    if c == NCK - 2:
                        sp.wait_ge(xn_ok, CH)
                        sp.dma_start(xn_d.rearrange("(t p) n -> p t n", p=P), XN[:, :, :]).then_inc(xn_out, 16)
                    sp.wait_ge(vo_ok, c + 1)
                    sp.dma_start(v_d[c * 512:(c + 1) * 512, :].rearrange("(t p) n -> p t n", p=P),
                                 vo[:, c % 2].rearrange("p t h e -> p t (h e)")).then_inc(v_out[c % 2], 16)
                sp.wait_ge(rb_ok, NCK)
                sp.dma_start(rb_d.rearrange("(t p) h -> p t h", p=P), rb[:, :, :]).then_inc(rb_out, 16)
                sp.wait_ge(xn_out, 16)
                for k in range(4):
                    sp.wait_ge(qk_out[k], 16 * 2 * NCK // 2)
                    sp.wait_ge(hx_out[k], 16 * 2 * NCK // 2)
                for k in range(2):
                    sp.wait_ge(v_out[k], 8 * NCK)
                sp.wait_ge(rb_out, 16)

            @block.gpsimd
            def _(pool):
                nc.gpsimd.memset(vo[:, :, :, :, D1:DE], 1.0).then_inc(vones, 1)
                nc.gpsimd.memset(kbd[:, :, :, :], 0.0).then_inc(bd_zero, 1)
                for n in range(2 * NCK):
                    pool.wait_ge(lo_ok, n + 1)
                    if n >= 4:
                        pool.wait_ge(hx_out[n % 4], 32 * (n // 4))
                    nc.gpsimd.tensor_copy(*grouped(n % 4, 1)).then_inc(hx_ok, 1)

            @block.scalar
            def _(act):
                act.wait_ge(w_in, 16 * 7)
                nc.scalar.copy(wh[:, :, :], w3[:, :, :]).then_inc(wh_ok, 1)
                act.wait_ge(eps_ok, 1)
                act.wait_ge(var_ok, CH)
                nc.scalar.activation(rstd[:, :], mv[:, :, 1], ACT.Sqrt, bias=eps[:, 0:1]).then_inc(std_ok, 1)

                def x_high(n):
                    act.wait_ge(tp_ok, n + 1)
                    nc.scalar.copy(XH[:, n * 512:(n + 1) * 512], TPp[n % 2][:, :]).then_inc(xh_ok, 1)

                def project(n):
                    act.wait_ge(pr_ok, n + 1)
                    if n >= 2:
                        act.wait_ge(lo_ok, n - 1)
                    if n % 2 == 0 and n >= 2:
                        act.wait_ge(abs_ok, n // 2)
                    nc.scalar.activation(qf[:, n % 2, :], PR[n % 2][:, :], ACT.Identity,
                                         bias=bqk[:, n % 2:n % 2 + 1]).then_inc(qf_ok, 1)
                    act.wait_ge(qf_ok, n + 1)
                    if n >= 4:
                        act.wait_ge(qk_out[n % 4], 32 * (n // 4))
                        act.wait_ge(hx_hi, n - 3)
                    nc.scalar.copy(hs[:, n % 4, 0, :], qf[:, n % 2, :]).then_inc(hi_ok, 1)
                    if n % 2 == 0:
                        if n >= 4:
                            act.wait_ge(rp_ok, n // 2 - 1)
                        nc.scalar.activation(qa[:, (n // 2) % 2, :], qf[:, 0, :], ACT.Abs).then_inc(abs_ok, 1)
                    else:
                        c = n // 2
                        act.wait_ge(vf_ok, c + 1)
                        if c == 0:
                            act.wait_ge(vones, 1)
                        if c >= 2:
                            act.wait_ge(v_out[c % 2], 16 * (c // 2))
                        nc.scalar.copy(vo[:, c % 2, :, :, 0:D1], vf[:, c % 2]).then_inc(vh_ok, 1)

                for c in range(CH + 1):
                    for n in range(2 * c, 2 * c + 2):
                        if c < CH:
                            x_high(n)
                    for n in range(4 * c - 4, 4 * c):
                        if c >= 1:
                            project(n)
                    if c == 1:
                        act.wait_ge(t_in, 48)
                        nc.scalar.copy(th[:, :, :], tf[:, :, :]).then_inc(tab_ok, 1)

            @block.vector
            def _(dve):
                step = Chain(dve, step_s)
                nc.vector.memset(eps[:, :], 1e-5).then_inc(eps_ok, 1)
                dve.wait_ge(wh_ok, 1)
                nc.vector.tensor_tensor(wl[:, :, :], w3[:, :, :], wh[:, :, :], ALU.subtract).then_inc(wl_ok, 1)

                def x_low(n):
                    dve.wait_ge(xh_ok, n + 1)
                    nc.vector.tensor_tensor(XL[:, n * 512:(n + 1) * 512], TPp[n % 2][:, :],
                                            XH[:, n * 512:(n + 1) * 512], ALU.subtract).then_inc(xl_ok, 1)

                for c in range(CH):
                    norm_stats(nc, step, X, stats, mv, c).then_inc(var_ok, 1)
                dve.wait_ge(d_in, 16 * H1)
                step(nc.vector.tensor_reduce(dmax[:, :], dT[:, :], AX.X, ALU.max, apply_absolute_value=True))
                dve.wait_ge(w_in, 16 * 7)
                nc.vector.tensor_scalar(bound[:, :], headm[:, :], dmax[:, 0:1], 1.01, ALU.mult, ALU.mult).then_inc(bound_ok, 1)
                bv = bvr[:, :].rearrange("p (h e) -> p h e", h=H1).unsqueeze(1).to_broadcast([P, 4, H1, D1])

                def project(c):
                    for k in range(2):
                        n = 2 * c + k
                        dve.wait_ge(hi_ok, n + 1)
                        if n >= 4:
                            dve.wait_ge(qk_out[n % 4], 32 * (n // 4))
                            dve.wait_ge(hx_ok, n - 3)
                        nc.vector.tensor_tensor(hs[:, n % 4, 1, :], qf[:, n % 2, :], hs[:, n % 4, 0, :],
                                                ALU.subtract).then_inc(lo_ok, 1)
                        if n >= 4:
                            dve.wait_ge(hx_out[n % 4], 32 * (n // 4))
                        nc.vector.tensor_copy(*grouped(n % 4, 0)).then_inc(hx_hi, 1)
                        if k == 0:
                            dve.wait_ge(vp_ok, c + 1)
                            if c >= 2:
                                dve.wait_ge(vo_ok, c - 1)
                            nc.vector.tensor_tensor(vf[:, c % 2],
                                                    VP[c % 2][:, :].rearrange("p (t h e) -> p t h e", t=4, h=H1),
                                                    bv, ALU.add).then_inc(vf_ok, 1)
                    dve.wait_ge(vh_ok, c + 1)
                    nc.vector.tensor_tensor(vo[:, c % 2, :, :, DE:DV], vf[:, c % 2], vo[:, c % 2, :, :, 0:D1],
                                            ALU.subtract).then_inc(vo_ok, 1)
                    dve.wait_ge(rp_ok, c + 1)
                    nc.vector.tensor_copy(rb[:, 4 * c:4 * c + 4, :],
                                          RP[:, 0:4 * H1].rearrange("p (t h) -> p t h", t=4)).then_inc(rb_ok, 1)

                dve.wait_ge(std_ok, 1)
                step(nc.vector.reciprocal(rstd[:, :], rstd[:, :]))
                for c in range(CH + 2):
                    if c < CH:
                        for i in normalise(nc, X, XN, mv, rstd, c):
                            pass
                        i.then_inc(xn_ok, 1)
                    if 1 <= c <= CH:
                        x_low(2 * c - 2)
                        x_low(2 * c - 1)
                    if c >= 2:
                        project(2 * c - 4)
                        project(2 * c - 3)
                dve.wait_ge(tab_ok, 1)
                dve.wait_ge(t_in, 48)
                step(nc.vector.tensor_tensor(tl[:, :, :], tf[:, :, :], th[:, :, :], ALU.subtract))
                for k in range(2):
                    step(nc.vector.tensor_scalar(toep[k][:, :], th[:, k, :], side[:, k, 0:1], None, ALU.mult))
                    step(nc.vector.scalar_tensor_tensor(out=toep[k][:, :], in0=tl[:, k, :], scalar=side[:, k, 1:2],
                                                        in1=toep[k][:, :], op0=ALU.mult, op1=ALU.add))

            @block.tensor
            def _(pe):
                def transposes(n):
                    pe.wait_ge(xn_ok, n // 2 + 1)
                    if n >= 2:
                        pe.wait_ge(xl_ok, n - 1)
                    for k in range(4):
                        mm = nc.tensor.transpose(TPp[n % 2][:, k * P:(k + 1) * P], XN[:, 4 * n + k, :], ident[:, :])
                    mm.then_inc(tp_ok, 1)

                def project(c):
                    pe.wait_ge(xl_ok, c + 1)
                    x = slice(c * 512, (c + 1) * 512)
                    for k in range(2):
                        n = 2 * c + k
                        if n >= 2:
                            pe.wait_ge(qf_ok, n - 1)
                        nc.tensor.matmul(PR[n % 2][:, :], wh[:, k, :], XH[:, x], start=True, stop=False)
                        nc.tensor.matmul(PR[n % 2][:, :], wl[:, k, :], XH[:, x], start=False, stop=False)
                        nc.tensor.matmul(PR[n % 2][:, :], wh[:, k, :], XL[:, x], start=False, stop=True).then_inc(pr_ok, 1)
                    if c >= 2:
                        pe.wait_ge(vf_ok, c - 1)
                    for k in range(4):
                        o = slice(k * P, (k + 1) * P)
                        xs = slice(c * 512 + k * P, c * 512 + (k + 1) * P)
                        nc.tensor.matmul(VP[c % 2][:, o], XH[:, xs], wh[:, 2, :], start=True, stop=False)
                        nc.tensor.matmul(VP[c % 2][:, o], XH[:, xs], wl[:, 2, :], start=False, stop=False)
                        mm = nc.tensor.matmul(VP[c % 2][:, o], XL[:, xs], wh[:, 2, :], start=False, stop=True)
                    mm.then_inc(vp_ok, 1)
                    pe.wait_ge(abs_ok, c + 1)
                    if c >= 1:
                        pe.wait_ge(rb_ok, c)
                    for k in range(4):
                        mm = nc.tensor.matmul(RP[:, k * H1:(k + 1) * H1], qa[:, c % 2, k * P:(k + 1) * P], bound[:, :],
                                              start=True, stop=True)
                    mm.then_inc(rp_ok, 1)

                for c in range(CH + 1):
                    for n in range(2 * c, 2 * c + 2):
                        if c < CH:
                            transposes(n)
                    if c == 1:
                        pe.wait_ge(wl_ok, 1)
                        pe.wait_ge(bound_ok, 1)
                    for n in range(2 * c - 2, 2 * c):
                        if c >= 1:
                            project(n)


def l1_attention(nc, sb, pb, sem, ins, S, toep, kbd, ident_bf, ones_bf, dram):
    fwd, bwd = toep
    q_d, k_d, qx_d, kx_d, v_d, rb_d, ctx_d, xn_d = dram
    KC, QC = 32, 64
    SLOTS = SEQ // KC
    UC = SLOTS // NHG
    LAG = 4
    QG = H1 // 4
    NA, NB, NP32 = 4, 2, 4
    assert SLOTS == NHG * LT * (P // QC)
    with ExitStack() as st:
        qst = sb("qst", [P, QG, SEQ], F16, st)
        kd = sb("kd", [P, H1, SEQ], F16, st)
        qd = sb("qd", [P, 2, H1, P], F16, st)
        rbb = sb("rbb", [P, LT, H1], F32, st)
        gm = sb("gm", [P, JG], F16, st)
        gmf = sb("gmf", [P, JG], F32, st)
        idh = sb("idh1", [P, P], F16, st)
        S1H = sb("S1H", [P, 2, H1, SEQ], F16, st)
        S1L = sb("S1L", [P, 2, H1, SEQ], F16, st)
        PF = sb("PF", [P, NP32, HG, QC], F32, st)
        PH = sb("PH", [P, NHG, LT, HG, P], F16, st)
        PL = sb("PL", [P, NHG, LT, HG, P], F16, st)
        dm = sb("dm", [P, NHG, HG, P], BF16, st)
        mq = sb("mq", [P, LT, H1], F32, st)
        mx = sb("mx1", [P, H1], F32, st)
        rz = sb("rz1", [P, HG], F32, st)
        ol = sb("ol", [P, HG, D1], F32, st)
        spare = S[:, :, :].rearrange("p t c -> p (t c)")
        nv = NHG * LT * HG * DV // 2
        ncx = LT * DIM
        vb = spare[:, 0:nv].bitcast(F16).rearrange("p (g t n) -> p g t n", g=NHG, t=LT)
        cb = spare[:, nv:nv + ncx].rearrange("p (t n) -> p t n", t=LT)
        nk = H1 * NA_ // 2
        kc, qc = (spare[:, nv + ncx + i * nk:nv + ncx + (i + 1) * nk].bitcast(F16).rearrange("p (h a) -> p h a", h=H1)
                  for i in range(2))
        A = [pb(f"A{i}", [P, 512], F32, st) for i in range(NA)]
        B = [pb(f"B{i}", [P, 512], F32, st) for i in range(NB)]
        O = [pb(f"O{i}", [P, 512], F32, st) for i in range(2)]
        gm_in, gm_ok, idh_ok = sem("gm_in"), sem("gm_ok"), sem("idh1_ok")
        kc_in, qc_in = sem("kc_in"), sem("qc_in")
        bd_in, qst_in = ([sem(f"{n}{k}") for k in range(2)] for n in ("bd_in", "qst_in"))
        rb_in, v_in = sem("rb_in"), [sem(f"v_in{g}") for g in range(NHG)]
        kd_ok, qd_ok = sem("kd_ok"), sem("qd_ok")
        a_ready, s1_hi, s1_lo = sem("a_ready"), sem("s1_hi"), sem("s1_lo")
        mx_step, dm_ok = sem("mx_step"), sem("dm_ok")
        b_ready, p_ready, pl_ok = sem("b_ready"), sem("p_ready1"), sem("pl_ok")
        o_ready, o_step, c_ready, c_out = sem("o_ready1"), sem("o_step"), sem("c_ready"), sem("c_out")

        def vb3(bank):
            return bank[:, :].rearrange("p (h c) -> p h c", h=HG)

        def back(b, t, n):
            if t >= n:
                return b, t - n
            return None if isinstance(b, int) and b == 0 else (b - 1, t - n + LT)

        def behind(b, t, i):
            at = back(b, t, 1 if i >= LAG else 2)
            return at and (*at, (i - LAG) % SLOTS)

        def split(j):
            return j // UC, j % UC // 2, j % 2

        def spread(dst, src):
            n = src.shape[2]
            return (dst.rearrange("p h (a j) -> p h a j", j=JG),
                    src.unsqueeze(3).to_broadcast([P, H1, n, JG]),
                    gm[:, :].unsqueeze(1).unsqueeze(1).to_broadcast([P, H1, n, JG]))

        def slots(b, t):
            return b * (LT * SLOTS) + t * SLOTS

        def units(b, t):
            return b * (LT * NHG) + t * NHG

        def values_at(b, t, i):
            first = {0: LAG + UC + 2, 1: LAG + 2}
            for g, n in ((0, 1), (0, 2), (1, 2)):
                k = i - first[g] + (SLOTS if (g, n) == (0, 2) else 0)
                if 0 <= k < HG // 2 and back(b, t, n):
                    return (*back(b, t, n), g, k)

        def finish(step):
            for t in (LT, LT + 1):
                for i in range(SLOTS):
                    step(BATCH - 1, t, i)

        def past(t):
            return t >= LT

        with nc.Block() as block:
            @block.sync
            def _(sp):
                kg = kx_d.rearrange("h e s b (j a) -> b j (e s) h a", j=JG)
                qg = qx_d.rearrange("h e s b (j a) -> b j (e s) h a", j=JG)
                ks = k_d.rearrange("(g f) e s (b t) -> b f (e s) g t", f=4, b=BATCH)
                qs = q_d.rearrange("(g f) e s (b t) -> b (f e s) g t", f=4, b=BATCH)
                vs = v_d.rearrange("(b t p) (g n) -> b g p t n", p=P, t=LT, g=NHG)

                def load(b):
                    h = SEQ // 2
                    wait_for(sp, kd_ok, b * LT)
                    for j in range(JG):
                        sp.dma_start(kc[32 * j:32 * j + 32], kg[b, j]).then_inc(kc_in, 16)

                    def queries(k):
                        wait_for(sp, a_ready, slots(b - 1, 2 * k + 2))
                        sp.dma_start(qst[:, :, k * h:(k + 1) * h], qs[b, :, :, k * h:(k + 1) * h]).then_inc(qst_in[k], 16)

                    def keys(k):
                        wait_for(sp, a_ready, slots(b - 1, LT - 1) + (k + 1) * SLOTS // 2)
                        for f in range(4):
                            sp.dma_start(kbd[32 * f:32 * f + 32, :, f, k * h:(k + 1) * h],
                                         ks[b, f, :, :, k * h:(k + 1) * h]).then_inc(bd_in[k], 16)

                    queries(0)
                    keys(0)
                    wait_for(sp, qd_ok, b * LT)
                    for j in range(JG):
                        sp.dma_start(qc[32 * j:32 * j + 32], qg[b, j]).then_inc(qc_in, 16)
                    keys(1)
                    queries(1)
                    wait_for(sp, dm_ok, units(b, 0))
                    sp.dma_start(rbb[:, :, :], rb_d.rearrange("(b t p) n -> b p t n", p=P, t=LT)[b]).then_inc(rb_in, 16)
                    for g in range(NHG):
                        wait_for(sp, o_ready, units(b - 1, LT - 1) + g + 1)
                        sp.dma_start(vb[:, g], vs[b, g]).then_inc(v_in[g], 16)

                load(0)
                with sp.Fori(1, BATCH) as b:
                    load(b)

            @block.gpsimd
            def _(pool):
                pool.dma_start(gmf[:, :], ins["group"]).then_inc(gm_in, 16)
                nc.gpsimd.tensor_copy(idh[:, :], ident_bf[:, :]).then_inc(idh_ok, 1)
                pool.wait_ge(gm_in, 16)
                nc.gpsimd.tensor_copy(gm[:, :], gmf[:, :]).then_inc(gm_ok, 1)
                pool.wait_ge(gm_ok, 1)

                def spread_q(b, t):
                    if t == 0:
                        pool.wait_ge(qc_in, (b + 1) * 16 * JG)
                    wait_for(pool, b_ready, slots(b, t - 1))
                    nc.gpsimd.tensor_tensor(*spread(qd[:, t % 2], qc[:, :, t * P // JG:(t + 1) * P // JG]), ALU.mult)\
                      .then_inc(qd_ok, 1)

                def step(b, t, i):
                    if i == LAG and not past(t):
                        spread_q(b, t)
                    at = behind(b, t, i)
                    if at:
                        b0, t0, j = at
                        if t0 < LT:
                            g, r, half = split(j)
                            o = slice(half * QC, (half + 1) * QC)
                            pool.wait_ge(p_ready, slots(b0, t0) + j + 1)
                            nc.gpsimd.tensor_tensor(PL[:, g, r, :, o], PF[:, j % NP32], PH[:, g, r, :, o],
                                                    ALU.subtract).then_inc(pl_ok, 1)

                def store(b):
                    pool.wait_ge(c_ready, units(b, LT))
                    pool.dma_start(ctx_d.rearrange("(b t p) n -> b p t n", p=P, t=LT)[b], cb[:, :, :]).then_inc(c_out, 16)

                def most(b):
                    for t in range(LT - 1):
                        for i in range(SLOTS):
                            step(b, t, i)
                            if t == 1 and i == LAG + 8 and back(b, 0, 1):
                                store(b - 1)

                most(0)
                with pool.Fori(1, BATCH) as b:
                    for i in range(SLOTS):
                        step(b - 1, LT - 1, i)
                    most(b)
                for i in range(SLOTS):
                    step(BATCH - 1, LT - 1, i)
                finish(step)
                store(BATCH - 1)
                pool.wait_ge(c_out, 16 * BATCH)

            @block.tensor
            def _(pe):
                pe.wait_ge(idh_ok, 1)

                def first(b, t, i):
                    if i == 0 and t % 2 == 0:
                        pe.wait_ge(qst_in[t // 2], (b + 1) * 16)
                    if t == 0 and i % (SLOTS // 2) == 0:
                        pe.wait_ge(bd_in[i // (SLOTS // 2)], (b + 1) * 64)
                    if t == 0 and i % LT == 0:
                        pe.wait_ge(kd_ok, b * LT + i // LT + 1)
                    bank = A[i % NA][:, :].rearrange("p (h c) -> p h c", h=H1)
                    wait_for(pe, s1_lo, slots(b, t) + i + 1 - NA)
                    for q in range(QG):
                        nc.tensor.matmul(bank[:, 4 * q:4 * q + 4, :], qst[:, q, t * P:(t + 1) * P],
                                         kbd[:, q, :, i * KC:(i + 1) * KC],
                                         start=(q == 0), stop=False, skip_group_check=True)
                    for a in range(KC // JG):
                        r = i * KC + a * JG
                        y = t * P - r + TOFF
                        mm = nc.tensor.matmul(bank[:, :, a * JG:(a + 1) * JG], fwd[:, y:y + P], kd[:, :, r:r + JG],
                                              start=False, stop=(a == KC // JG - 1), skip_group_check=True)
                    mm.then_inc(a_ready, 1)

                def scores(b, t, j):
                    g, r, half = split(j)
                    if j == 0:
                        pe.wait_ge(qd_ok, b * LT + t + 1)
                    if j % UC == 0:
                        pe.wait_ge(dm_ok, units(b, t) + g + 1)
                    bank = B[j % NB]
                    v = vb3(bank)
                    wait_for(pe, p_ready, slots(b, t) + j + 1 - NB)
                    nc.tensor.matmul(bank[:, :], ones_bf[:, :], dm[:, g, :, half * QC:(half + 1) * QC],
                                     start=True, stop=False, skip_group_check=True)
                    for a in range(QC // JG):
                        l = half * QC + a * JG
                        y = r * P - t * P - l + TOFF
                        nc.tensor.matmul(v[:, :, a * JG:(a + 1) * JG], bwd[:, y:y + P],
                                         qd[:, t % 2, g * HG:(g + 1) * HG, l:l + JG], start=False, stop=False,
                                         skip_group_check=True)
                    for h in range(HG):
                        for part in (S1H, S1L):
                            mm = nc.tensor.matmul(v[:, h, :], part[:, t % 2, g * HG + h, r * P:(r + 1) * P],
                                                  idh[:, half * QC:(half + 1) * QC], start=False,
                                                  stop=(h == HG - 1 and part is S1L), skip_group_check=True)
                    mm.then_inc(b_ready, 1)

                def values(b, t, g, k):
                    if t == 0 and k == 0:
                        pe.wait_ge(v_in[g], (b + 1) * 16)
                    if k == 0:
                        pe.wait_ge(pl_ok, (units(b, t) + g + 1) * UC)
                        wait_for(pe, c_ready, units(b, t) + g - 1)
                    for h in range(2 * k, 2 * k + 2):
                        for r in range(LT):
                            o, w = h * DV, vb[:, g, r, h * DV:(h + 1) * DV]
                            nc.tensor.matmul(O[g][:, o:o + DV], PH[:, g, r, h, :], w,
                                             start=(r == 0), stop=False, skip_group_check=True)
                            mm = nc.tensor.matmul(O[g][:, o:o + DE], PL[:, g, r, h, :], w[:, 0:DE],
                                                  start=False, stop=(r == LT - 1), skip_group_check=True)
                    if k == HG // 2 - 1:
                        mm.then_inc(o_ready, 1)

                def step(b, t, i):
                    if not past(t):
                        first(b, t, i)
                    at = behind(b, t, i)
                    if at and not past(at[1]):
                        scores(*at)
                    at = values_at(b, t, i)
                    if at and not past(at[1]):
                        values(*at)

                def batch(b):
                    for t in range(LT):
                        for i in range(SLOTS):
                            step(b, t, i)

                batch(0)
                with pe.Fori(1, BATCH) as b:
                    batch(b)
                finish(step)

            @block.scalar
            def _(act):
                def step(b, t, i):
                    if not past(t):
                        act.wait_ge(a_ready, slots(b, t) + i + 1)
                        nc.scalar.copy(S1H[:, t % 2, :, i * KC:(i + 1) * KC],
                                       A[i % NA][:, :].rearrange("p (h c) -> p h c", h=H1)).then_inc(s1_hi, 1)
                    at = behind(b, t, i)
                    if at and not past(at[1]):
                        b0, t0, j = at
                        g, r, half = split(j)
                        bank = vb3(B[j % NB])
                        act.wait_ge(b_ready, slots(b0, t0) + j + 1)
                        nc.scalar.activation(PH[:, g, r, :, half * QC:(half + 1) * QC], bank, ACT.Exp, scale=SM1)
                        wait_for(act, pl_ok, slots(b0, t0) + j + 1 - NP32)
                        nc.scalar.activation(PF[:, j % NP32], bank, ACT.Exp, scale=SM1).then_inc(p_ready, 1)

                def batch(b):
                    for t in range(LT):
                        for i in range(SLOTS):
                            step(b, t, i)

                batch(0)
                with act.Fori(1, BATCH) as b:
                    batch(b)
                finish(step)

            @block.vector
            def _(dve):
                NMX = LT + 2

                def low(b, t, i):
                    dve.wait_ge(s1_hi, slots(b, t) + i + 1)
                    o = slice(i * KC, (i + 1) * KC)
                    nc.vector.tensor_tensor(S1L[:, t % 2, :, o], A[i % NA][:, :].rearrange("p (h c) -> p h c", h=H1),
                                            S1H[:, t % 2, :, o], ALU.subtract).then_inc(s1_lo, 1)

                def quarter(b, t, q):
                    if q == 0:
                        wait_for(dve, mx_step, (b * LT + t) * NMX)
                    nc.vector.tensor_reduce(mq[:, q, :], S1H[:, t % 2, :, q * P:(q + 1) * P], AX.X, ALU.max)\
                        .then_inc(mx_step, 1)

                def shift(b, t):
                    n = (b * LT + t) * NMX
                    if t == 0:
                        dve.wait_ge(rb_in, (b + 1) * 16)
                    dve.wait_ge(mx_step, n + LT)
                    wait_for(dve, dm_ok, units(b, t))
                    nc.vector.tensor_reduce(mx[:, :], mq[:, :, :].rearrange("p q h -> p h q"), AX.X, ALU.max)\
                        .then_inc(mx_step, 1)
                    dve.wait_ge(mx_step, n + LT + 1)
                    nc.vector.scalar_tensor_tensor(out=mx[:, :], in0=mx[:, :], scalar=-1.0, in1=rbb[:, t, :],
                                                   op0=ALU.mult, op1=ALU.subtract).then_inc(mx_step, 1)
                    dve.wait_ge(mx_step, n + LT + 2)

                def diagonal(b, t, g):
                    wait_for(dve, b_ready, slots(b, t - 1) + (g + 1) * UC)
                    nc.vector.tensor_tensor(dm[:, g, :, :], bc_mid(ident_bf[:, :], HG),
                                            bc_last(mx[:, g * HG:(g + 1) * HG], P), ALU.mult).then_inc(dm_ok, 1)

                def divide(b, t, g):
                    n = units(b, t) + g
                    dve.wait_ge(o_ready, n + 1)
                    wait_for(dve, c_ready, n)
                    if t == 0 and g == 0:
                        wait_for(dve, c_out, b * 16)
                    o = O[g][:, 0:HG * DV].rearrange("p (h e) -> p h e", h=HG)
                    c = cb[:, t, g * HG * D1:(g + 1) * HG * D1].rearrange("p (h e) -> p h e", h=HG)
                    nc.vector.reciprocal(rz[:, :], o[:, :, D1]).then_inc(o_step, 1)
                    nc.vector.tensor_copy(ol[:, :, :], o[:, :, DE:DV]).then_inc(o_step, 1)
                    dve.wait_ge(o_step, n * 3 + 2)
                    nc.vector.tensor_tensor(ol[:, :, :], o[:, :, 0:D1], ol[:, :, :], ALU.add).then_inc(o_step, 1)
                    dve.wait_ge(o_step, n * 3 + 3)
                    nc.vector.tensor_tensor(c, ol[:, :, :], bc_last(rz[:, :], D1), ALU.mult).then_inc(c_ready, 1)

                def step(b, t, i):
                    if not past(t):
                        low(b, t, i)
                        if i % LT == LT - 1:
                            quarter(b, t, i // LT)
                        if i == SLOTS - 1:
                            shift(b, t)
                            diagonal(b, t, 0)
                    if i == LAG + 1 and back(b, t, 1) and not past(t - 1):
                        diagonal(*back(b, t, 1), 1)
                    at = i > 0 and values_at(b, t, i - 1)
                    if at and at[3] == HG // 2 - 1 and not past(at[1]):
                        divide(*at[0:3])

                def spread_k(b, q):
                    if q == 0:
                        dve.wait_ge(kc_in, (b + 1) * 16 * JG)
                    wait_for(dve, a_ready, slots(b - 1, LT - 1) + (q + 1) * SLOTS // LT)
                    nc.vector.tensor_tensor(*spread(kd[:, :, q * P:(q + 1) * P], kc[:, :, q * P // JG:(q + 1) * P // JG]),
                                            ALU.mult).then_inc(kd_ok, 1)

                def most(b):
                    for t in range(LT - 1):
                        for i in range(SLOTS):
                            step(b, t, i)
                            if t == 0 and i == 0 and back(b, 0, 1):
                                spread_k(b, LT - 1)

                dve.wait_ge(gm_ok, 1)
                for q in range(LT):
                    spread_k(0, q)
                most(0)
                with dve.Fori(1, BATCH) as b:
                    for i in range(SLOTS):
                        step(b - 1, LT - 1, i)
                        if i % LT == 1 and i > LT:
                            spread_k(b, i // LT - 1)
                    most(b)
                for i in range(SLOTS):
                    step(BATCH - 1, LT - 1, i)
                finish(step)


def l1_project(nc, sb, pb, sem, ins, S, ident, dram):
    ctx_d, xn_d = dram[6:8]
    with ExitStack() as st:
        XN = sb("XNb", [P, TILES, DIM], F32, st)
        C = sb("C", [P, TILES, DIM], F32, st)
        CTt = sb("CTt", [P, 2, 512], F32, st)
        wo = sb("wo1", [P, P], F32, st)
        rows = sb("rows", [P, 3, P], F32, st)
        stats = sb("stats2", [P, TILES, 6], F32, st)
        mv = sb("mv2", [P, TILES, 2], F32, st)
        rstd = sb("rstd2", [P, TILES], F32, st)
        eps = sb("eps2", [P, 1], F32, st)
        TPp = [pb(f"tc{i}", [P, 512], F32, st) for i in range(2)]
        PR = [pb(f"pc{i}", [P, 512], F32, st) for i in range(2)]
        c_in, w_in = [sem(f"ctx_in{c}") for c in range(CH)], sem("wo_in")
        step_s, var_ok, std_ok, eps_ok = sem("p2_step"), sem("var2_ok"), sem("std2_ok"), sem("eps2_ok")
        tp_ok, ct_ok, pr_ok, h_ok = sem("tc_ok"), sem("ct_ok"), sem("pc_ok"), sem("h_ok")
        NCK = TOK // 512
        with nc.Block() as block:
            @block.sync
            def _(sp):
                for c in range(CH):
                    t = slice(c * CT, (c + 1) * CT)
                    sp.dma_start(C[:, t, :], ctx_d.rearrange("(t p) n -> p t n", p=P)[:, t, :]).then_inc(c_in[c], 16)
                sp.dma_start(XN[:, :, :], xn_d.rearrange("(t p) n -> p t n", p=P)).then_inc(w_in, 16)
                sp.dma_start(wo[:, :], ins["wo"]).then_inc(w_in, 16)
                for k, n in enumerate(("bo", "ln_g", "ln_b")):
                    sp.dma_start(rows[:, k, :], ins[n].partition_broadcast(P)).then_inc(w_in, 16)

            @block.tensor
            def _(pe):
                for n in range(NCK + 1):
                    if n < NCK:
                        pe.wait_ge(c_in[n // 2], 16)
                        if n >= 2:
                            pe.wait_ge(ct_ok, n - 1)
                        for k in range(4):
                            mm = nc.tensor.transpose(TPp[n % 2][:, k * P:(k + 1) * P], C[:, 4 * n + k, :], ident[:, :])
                        mm.then_inc(tp_ok, 1)
                    if n >= 1:
                        m = n - 1
                        if m == 0:
                            pe.wait_ge(w_in, 80)
                        pe.wait_ge(ct_ok, m + 1)
                        if m >= 2:
                            pe.wait_ge(h_ok, m - 1)
                        for k in range(4):
                            mm = nc.tensor.matmul(PR[m % 2][:, k * P:(k + 1) * P], CTt[:, m % 2, k * P:(k + 1) * P],
                                                  wo[:, :], start=True, stop=True)
                        mm.then_inc(pr_ok, 1)

            @block.scalar
            def _(act):
                for n in range(NCK):
                    act.wait_ge(tp_ok, n + 1)
                    if n >= 2:
                        act.wait_ge(pr_ok, n - 1)
                    nc.scalar.copy(CTt[:, n % 2, :], TPp[n % 2][:, :]).then_inc(ct_ok, 1)
                act.wait_ge(eps_ok, 1)
                for c in range(CH):
                    t = slice(c * CT, (c + 1) * CT)
                    act.wait_ge(var_ok, c + 1)
                    nc.scalar.activation(rstd[:, t], mv[:, t, 1], ACT.Sqrt, bias=eps[:, 0:1]).then_inc(std_ok, 1)

            @block.vector
            def _(dve):
                step = Chain(dve, step_s)
                nc.vector.memset(eps[:, :], 1e-12).then_inc(eps_ok, 1)
                dve.wait_ge(w_in, 80)
                step(nc.vector.tensor_tensor(XN[:, :, :], XN[:, :, :], bc_mid(rows[:, 0, :], TILES), ALU.add))
                for n in range(NCK):
                    dve.wait_ge(pr_ok, n + 1)
                    t = slice(4 * n, 4 * n + 4)
                    nc.vector.tensor_tensor(S[:, t, :], PR[n % 2][:, :].rearrange("p (t c) -> p t c", t=4),
                                            XN[:, t, :], ALU.add).then_inc(h_ok, 1)
                def affine(c):
                    for i in normalise(nc, S, S, mv, rstd, c):
                        step.more(i)
                    step.wait()
                    t = slice(c * CT, (c + 1) * CT)
                    step(nc.vector.tensor_tensor(S[:, t, :], S[:, t, :], bc_mid(rows[:, 1, :], CT), ALU.mult))
                    step(nc.vector.tensor_tensor(S[:, t, :], S[:, t, :], bc_mid(rows[:, 2, :], CT), ALU.add))

                dve.wait_ge(h_ok, NCK)
                for c in range(CH + 1):
                    if c < CH:
                        norm_stats(nc, step, S, stats, mv, c).then_inc(var_ok, 1)
                    if c >= 1:
                        t = slice((c - 1) * CT, c * CT)
                        dve.wait_ge(std_ok, c)
                        step(nc.vector.reciprocal(rstd[:, t], rstd[:, t]))
                        affine(c - 1)


def l1_experts(nc, sb, pb, sem, ins, out, X, XH, XL, S, ident):
    with ExitStack() as st:
        wr = sb("wr", [P, NEXP], F32, st)
        wrh = sb("wrh", [P, NEXP], F16, st)
        wrl = sb("wrl", [P, NEXP], F16, st)
        wf = sb("wf", [P, 3, PAIRS + 1, P], F32, st)
        wh = sb("wh", [P, 3, PAIRS + 1, P], F16, st)
        wl = sb("wl", [P, 3, PAIRS + 1, P], F16, st)
        pkf = sb("pkf", [2 * NEXP, PAIRS, P], F32, st)
        pk = sb("pk", [2 * NEXP, PAIRS, P], F16, st)
        L = sb("L", [P, TILES, NEXP + 6], F32, st)
        best = sb("best", [P, TILES, 8], F32, st)
        rest = sb("rest", [P, TILES, NEXP + 6], F32, st)
        lm = sb("lm", [P, TILES], F32, st)
        cwT = sb("cwT", [2 * NEXP, TOK], F16, st)
        cl = sb("cl", [P, TILES, 2 * NEXP], F16, st)
        idh = sb("idh", [P, P], F16, st)
        sg = sb("sgs", [P, 2, 512], F32, st)
        hb = sb("hb", [P, 2, 512], F32, st)
        hh = sb("hh", [P, 2, 512], F16, st)
        hl = sb("hl", [P, 2, 512], F16, st)
        Y = sb("Y1", [P, TILES, P], F32, st)
        G = [pb(f"G{i}", [P, 512], F32, st) for i in range(2)]
        U = [pb(f"U{i}", [P, 512], F32, st) for i in range(2)]
        W = [pb(f"W{i}", [P, 512], F32, st) for i in range(2)]
        Dn = [pb(f"D{i}", [P, 512], F32, st) for i in range(2)]
        w_in, r_in = sem("we_in"), sem("wr_in")
        step_s, log_ok, log_used = sem("p3_step"), sem("log_ok"), sem("log_used")
        exp_in, exp_ok, best_ok, cw_ok = sem("exp_in"), sem("exp_ok"), sem("best_ok"), sem("cw_ok")
        ct_ok, ct_used, pk_ok, idh_ok = sem("cwt_ok"), sem("cwt_used"), sem("pk_ok"), sem("idh_ok")
        gu_ok, silu_ok, h2_ok, hh_ok, hl_ok = (sem(n) for n in ("gu_ok", "sg_ok", "h2_ok", "hh_ok", "hl_ok"))
        wrh_ok, wrl_ok, wh_ok, wl_ok = (sem(n) for n in ("wrh_ok", "wrl_ok", "wh_ok", "wl_ok"))
        dn_ok, y_ok, s_ok, out_ok, stored = sem("dn2_ok"), sem("y2_ok"), sem("s2_ok"), sem("out_ok"), sem("stored")
        NCK, NP = TOK // 512, PAIRS + 1
        out_v = out.rearrange("b (t p) c -> p (b t) c", p=P)
        with nc.Block() as block:
            @block.sync
            def _(sp):
                sp.dma_start(wr[:, :], ins["wr"]).then_inc(r_in, 16)
                for i, n, s in ((0, "wg", "sg"), (1, "wu", "su")):
                    d = wf[:, i]
                    sp.dma_start(d[:, 0:PAIRS, :].rearrange("p k (e f) -> p (k e) f", e=2),
                                 ins[n].rearrange("e d f -> d e f")).then_inc(w_in, 16)
                    sp.dma_start(d[:, PAIRS, :], ins[s]).then_inc(w_in, 16)
                sp.dma_start(wf[:, 2, 0:PAIRS, :], ins["wd"].rearrange("(k e) f d -> (e f) k d", e=2)).then_inc(w_in, 16)
                sp.dma_start(wf[:, 2, PAIRS, :], ins["sd"]).then_inc(w_in, 16)
                sp.dma_start(pkf[:, :, :], ins["pick"]).then_inc(w_in, 16)
                for c in range(CH):
                    t = slice(c * CT, (c + 1) * CT)
                    sp.wait_ge(out_ok, c + 1)
                    sp.dma_start(out_v[:, t, :], Y[:, t, :]).then_inc(stored, 16)
                sp.wait_ge(stored, 16 * CH)

            @block.gpsimd
            def _(pool):
                nc.gpsimd.tensor_copy(idh[:, :], ident[:, :]).then_inc(idh_ok, 1)
                pool.wait_ge(w_in, 16 * 7)
                nc.gpsimd.tensor_copy(pk[:, :, :], pkf[:, :, :]).then_inc(pk_ok, 1)

            @block.tensor
            def _(pe):
                pe.wait_ge(wrl_ok, 1)
                for t in range(TILES):
                    o, x = slice(t * NEXP, (t + 1) * NEXP), slice(t * P, (t + 1) * P)
                    nc.tensor.matmul(G[0][:, o], XH[:, x], wrh[:, :], start=True, stop=False)
                    nc.tensor.matmul(G[0][:, o], XH[:, x], wrl[:, :], start=False, stop=False)
                    mm = nc.tensor.matmul(G[0][:, o], XL[:, x], wrh[:, :], start=False, stop=True)
                mm.then_inc(log_ok, 1)
                pe.wait_ge(idh_ok, 1)
                pe.wait_ge(cw_ok, 1)
                for n in range(NCK):
                    if n >= 2:
                        pe.wait_ge(ct_used, n - 1)
                    for k in range(4):
                        mm = nc.tensor.matmul(W[n % 2][0:2 * NEXP, k * P:(k + 1) * P], cl[:, 4 * n + k, :],
                                              idh[:, :], start=True, stop=True)
                    mm.then_inc(ct_ok, 1)
                pe.wait_ge(wl_ok, 1)
                pe.wait_ge(pk_ok, 1)
                pe.wait_ge(ct_used, NCK)

                def up(n):
                    c, p = n // NP, n % NP
                    x = slice(c * 512, (c + 1) * 512)

                    def halves(bank, i):
                        nc.tensor.matmul(bank[:, :], wh[:, i, p, :], XH[:, x], start=True, stop=False)
                        nc.tensor.matmul(bank[:, :], wl[:, i, p, :], XH[:, x], start=False, stop=False)
                        return nc.tensor.matmul(bank[:, :], wh[:, i, p, :], XL[:, x], start=False, stop=True)

                    if n >= 2:
                        pe.wait_ge(h2_ok, n - 1)
                    halves(G[n % 2], 0)
                    if p < PAIRS:
                        nc.tensor.matmul(W[n % 2][:, :], pk[:, p, :], cwT[:, c * 512:(c + 1) * 512],
                                         start=True, stop=True)
                    halves(U[n % 2], 1).then_inc(gu_ok, 1)

                def down(n):
                    c, p = n // NP, n % NP
                    pe.wait_ge(hl_ok, n + 1)
                    if p == 0 and c >= 2:
                        pe.wait_ge(y_ok, c - 1)
                    for k in range(4):
                        o = slice(k * P, (k + 1) * P)
                        for i, (a, w) in enumerate(((hh, wh), (hh, wl), (hl, wh))):
                            mm = nc.tensor.matmul(Dn[c % 2][:, o], a[:, n % 2, o], w[:, 2, p, :],
                                                  start=(p == 0 and k == 0 and i == 0),
                                                  stop=(p == NP - 1 and i == 2), skip_group_check=True)
                    mm.then_inc(dn_ok, 1)

                for n in range(NCK * NP + 2):
                    if n < NCK * NP:
                        up(n)
                    if n >= 2:
                        down(n - 2)

            @block.scalar
            def _(act):
                act.wait_ge(r_in, 16)
                nc.scalar.copy(wrh[:, :], wr[:, :]).then_inc(wrh_ok, 1)
                act.wait_ge(w_in, 16 * 7)
                for i in range(3):
                    nc.scalar.copy(wh[:, i], wf[:, i]).then_inc(wh_ok, 1)
                act.wait_ge(exp_in, 1)
                nc.scalar.activation(L[:, :, 0:NEXP], L[:, :, 0:NEXP], ACT.Exp).then_inc(exp_ok, 1)
                for n in range(NCK):
                    act.wait_ge(ct_ok, n + 1)
                    nc.scalar.copy(cwT[:, n * 512:(n + 1) * 512], W[n % 2][0:2 * NEXP, :]).then_inc(ct_used, 1)
                for n in range(NCK * NP + 1):
                    if n < NCK * NP:
                        act.wait_ge(gu_ok, n + 1)
                        if n >= 2:
                            act.wait_ge(h2_ok, n - 1)
                        nc.scalar.activation(sg[:, n % 2, :], G[n % 2][:, :], ACT.Silu).then_inc(silu_ok, 1)
                    if n >= 1:
                        act.wait_ge(h2_ok, n)
                        if n >= 3:
                            act.wait_ge(dn_ok, n - 2)
                        nc.scalar.copy(hh[:, (n - 1) % 2, :], hb[:, (n - 1) % 2, :]).then_inc(hh_ok, 1)
                for c in range(CH):
                    t = slice(c * CT, (c + 1) * CT)
                    act.wait_ge(y_ok, 2 * c + 2)
                    nc.scalar.activation(Y[:, t, :], Y[:, t, :], ACT.Silu).then_inc(s_ok, 1)

            @block.vector
            def _(dve):
                step = Chain(dve, step_s)
                dve.wait_ge(wrh_ok, 1)
                nc.vector.tensor_tensor(wrl[:, :], wr[:, :], wrh[:, :], ALU.subtract).then_inc(wrl_ok, 1)
                step(nc.vector.memset(L[:, :, NEXP:NEXP + 6], -1.0))
                dve.wait_ge(wh_ok, 3)
                nc.vector.tensor_tensor(wl[:, :, :, :], wf[:, :, :, :], wh[:, :, :, :], ALU.subtract).then_inc(wl_ok, 1)
                dve.wait_ge(log_ok, 1)
                lv = L[:, :, 0:NEXP]
                lp = G[0][:, :].rearrange("p (t e) -> p t e", e=NEXP)
                step(nc.vector.tensor_reduce(lm[:, :], lp, AX.X, ALU.max))
                nc.vector.tensor_tensor(lv, lp, bc_last(lm[:, :], NEXP), ALU.subtract).then_inc(exp_in, 1)
                dve.wait_ge(exp_ok, 1)
                step(nc.vector.tensor_reduce(lm[:, :], lv, AX.X, ALU.add))
                step(nc.vector.reciprocal(lm[:, :], lm[:, :]))
                step(nc.vector.tensor_tensor(lv, lv, bc_last(lm[:, :], NEXP), ALU.mult))
                for t in range(TILES):
                    i = nc.vector.max(best[:, t, :], L[:, t, :])
                    i.then_inc(best_ok, 1)
                dve.wait_ge(best_ok, TILES)
                step(nc.vector.memset(best[:, :, 2:8], -1.0))
                for t in range(TILES):
                    nc.vector.match_replace(rest[:, t, :], best[:, t, :], L[:, t, :], 0.0).then_inc(best_ok, 1)
                dve.wait_ge(best_ok, 2 * TILES)
                step(nc.vector.tensor_tensor(lv, lv, rest[:, :, 0:NEXP], ALU.subtract))
                step(nc.vector.tensor_copy(cl[:, :, 0:NEXP], lv))
                nc.vector.tensor_tensor(cl[:, :, NEXP:2 * NEXP], lv, cl[:, :, 0:NEXP], ALU.subtract).then_inc(cw_ok, 1)
                for n in range(NCK * NP + 1):
                    c, p = n // NP, n % NP
                    if n < NCK * NP:
                        dve.wait_ge(silu_ok, n + 1)
                        if n >= 2:
                            dve.wait_ge(hl_ok, n - 1)
                        m = nc.vector.tensor_tensor(hb[:, n % 2, :], U[n % 2][:, :], sg[:, n % 2, :], ALU.mult)
                        if p < PAIRS:
                            step(m)
                            m = nc.vector.tensor_tensor(hb[:, n % 2, :], hb[:, n % 2, :], W[n % 2][:, :], ALU.mult)
                        m.then_inc(h2_ok, 1)
                    if n >= 1:
                        dve.wait_ge(hh_ok, n)
                        nc.vector.tensor_tensor(hl[:, (n - 1) % 2, :], hb[:, (n - 1) % 2, :], hh[:, (n - 1) % 2, :],
                                                ALU.subtract).then_inc(hl_ok, 1)
                    if p == 1 and 1 <= c < NCK:
                        keep2(nc, dve, dn_ok, y_ok, Y, Dn, c - 1, NP)
                keep2(nc, dve, dn_ok, y_ok, Y, Dn, NCK - 1, NP)
                for c in range(CH):
                    t = slice(c * CT, (c + 1) * CT)
                    dve.wait_ge(s_ok, c + 1)
                    step(nc.vector.tensor_tensor(Y[:, t, :], Y[:, t, :], S[:, t, :], ALU.mult))
                    nc.vector.tensor_tensor(Y[:, t, :], Y[:, t, :], X[:, t, :], ALU.add).then_inc(out_ok, 1)


def keep2(nc, dve, dn_ok, y_ok, Y, Dn, c, NP):
    dve.wait_ge(dn_ok, (c + 1) * NP)
    nc.vector.tensor_copy(Y[:, 4 * c:4 * c + 4, :], Dn[c % 2][:, :].rearrange("p (t c) -> p t c", t=4)).then_inc(y_ok, 1)


def kernel(**inputs):
    import numpy as _np
    import concourse.bacc as _bacc
    from concourse import mybir as _mybir
    from concourse.bass_utils import run_bass_kernel_spmd as _run

    a = {k: _np.asarray(v) for k, v in inputs.items()}
    dist = a["L1_attn_dist_emb"]
    delta = _np.arange(-(SEQ - 1), SEQ) + M_REL - 1
    row = _np.clip(_np.where(delta < 0, delta + NDIST, delta), 0, NDIST - 1)
    y = _np.arange(TW)
    rows = _np.arange(P)
    j_of, s_of, e_of = rows // (4 * D1), rows % 4, rows // 4 % D1
    fwd = row[(y[None, :] - TOFF - j_of[:, None]) + SEQ - 1]
    bwd = row[(j_of[:, None] - (y[None, :] - TOFF)) + SEQ - 1]
    eye = _np.eye(P, dtype=_np.float32)
    key_after = _np.triu(_np.ones((P, P), _np.float32), k=1) * _np.float32(NEG)
    side = _np.zeros((P, 2, 2), _np.float32)
    side[rows, 0, _np.array(Q_STACK)[s_of]] = 1.0
    side[rows, 1, _np.array(K_STACK)[s_of]] = 1.0
    group = _np.zeros((P, JG), _np.float32)
    group[rows, j_of] = 1.0
    head = _np.zeros((P, H1), _np.float32)
    head[_np.arange(P), _np.arange(P) // D1] = 1.0
    pick = _np.zeros((2 * NEXP, PAIRS, P), _np.float32)
    for e in range(NEXP):
        pick[[e, NEXP + e], e // 2, (e % 2) * FE:(e % 2 + 1) * FE] = 1.0
    host = {
        "x": a["L0_attn_x"], "gamma": a["L0_attn_gamma"], "w_qkv": a["L0_attn_w_qkv"],
        "w_outT": a["L0_attn_w_out"].T, "w_upT": a["L0_ffn_w_up"].T, "w_downT": a["L0_ffn_w_down"].T,
        "wq": a["L1_attn_Wq"], "bq": a["L1_attn_bq"], "wk": a["L1_attn_Wk"], "bk": a["L1_attn_bk"],
        "wv": a["L1_attn_Wv"], "bv": a["L1_attn_bv"], "wo": a["L1_attn_Wo"], "bo": a["L1_attn_bo"],
        "ln_g": a["L1_attn_ln_gamma"], "ln_b": a["L1_attn_ln_beta"],
        "toep_f": dist[fwd, e_of[:, None]], "toep_b": dist[bwd, e_of[:, None]], "distT": dist.T,
        "wr": a["L1_ffn_Wr"], "wg": a["L1_ffn_Wg"], "wu": a["L1_ffn_Wu"], "wd": a["L1_ffn_Wd"],
        "sg": a["L1_ffn_Sg"], "su": a["L1_ffn_Su"], "sd": a["L1_ffn_Sd"],
        "identity": eye, "causal": _np.stack([key_after, key_after.T]), "side": side, "group": group, "head": head,
        "pick": pick,
    }
    nc = _bacc.Bacc("TRN2", target_bir_lowering=False, num_devices=1)
    arrays, ins = {}, {}
    for name, value in host.items():
        value = _np.ascontiguousarray(value)
        arrays[f"in_{name}"] = value
        ins[name] = nc.dram_tensor(f"in_{name}", value.shape, _mybir.dt.from_np(value.dtype),
                                   kind="ExternalInput").ap()
    out = nc.dram_tensor("out_x", (BATCH, SEQ, DIM), F32, kind="ExternalOutput").ap()
    build(nc, ins, out)
    r = _run(nc, [arrays], core_ids=[0])
    return r.results[0]["out_x"]
```
